# Optimizing a Trainium2 kernel written in Bass

```python
import numpy as np
import jax
import jax.numpy as jnp

def _softmax(x, axis=-1):
    return jax.nn.softmax(x, axis=axis)

def _gelu(x):
    return jax.nn.gelu(x, approximate=True)

def _silu(x):
    return jax.nn.silu(x)

def _sigmoid(x):
    return jax.nn.sigmoid(x)

def _layernorm(x, axis=-1, eps=1e-05):
    m = jnp.mean(x, axis=axis, keepdims=True)
    v = jnp.var(x, axis=axis, keepdims=True)
    return (x - m) / jnp.sqrt(v + eps)

def _scatter_add(tgt, idx, src, axis=0):
    return tgt.at[idx].add(src)

def _segment_sum(src, seg, n):
    return jax.ops.segment_sum(src, seg, n)
kernel_name = 'mk_adj_ffn_d1_adj_r2_1238fc'

def setup_inputs(seed: int=0):
    np.random.seed(seed)
    _w = jnp.asarray

    def _rec_inputs():
        import jax
        import jax.numpy as jnp
        _gk = jax.random.key(seed)
        x = -0.0001538 + 1 * jax.random.normal(jax.random.fold_in(_gk, 1), (128, 64, 384), jnp.float32)
        _w = (1.0 + jnp.arange(64, dtype=jnp.float32)) ** (-0.5)
        _w = _w / _w.mean()
        _pij = jnp.clip(0.125 * _w[:, None] * _w[None, :], 0.0, 1.0)
        _a = jax.random.uniform(jax.random.fold_in(_gk, 2), (128, 64, 64)) < _pij
        _af = _a.astype(jnp.float32)
        _af = _af * jax.random.uniform(jax.random.fold_in(_gk, 3), (128, 64, 64), jnp.float32, 0.05, 0.999992)
        adj = _af
        return (x, adj)
    x, adj = _rec_inputs()

    def _L0_gnn_setup():
        import jax, jax.numpy as jnp
        import numpy as np
        B, N, D, H = (8, 512, 384, 12)
        HD = D // H

        def _split_heads(x):
            b, n, _ = x.shape
            return x.reshape(b, n, H, HD).transpose(0, 2, 1, 3)
        key = jax.random.key(seed)
        ks = jax.random.split(key, 10)
        input_graph = jax.random.normal(ks[0], (B, N, D), dtype=jnp.float32)
        u = jax.random.uniform(ks[1], (B, N, N), dtype=jnp.float32)
        keep = jax.random.uniform(ks[2], (B, N, N)) < 0.15
        adj = jnp.where(keep, u, 0.0)
        s = 1.0 / np.sqrt(D)
        Wq = jax.random.normal(ks[3], (D, D), dtype=jnp.float32) * s
        bq = jnp.zeros((D,), dtype=jnp.float32)
        Wk = jax.random.normal(ks[4], (D, D), dtype=jnp.float32) * s
        bk = jnp.zeros((D,), dtype=jnp.float32)
        Wv = jax.random.normal(ks[5], (D, D), dtype=jnp.float32) * s
        bv = jnp.zeros((D,), dtype=jnp.float32)
        beta = jnp.asarray(0.1, dtype=jnp.float32)
        return {'input_graph': input_graph, 'adj': adj, 'Wq': Wq, 'bq': bq, 'Wk': Wk, 'bk': bk, 'Wv': Wv, 'bv': bv, 'beta': beta}
    _L0_gnn_all = _L0_gnn_setup()
    _L0_gnn_in = {k: v for k, v in _L0_gnn_all.items() if k in ('Wq', 'bq', 'Wk', 'bk', 'Wv', 'bv', 'beta')}
    del _L0_gnn_all

    def _L0_ffn_setup():
        import jax, jax.numpy as jnp
        import numpy as np
        B, L, D, H, F = (4, 1024, 384, 12, 1536)
        ROUTE_FRAC = 0.15
        LN_EPS = 1e-05

        def _ln(x, g, b):
            m = jnp.mean(x, axis=-1, keepdims=True)
            v = jnp.mean((x - m) ** 2, axis=-1, keepdims=True)
            return (x - m) * jax.lax.rsqrt(v + LN_EPS) * g + b
        key = jax.random.key(seed)
        ks = jax.random.split(key, 20)
        s = 0.02
        return {'hidden_states': jax.random.normal(ks[0], (B, L, D), dtype=jnp.float32), 'g1': jnp.ones((D,), jnp.float32), 'b1': jnp.zeros((D,), jnp.float32), 'g2': jnp.ones((D,), jnp.float32), 'b2': jnp.zeros((D,), jnp.float32), 'Wr': jax.random.normal(ks[1], (D,), jnp.float32) * s, 'br': jnp.zeros((), jnp.float32), 'Wq': jax.random.normal(ks[2], (D, D), jnp.float32) * s, 'bq': jnp.zeros((D,), jnp.float32), 'Wk': jax.random.normal(ks[3], (D, D), jnp.float32) * s, 'bk': jnp.zeros((D,), jnp.float32), 'Wv': jax.random.normal(ks[4], (D, D), jnp.float32) * s, 'bv': jnp.zeros((D,), jnp.float32), 'Wo': jax.random.normal(ks[5], (D, D), jnp.float32) * s, 'bo': jnp.zeros((D,), jnp.float32), 'Wm': jax.random.normal(ks[6], (D, D), jnp.float32) * s, 'bm': jnp.zeros((D,), jnp.float32), 'W1': jax.random.normal(ks[7], (D, F), jnp.float32) * s, 'bf1': jnp.zeros((F,), jnp.float32), 'W2': jax.random.normal(ks[8], (F, D), jnp.float32) * s, 'bf2': jnp.zeros((D,), jnp.float32)}
    _L0_ffn_all = _L0_ffn_setup()
    _L0_ffn_in = {k: v for k, v in _L0_ffn_all.items() if k in ('g1', 'b1', 'g2', 'b2', 'Wr', 'br', 'Wq', 'bq', 'Wk', 'bk', 'Wv', 'bv', 'Wo', 'bo', 'Wm', 'bm', 'W1', 'bf1', 'W2', 'bf2')}
    del _L0_ffn_all
    return {'x': x, 'adj': adj, 'L0_gnn_Wq': _L0_gnn_in['Wq'], 'L0_gnn_bq': _L0_gnn_in['bq'], 'L0_gnn_Wk': _L0_gnn_in['Wk'], 'L0_gnn_bk': _L0_gnn_in['bk'], 'L0_gnn_Wv': _L0_gnn_in['Wv'], 'L0_gnn_bv': _L0_gnn_in['bv'], 'L0_gnn_beta': _L0_gnn_in['beta'], 'L0_ffn_g1': _L0_ffn_in['g1'], 'L0_ffn_b1': _L0_ffn_in['b1'], 'L0_ffn_g2': _L0_ffn_in['g2'], 'L0_ffn_b2': _L0_ffn_in['b2'], 'L0_ffn_Wr': _L0_ffn_in['Wr'], 'L0_ffn_br': _L0_ffn_in['br'], 'L0_ffn_Wq': _L0_ffn_in['Wq'], 'L0_ffn_bq': _L0_ffn_in['bq'], 'L0_ffn_Wk': _L0_ffn_in['Wk'], 'L0_ffn_bk': _L0_ffn_in['bk'], 'L0_ffn_Wv': _L0_ffn_in['Wv'], 'L0_ffn_bv': _L0_ffn_in['bv'], 'L0_ffn_Wo': _L0_ffn_in['Wo'], 'L0_ffn_bo': _L0_ffn_in['bo'], 'L0_ffn_Wm': _L0_ffn_in['Wm'], 'L0_ffn_bm': _L0_ffn_in['bm'], 'L0_ffn_W1': _L0_ffn_in['W1'], 'L0_ffn_bf1': _L0_ffn_in['bf1'], 'L0_ffn_W2': _L0_ffn_in['W2'], 'L0_ffn_bf2': _L0_ffn_in['bf2']}

def reference(x, adj, L0_gnn_Wq, L0_gnn_bq, L0_gnn_Wk, L0_gnn_bk, L0_gnn_Wv, L0_gnn_bv, L0_gnn_beta, L0_ffn_g1, L0_ffn_b1, L0_ffn_g2, L0_ffn_b2, L0_ffn_Wr, L0_ffn_br, L0_ffn_Wq, L0_ffn_bq, L0_ffn_Wk, L0_ffn_bk, L0_ffn_Wv, L0_ffn_bv, L0_ffn_Wo, L0_ffn_bo, L0_ffn_Wm, L0_ffn_bm, L0_ffn_W1, L0_ffn_bf1, L0_ffn_W2, L0_ffn_bf2):
    import jax
    import jax.numpy as jnp

    def _L0_gnn_ref(input_graph, adj, Wq, bq, Wk, bk, Wv, bv, beta):
        import jax, jax.numpy as jnp
        import numpy as np
        B, N, D, H = (8, 512, 384, 12)
        HD = D // H

        def _split_heads(x):
            b, n, _ = x.shape
            return x.reshape(b, n, H, HD).transpose(0, 2, 1, 3)
        q = _split_heads(input_graph @ Wq + bq)
        k = _split_heads(input_graph @ Wk + bk)
        v = _split_heads(input_graph @ Wv + bv)
        scores = jnp.einsum('bhqd,bhkd->bhqk', q, k) / jnp.sqrt(jnp.asarray(HD, input_graph.dtype))
        adj_e = adj[:, None, :, :]
        scores = scores + beta * adj_e
        scores = jnp.where(adj_e > 0, scores, jnp.asarray(-9000000000000000.0, scores.dtype))
        probs = jax.nn.softmax(scores, axis=-1)
        out = jnp.einsum('bhqk,bhkd->bhqd', probs, v)
        return out.transpose(0, 2, 1, 3).reshape(input_graph.shape[0], input_graph.shape[1], D)

    def _L0_ffn_ref(hidden_states, g1, b1, g2, b2, Wr, br, Wq, bq, Wk, bk, Wv, bv, Wo, bo, Wm, bm, W1, bf1, W2, bf2):
        import jax, jax.numpy as jnp
        import numpy as np
        B, L, D, H, F = (4, 1024, 384, 12, 1536)
        ROUTE_FRAC = 0.15
        LN_EPS = 1e-05

        def _ln(x, g, b):
            m = jnp.mean(x, axis=-1, keepdims=True)
            v = jnp.mean((x - m) ** 2, axis=-1, keepdims=True)
            return (x - m) * jax.lax.rsqrt(v + LN_EPS) * g + b
        b, l, d = hidden_states.shape
        dh = d // H
        normed = _ln(hidden_states, g1, b1)
        scores = jax.nn.sigmoid(jnp.einsum('bld,d->bl', normed, Wr) + br)
        k = max(1, int(round(ROUTE_FRAC * l)))
        _, idx = jax.lax.top_k(-scores, k)
        attn_mask = jnp.zeros((b, l), bool).at[jnp.arange(b)[:, None], idx].set(True)
        q = (normed @ Wq + bq).reshape(b, l, H, dh)
        kk = (normed @ Wk + bk).reshape(b, l, H, dh)
        v = (normed @ Wv + bv).reshape(b, l, H, dh)
        logits = jnp.einsum('blhd,bmhd->bhlm', q, kk) / jnp.sqrt(jnp.float32(dh))
        probs = jax.nn.softmax(logits, axis=-1)
        ctx = jnp.einsum('bhlm,bmhd->blhd', probs, v).reshape(b, l, d)
        attn_out = ctx @ Wo + bo
        w = scores / (jnp.sum(scores, axis=1, keepdims=True) + 1e-06)
        pooled = jnp.einsum('bl,bld->bd', w, normed)
        mix_out = (normed + scores[..., None] * pooled[:, None, :]) @ Wm + bm
        merged = jnp.where(attn_mask[..., None], attn_out, mix_out)
        h = hidden_states + merged
        n2 = _ln(h, g2, b2)
        ffn = jax.nn.gelu(n2 @ W1 + bf1, approximate=False) @ W2 + bf2
        return h + ffn
    x = x + _L0_gnn_ref(_layernorm(x, axis=-1), adj, L0_gnn_Wq, L0_gnn_bq, L0_gnn_Wk, L0_gnn_bk, L0_gnn_Wv, L0_gnn_bv, L0_gnn_beta)
    x = x + _L0_ffn_ref(_layernorm(x, axis=-1), L0_ffn_g1, L0_ffn_b1, L0_ffn_g2, L0_ffn_b2, L0_ffn_Wr, L0_ffn_br, L0_ffn_Wq, L0_ffn_bq, L0_ffn_Wk, L0_ffn_bk, L0_ffn_Wv, L0_ffn_bv, L0_ffn_Wo, L0_ffn_bo, L0_ffn_Wm, L0_ffn_bm, L0_ffn_W1, L0_ffn_bf1, L0_ffn_W2, L0_ffn_bf2)
    return x

_drawn_inputs = setup_inputs


def setup_inputs(seed=0):
    import zlib

    import numpy as np

    out = dict(_drawn_inputs(seed))
    spreads = {'L0_gnn_bq': (0.0, 0.1),
     'L0_gnn_bk': (0.0, 2.0),
     'L0_gnn_bv': (0.0, 0.1),
     'L0_ffn_g1': (1.0, 0.2),
     'L0_ffn_b1': (0.0, 0.302),
     'L0_ffn_g2': (1.0, 0.6),
     'L0_ffn_b2': (0.0, 0.8),
     'L0_ffn_bq': (0.0, 0.8),
     'L0_ffn_bk': (0.0, 2.0),
     'L0_ffn_bv': (0.0, 0.8),
     'L0_ffn_bo': (0.0, 0.42),
     'L0_ffn_bm': (0.0, 0.318),
     'L0_ffn_bf1': (0.0, 0.392),
     'L0_ffn_bf2': (0.0, 0.289)}
    factors = {'L0_ffn_Wq': 8.0, 'L0_ffn_Wk': 8.0, 'L0_ffn_Wv': 8.0, 'L0_ffn_Wo': 5.817}
    for name, (base, spread) in spreads.items():
        noise = np.random.default_rng([zlib.crc32(name.encode()), seed]).standard_normal(out[name].shape)
        drawn = base * np.exp(spread * noise) if base else spread * noise
        out[name] = jnp.asarray(drawn.astype(out[name].dtype))
    for name, factor in factors.items():
        out[name] = (out[name] * factor).astype(out[name].dtype)
    return out
```

```python
from contextlib import ExitStack

import concourse.bass as bass
from concourse import mybir

F32 = mybir.dt.float32
F16 = mybir.dt.float16
ALU = mybir.AluOpType
ACT = mybir.ActivationFunctionType
AX_X = mybir.AxisListType.X

P = 128
BATCH, NODES, D = 128, 64, 384
HEADS, HD = 12, 32
HIDDEN = 1536
KC = D // P
HC = HIDDEN // P
TOKENS = BATCH * NODES
TILES = 4
GROUP = TILES * P
GROUPS = TOKENS // GROUP
GB = GROUP // NODES
HQ = P // HD
PAIRS = HEADS // 2
VW = HD + 1
VROW = PAIRS * VW
TOPK = 10
SELN = GB * TOPK
SROWS = HEADS * TOPK
ZW = SELN + GB
EPS = 1e-5
MASKED = -9.0e15
QSCALE = float(HD) ** -0.5

C_ID, C_LT, C_GT, C_HALF, C_IOTA = 0, 128, 256, 384, 386
C_WIDTH = C_IOTA + 2 * TOPK



def gnn_ffn_kernel(nc, x, adj, w, consts, out, groups=GROUPS, debug=None):
    ctx = ExitStack()
    with ctx:
        def sb(name, shape, dt=F32):
            return ctx.enter_context(nc.sbuf_tensor(name, shape, dt))

        def sem(name):
            return ctx.enter_context(nc.semaphore(name))

        w_qk = [sb(f"w_qk_{h}", [P, KC, 2 * D], F16) for h in ("hi", "lo")]
        w_v = [sb(f"w_v_{h}", [P, KC, D], F16) for h in ("hi", "lo")]
        w_q2 = [sb(f"w_q2_{h}", [P, KC, D], F16) for h in ("hi", "lo")]
        w_k2 = [sb(f"w_k2_{h}", [P, KC, D], F16) for h in ("hi", "lo")]
        w_v2 = [sb(f"w_v2_{h}", [P, KC, D + 1], F16) for h in ("hi", "lo")]
        w_o = [sb(f"w_o_{h}", [P, KC, D], F16) for h in ("hi", "lo")]
        w_m = [sb(f"w_m_{h}", [P, KC, D], F16) for h in ("hi", "lo")]
        w_1 = [sb(f"w_1_{h}", [P, KC, HIDDEN], F16) for h in ("hi", "lo")]
        w_2 = [sb(f"w_2_{h}", [P, HC, D], F16) for h in ("hi", "lo")]

        const = sb("const", [P, C_WIDTH])
        ident = const[:, C_ID:C_ID + P]
        before = const[:, C_LT:C_LT + P]
        after = const[:, C_GT:C_GT + P]
        half = const[:, C_HALF:C_HALF + 2]
        iota = const[:, C_IOTA:C_IOTA + 2 * TOPK]
        ones = sb("ones", [P, P])
        minus_half = sb("minus_half", [P, TILES])
        minus_one = sb("minus_one", [P, TILES])
        eps = sb("eps", [P, TILES])
        pause = sb("pause", [P, 1])
        beta_bc = sb("beta_bc", [P, 1])
        VECTORS = ["L0_ffn_g1", "L0_ffn_b1", "L0_ffn_g2", "L0_ffn_b2", "L0_ffn_Wr", "L0_gnn_bq", "L0_gnn_bk",
                   "L0_ffn_bq", "L0_ffn_bk", "L0_ffn_bv", "L0_ffn_bf1"]
        NVEC = KC * (len(VECTORS) - 1) + HC
        vec_rows = sb("vec_rows", [NVEC, P])
        vecs = sb("vecs", [P, NVEC])
        g1, b1, g2, b2, wr, bq, bk, bq2, bk2, bv2 = (vecs[:, KC * n:KC * n + KC] for n in range(len(VECTORS) - 1))
        bf1 = vecs[:, KC * (len(VECTORS) - 1):NVEC]
        g1q = sb("g1q", [P, KC])
        wrg = sb("wrg", [P, KC])
        br_bc = sb("br_bc", [P, 1])
        bv_bc = sb("bv_bc", [P, D])
        bf2_bc = sb("bf2_bc", [P, D])
        bo_bc = sb("bo_bc", [SELN, D])
        b1wm_bc = sb("b1wm_bc", [96, D])
        neg_z0 = sb("neg_z0", [P, 1])

        space_n = sb("space_n", [P, TILES * D])
        space_t = [sb(f"space_t_{h}", [P, KC, GROUP], F16) for h in ("hi", "lo")]
        space_q = [sb(f"space_q_{h}", [P, KC, GROUP], F16) for h in ("hi", "lo")]
        space_k = sb("space_k", [P, TILES * D])
        space_v = sb("space_v", [P, 2, TILES * 2 * VROW], F16)
        space_p = [sb(f"space_p_{i}", [P, 2 * HEADS * NODES]) for i in range(1)][0]
        space_u = sb("space_u", [P, 4 * HEADS * NODES], F16)
        space_g = sb("space_g", [P, 2, GROUP])
        space_w = sb("space_w", [96, D])

        xin = sb("xin", [P, TILES, D])
        adj_in = sb("adj_in", [P, TILES, NODES])
        mask = sb("mask", [P, TILES, NODES])
        y = space_n[:, :].rearrange("p (t d) -> p t d", d=D)
        bn = sb("bn", [P, TILES, 6])

        def norm_buffers(k):
            return (sb(f"mv_{k}", [P, TILES, 2]), *(sb(f"{n}_{k}", [P, TILES]) for n in ("ve", "rstd", "mr", "nmr")))

        mv1, ve1, rstd1, mr1, nmr1 = norm_buffers(1)
        mv2, ve2, rstd2, mr2, nmr2 = norm_buffers(2)
        mvh, veh, rstdh, mrh, nmrh = norm_buffers("h")
        mv3, ve3, rstd3, mr3, nmr3 = norm_buffers(3)
        yT = space_t
        qT = space_q
        k_stage = space_k[:, :].bitcast(F16).rearrange("p (h c n) -> p h c n", h=2, c=KC)
        kB = sb("kB", [P, 2, 2 * KC, HQ, P], F16)
        v_stage = space_v[:, :, :].rearrange("p h (t w) -> p h t w", t=TILES)
        vB = sb("vB", [P, 2, 2, 2, 2 * VROW], F16)
        probs = [space_p[:, i * HEADS * NODES:(i + 1) * HEADS * NODES].rearrange("p (h n) -> p h n", n=NODES)
                 for i in range(2)]
        smax = sb("smax", [P, HEADS])
        pT = [[space_u[:, (2 * i + h) * PAIRS * P:(2 * i + h + 1) * PAIRS * P] for h in range(2)] for i in range(2)]
        rden = sb("rden", [P, HEADS])
        att = [space_g[:, i, 0:D] for i in range(2)]
        x1 = sb("x1", [P, TILES, D])

        hid = space_k[:, :].rearrange("p (t d) -> p t d", d=D)
        nh = y
        nT = space_t
        kT2 = space_q
        v2 = [space_v[:, h, 0:TILES * D].rearrange("p (t d) -> p t d", d=D) for h in range(2)]
        ez = sb("ez", [P, TILES])
        ez1 = sb("ez1", [P, TILES])
        score = sb("score", [P, TILES])
        diag = space_g[:, 0, :].rearrange("p (t n) -> p t n", n=P)
        scratch = sb("scratch", [P, 2 * TILES, P], F16)
        cnt_b = sb("cnt_b", [P, TILES])
        cnt_a = sb("cnt_a", [P, TILES])
        rank = sb("rank", [P, TILES])
        unchosen = sb("unchosen", [P, TILES])
        Z = sb("Z", [P, TILES * ZW + 112])
        Y3 = sb("Y3", [P, TILES * 96 + 80])
        selT = sb("selT", [SELN, GROUP], F16)
        sT = sb("sT", [96, GROUP], F16)
        gat = [sb(f"gat_{h}", [P, KC, SELN], F16) for h in ("hi", "lo")]
        pool = [sb(f"pool_{h}", [P, KC, 96], F16) for h in ("hi", "lo")]
        ssum = sb("ssum", [96, 1])
        ssum_e = sb("ssum_e", [96, 1])
        rsum = sb("rsum", [96, 1])
        pw = space_w
        R = sb("R", [96, D], F16)
        q2 = sb("q2", [P, KC, SELN])
        QCHUNK = GB * SROWS + HQ * TOPK
        qB = [space_p[:, :].bitcast(F16), space_u[:, :]]
        smax2 = sb("smax2", [SROWS, GB])
        den2 = sb("den2", [SROWS, GB])
        rden2 = sb("rden2", [SROWS, GB])
        p2 = space_n[0:SROWS, 0:GB * NODES].rearrange("p (b n) -> p b n", n=NODES)
        p2z = space_g[0:SROWS, :, :].rearrange("p a (b k) -> p (a b) k", k=P)
        p2T = [space_n[:, GB * NODES + h * GB * SROWS // 2:GB * NODES + (h + 1) * GB * SROWS // 2].bitcast(F16)
               .rearrange("p (b r) -> p b r", r=SROWS) for h in range(2)]
        ctxT = [sb(f"ctxT_{h}", [P, KC * SELN], F16) for h in ("hi", "lo")]
        A = space_w[0:SELN, :]
        Ah = [sb(f"A_{h}", [SELN, D], F16) for h in ("hi", "lo")]
        mixed = att
        n2 = y
        n2T = space_q
        resid = sb("resid", [P, TILES, D])
        gel = [space_g[:, i, :] for i in range(2)]
        hT = [sb(f"hT_{h}", [P, HC, GROUP], F16) for h in ("hi", "lo")]
        bm_bc = space_w
        setup_space = space_g[:, :, :].rearrange("p a b -> p (a b)")
        wr_bc = setup_space[:, 0:KC * P].rearrange("p (c k) -> p c k", c=KC)
        b1_bc = setup_space[:, KC * P:KC * (P + 96)].rearrange("p (c k) -> p c k", c=KC)
        bv2_bc = setup_space[:, KC * (P + 96):KC * (P + 96 + SELN)].rearrange("p (c k) -> p c k", c=KC)

        psum = ctx.enter_context(nc.psum_tensor("psum", [P, 8, 512], F32))

        def bank(i, rows=P, width=512):
            return psum[0:rows, i, 0:width]

        def banks(i, n, rows=P):
            return psum[0:rows, i:i + n, :]

        def along(buf, start, width, step, n=TILES):
            return buf[:, start:start + n * step].rearrange("p (t k) -> p t k", k=step)[:, :, 0:width]

        Z_tiles = along(Z, 0, ZW, ZW)
        Z_sel = along(Z, 0, 2 * TOPK, ZW + 2 * TOPK)
        Z_score = along(Z, SELN, 2, ZW + 2)
        Y3_tiles = along(Y3, 0, 96, 96)
        Y3_score = [along(Y3, o, 2, 98) for o in (0, 32, 64)]

        def qB_head(buf, i):
            q = buf[HD * i:HD * i + HD, TOPK * i:TOPK * i + KC * QCHUNK].rearrange("p (c k) -> p c k", k=QCHUNK)
            return q[:, :, 0:GB * SROWS].rearrange("p c (b k) -> p c b k", k=SROWS)[:, :, :, 0:TOPK]

        def qB_rows(buf, c, b):
            o = (c * GB + b) * SROWS
            return buf[:, o:o + SROWS]

        def cx_head(i):
            return psum[HD * i:HD * i + HD, 2:2 + KC, 0:GB * HQ * TOPK].rearrange(
                "p c (b k) -> p c b k", k=HQ * TOPK)[:, :, :, TOPK * i:TOPK * i + TOPK]

        def ctx_head(buf, i):
            return buf[HD * i:HD * i + HD, :].rearrange("p (c b q) -> p c b q", c=KC, q=TOPK)

        stage = [hT[0][:, :, :].rearrange("p a b -> p (a b)").bitcast(F32),
                 hT[1][:, :, :].rearrange("p a b -> p (a b)").bitcast(F32),
                 kB[:, :, :, :, :].rearrange("p t c i n -> p (t c i n)").bitcast(F32)]
        Q_BANK = [4, 5, 0]
        V2_BANK = [3, 4, 5, 3]
        T3_BANK = [2, 3, 5]
        F1_BEFORE_T1 = 4
        BIAS = {3: 1, 4: 1, 5: 1, 6: 1, 7: 1, 8: 1, 9: 1}
        BIAS_AFTER = [sum(BIAS.get(m, 0) for m in range(n + 1)) for n in range(12)]
        NCONST = 16 * 18
        POOL_SETUP = 10
        DVE_SETUP = 9

        names = """const_in vec_ps setup_dve setup_pool setup_act w_in0 w_in1 w_in2
            w_split bias_ps bias_set rows_in bm_rows
            x_in adj_in_ stats1 norm1 y_ready t1_ps yT_hi yT_lo k_ps k_hi k_lo kB_in0 kB_in1 v_ps v_hi v_lo vB_in0 vB_in1
            q_ps q_hi q_lo mask0_set ones_set xbv_set qB_clear p2z_clear adj_used s_ps s_read p_shift p_exp pt_ps pt_hi pt_lo pv_ps att_ready
            x1_ready stats2 norm2 hid_ready statsh normh nh_ready t2_ps nT_hi nT_lo v2_ps v2_hi v2_lo
            k2_ps k2_hi k2_lo diag_set bc_ps z_set selT_ps y3T_ps gp_ps selT_set sT_hi sT_set
            gat_hi gat_lo pool_hi pool_lo q2_ps q2_set qB_hi qB_lo pw_ps pw_set R_lo_set R_hi s2_ps
            p2_shift p2_exp p2_set pt2_ps p2T_hi p2T_lo cx_ps ctx_hi ctx_lo o_ps A_set A_hi A_lo
            mix_ps sc_ps mix_read h_ready stats3 norm3 n2_ready t3_ps n2T_hi n2T_lo resid_set
            f1_ps f1_hi f1_lo f2_ps o_ready out_done dve_step pool_step x1b_set""".split()
        s = {n: sem(n) for n in names}

        block = ctx.enter_context(nc.Block())

        def count(g, per, j):
            return g * per + j

        class Steps:

            def __init__(self, eng, sem_):
                self.eng, self.sem, self.per, self.n, self.g = eng, sem_, None, 0, 0

            def group(self, g, base):
                self.g, self.n, self.base = g, 0, base

            def done(self, ins):
                self.n += 1
                return ins.then_inc(self.sem, 1)

            def settle(self):
                if isinstance(self.g, int) and self.g == 0:
                    self.eng.wait_ge(self.sem, self.base + self.n)
                else:
                    self.eng.wait_ge(self.sem, self.g * self.per + (self.base + self.n))

            def close(self):
                if self.per is None:
                    self.per = self.n
                assert self.per == self.n, (self.per, self.n)

        def for_groups(eng, attention, feed, both):
            both(0, True, False)
            if groups > 1:
                with eng.Fori(1, groups) as g:
                    both(g, True, True)
            both(groups, False, True)

        LOADS = [("L0_gnn_Wq", KC, D), ("L0_gnn_Wk", KC, D), ("L0_gnn_Wv", KC, D), ("L0_ffn_Wv", KC, D),
                 ("L0_ffn_Wk", KC, D), ("L0_ffn_Wq", KC, D), ("L0_ffn_Wo", KC, D), ("L0_ffn_Wm", KC, D),
                 ("L0_ffn_W1", KC, HIDDEN // 2), ("L0_ffn_W1", KC, HIDDEN // 2),
                 ("L0_ffn_W2", HC // 2, D), ("L0_ffn_W2", HC // 2, D)]
        NST = len(stage)

        def staged(n):
            _, chunks, cols = LOADS[n]
            return stage[n % NST][:, 0:chunks * cols].rearrange("p (c n) -> p c n", c=chunks)

        SPLIT_STEPS = []
        for n_, (_, chunks_, _) in enumerate(LOADS):
            SPLIT_STEPS += [(n_, c_) for c_ in range(chunks_)]
        SPLIT_END = [sum(1 for m_, _ in SPLIT_STEPS if m_ <= n_) for n_ in range(len(LOADS))]

        def target(n, c, half_):
            name, src = LOADS[n][0], staged(n)[:, c, :]
            first_half = n % 2 == 0
            if name == "L0_gnn_Wq":
                return w_qk[half_][:, c, 0:D], src
            if name == "L0_gnn_Wk":
                return w_qk[half_][:, c, D:2 * D], src
            if name == "L0_gnn_Wv":
                return (w_v[half_][:, c, :].rearrange("p (e a d) -> p e a d", e=2, a=PAIRS),
                        src.rearrange("p (a e d) -> p e a d", e=2, a=PAIRS))
            if name == "L0_ffn_Wv":
                return w_v2[half_][:, c, 0:D], src
            if name == "L0_ffn_W1":
                o = 0 if first_half else HIDDEN // 2
                return w_1[half_][:, c, o:o + HIDDEN // 2], src
            if name == "L0_ffn_W2":
                return w_2[half_][:, c + (0 if first_half else HC // 2), :], src
            return {"L0_ffn_Wk": w_k2, "L0_ffn_Wq": w_q2, "L0_ffn_Wo": w_o, "L0_ffn_Wm": w_m}[name][half_][:, c, :], src

        def gain(n, c):
            name = LOADS[n][0]
            if name in ("L0_ffn_Wq", "L0_ffn_Wk", "L0_ffn_Wv", "L0_ffn_Wm"):
                return g1[:, c:c + 1]
            if name == "L0_ffn_W1":
                return g2[:, c:c + 1]
            return None

        x_v = x.rearrange("(g t p) d -> g p t d", p=P, t=TILES)
        adj_v = adj.rearrange("(g t p) d -> g p t d", p=P, t=TILES)
        out_v = out.rearrange("(g t p) d -> g p t d", p=P, t=TILES)

        def of_group(v, g):
            if isinstance(g, int):
                return v[g]
            return v[bass.ds(g, 1)].rearrange("o p t d -> (o p) t d")

        @block.sync
        def _(sp):
            def load_x(g):
                sp.dma_start(xin[:, :, :], of_group(x_v, g)).then_inc(s["x_in"], 16)
                sp.dma_start(adj_in[:, :, :], of_group(adj_v, g)).then_inc(s["adj_in_"], 16)

            def wide(dst, name, rows):
                sp.dma_start(dst, w[name].rearrange("(a n) -> a n", a=1).to_broadcast([rows, D]))\
                  .then_inc(s["const_in"], 16)

            sp.dma_start(const[:, :], consts).then_inc(s["const_in"], 16)
            for n, name in enumerate(VECTORS):
                rows = w[name].rearrange("(c p) -> c p", p=P)
                sp.dma_start(vec_rows[KC * n:KC * n + rows.shape[0], :], rows).then_inc(s["const_in"], 16)
            for dst, name, rows in ((bv_bc, "L0_gnn_bv", P), (bf2_bc, "L0_ffn_bf2", P),
                                    (bo_bc, "L0_ffn_bo", SELN), (bm_bc, "L0_ffn_bm", 96)):
                wide(dst[:, :], name, rows)
            for dst, name in ((beta_bc, "L0_gnn_beta"), (br_bc, "L0_ffn_br")):
                sp.dma_start(dst[:, :], w[name].rearrange("(a n) -> a n", a=1).to_broadcast([P, 1]))\
                  .then_inc(s["const_in"], 16)
            for n, (name, chunks, cols) in enumerate(LOADS):
                if n >= NST:
                    sp.wait_ge(s["w_split"], SPLIT_END[n - NST])
                    sp.wait_ge(s["bias_ps"], BIAS_AFTER[n - NST])
                src = w[name]
                if name == "L0_ffn_W1":
                    o = 0 if n % 2 == 0 else HIDDEN // 2
                    src = src[:, o:o + HIDDEN // 2]
                if name == "L0_ffn_W2":
                    o = 0 if n % 2 == 0 else HIDDEN // 2
                    src = src[o:o + HIDDEN // 2, :]
                sp.dma_start(staged(n), src.rearrange("(c p) n -> p c n", p=P)).then_inc(s[f"w_in{n % NST}"], 16)
                if n == 3:
                    load_x(0)
            sp.wait_ge(s["setup_pool"], POOL_SETUP)
            sp.wait_ge(s["bm_rows"], 2)
            sp.dma_start(R[73:74, :], Ah[0][0:1, :]).then_inc(s["rows_in"], 16)
            sp.dma_start(R[74:75, :], Ah[1][0:1, :]).then_inc(s["rows_in"], 16)

            def spread_k(t):
                for i in range(HQ):
                    q = slice(HD * i, HD * i + HD)
                    sp.dma_start(kB[q, t % 2, :, i, :],
                                 k_stage[q, :, :, t * P:(t + 1) * P].rearrange("p h c n -> p (h c) n"))\
                      .then_inc(s[f"kB_in{t % 2}"], 16)

            def spread_v(t):
                for b in range(2):
                    for e in range(2):
                        sp.dma_start(vB[64 * e:64 * e + 64, t % 2, :, b, e * VROW:(e + 1) * VROW],
                                     v_stage[64 * b:64 * b + 64, :, t, e * VROW:(e + 1) * VROW])\
                          .then_inc(s[f"vB_in{t % 2}"], 16)

            def both(g, attention, feed, more=True):
                if attention:
                    sp.wait_ge(s["k_lo"], count(g, KC, KC))
                    spread_k(0)
                    spread_k(1)
                    sp.wait_ge(s["v_lo"], count(g, TILES, TILES))
                    sp.wait_ge(s["ones_set"], count(g, 2, 2))
                    spread_v(0)
                    spread_v(1)
                    for t in range(2, TILES):
                        sp.wait_ge(s["s_ps"], count(g, TILES, t - 1))
                        spread_k(t)
                        sp.wait_ge(s["pv_ps"], count(g, TILES, t - 1))
                        spread_v(t)
                    if more:
                        sp.wait_ge(s["adj_used"], count(g, 1, 1))
                        sp.wait_ge(s["x1_ready"], count(g, TILES, TILES))
                        load_x(g + 1)
                if feed:
                    f = g - 1
                    sp.wait_ge(s["o_ready"], count(f, TILES, TILES))
                    sp.dma_start(of_group(out_v, f), resid[:, :, :]).then_inc(s["out_done"], 16)

            both(0, True, False)
            if groups > 2:
                with sp.Fori(1, groups - 1) as g:
                    both(g, True, True)
            if groups > 1:
                both(groups - 1, True, True, more=False)
            both(groups, False, True)
            sp.wait_ge(s["out_done"], 16 * groups)

        @block.gpsimd
        def _(pl):
            steps = Steps(pl, s["pool_step"])
            pl.memset(vB[:, :, :, :, :], 0.0).then_inc(s["setup_pool"], 1)
            for h in range(2):
                pl.memset(pool[h][:, :, :], 0.0).then_inc(s["setup_pool"], 1)
            pl.memset(R[:, :], 0.0).then_inc(s["setup_pool"], 1)
            pl.memset(Z[:, :], 0.0).then_inc(s["setup_pool"], 1)
            pl.memset(minus_half[:, :], -0.5).then_inc(s["setup_pool"], 1)
            pl.memset(minus_one[:, :], -1.0).then_inc(s["setup_pool"], 1)
            pl.memset(eps[:, :], EPS).then_inc(s["setup_pool"], 1)
            pl.memset(Y3[:, :], 0.0).then_inc(s["setup_pool"], 1)
            pl.wait_ge(s["setup_pool"], 9)
            pl.memset(Y3_tiles[:, :, 73:75], 1.0)
            pl.wait_ge(s["w_split"], SPLIT_END[-1])
            pl.wait_ge(s["bias_ps"], BIAS_AFTER[-1])
            pl.memset(kB[:, :, :, :, :], 0.0).then_inc(s["setup_pool"], 1)

            def norm(mean, var, ve, rstd, mr, nmr, signal):
                steps.done(pl.tensor_tensor(ve[:, :], var, eps[:, :], ALU.add))
                steps.settle()
                steps.done(pl.tensor_tensor(rstd[:, :], ve[:, :], minus_half[:, :], ALU.pow))
                steps.settle()
                steps.done(pl.tensor_tensor(mr[:, :], mean, rstd[:, :], ALU.mult))
                steps.settle()
                pl.tensor_tensor(nmr[:, :], mr[:, :], minus_one[:, :], ALU.mult).then_inc(signal, 1)

            def feed_lo(f, m):
                pl.wait_ge(s["f1_hi"], count(f, HC, m + 1))
                pl.tensor_tensor(hT[1][:, m, :], gel[m % 2][:, :], hT[0][:, m, :], ALU.subtract)\
                  .then_inc(s["f1_lo"], 1)

            def both(g, attention, feed):
                f = g - 1
                if attention:
                    steps.group(g, 0)
                    pl.wait_ge(s["stats1"], count(g, 1, 1))
                    pl.wait_ge(s["adj_in_"], count(g, 16, 16))
                    norm(mv1[:, :, 0], mv1[:, :, 1], ve1, rstd1, mr1, nmr1, s["norm1"])
                    pl.tensor_scalar(mask[:, :, :], adj_in[:, :, :], 0.0, MASKED, ALU.is_le, ALU.mult)\
                      .then_inc(s["mask0_set"], 1)
                    sums = [v_stage[:, h, :, :].rearrange("p t (a w) -> p (t a) w", w=VW)[:, :, HD:VW] for h in range(2)]
                    pl.memset(sums[0], 1.0).then_inc(s["ones_set"], 1)
                    pl.memset(sums[1], 0.0).then_inc(s["ones_set"], 1)
                    pl.wait_ge(s["const_in"], NCONST)
                    pl.wait_ge(s["y_ready"], count(g, TILES, TILES))
                    for t in range(TILES):
                        pl.tensor_tensor(xin[:, t, :], xin[:, t, :], bv_bc[:, :], ALU.add).then_inc(s["xbv_set"], 1)
                if feed:
                    for m in range(HC):
                        feed_lo(f, m)
                if attention:
                    for t in range(TILES):
                        pl.wait_ge(s["att_ready"], count(g, TILES, t + 1))
                        if t == 0:
                            pl.wait_ge(s["xbv_set"], count(g, TILES, TILES))
                        pl.tensor_tensor(x1[:, t, :], att[t % 2], xin[:, t, :], ALU.add).then_inc(s["x1_ready"], 1)
                    for h in range(2):
                        pl.memset(qB[h].bitcast(F32), 0.0).then_inc(s["qB_clear"], 1)
                    pl.wait_ge(s["stats2"], count(g, 1, 1))
                    norm(mv2[:, :, 0], mv2[:, :, 1], ve2, rstd2, mr2, nmr2, s["norm2"])
                    pl.wait_ge(s["statsh"], count(g, 1, 1))
                    norm(mvh[:, :, 0], mvh[:, :, 1], veh, rstdh, mrh, nmrh, s["normh"])
                    pl.wait_ge(s["hid_ready"], count(g, TILES, TILES))
                    for t in range(TILES):
                        if t == TILES - 1:
                            pl.wait_ge(s["bc_ps"], count(g, 1, 1))
                        pl.tensor_tensor(x1[:, t, :], x1[:, t, :], bf2_bc[:, :], ALU.add).then_inc(s["x1b_set"], 1)
                    pl.memset(space_g[0:SROWS, :, :], 0.0).then_inc(s["p2z_clear"], 1)
                    pl.wait_ge(s["stats3"], count(g, 1, 1))
                    norm(mv3[:, :, 0], mv3[:, :, 1], ve3, rstd3, mr3, nmr3, s["norm3"])
                    pl.wait_ge(s["x1b_set"], count(g, TILES, TILES))
                    if not (isinstance(g, int) and g == 0):
                        pl.wait_ge(s["out_done"], count(g, 16, 0))
                    for t in range(TILES):
                        pl.wait_ge(s["h_ready"], count(g, TILES, t + 1))
                        pl.tensor_tensor(resid[:, t, :], hid[:, t, :], x1[:, t, :], ALU.add)\
                          .then_inc(s["resid_set"], 1)
                    steps.close()

            for_groups(pl, None, None, both)

        @block.scalar
        def _(act):
            act.wait_ge(s["const_in"], NCONST)

            act.wait_ge(s["setup_dve"], 2)
            for i, (n, c) in enumerate(SPLIT_STEPS):
                if c == 0:
                    act.wait_ge(s[f"w_in{n % NST}"], 16 * (n // NST + 1))
                dst, src = target(n, c, 0)
                scale = gain(n, c)
                if LOADS[n][0] in ("L0_gnn_Wq",):
                    act.activation(dst, src, ACT.Copy, scale=QSCALE).then_inc(s["setup_act"], 1)
                elif LOADS[n][0] == "L0_ffn_Wq":
                    act.wait_ge(s["setup_dve"], 4)
                    act.activation(dst, src, ACT.Copy, scale=g1q[:, c:c + 1]).then_inc(s["setup_act"], 1)
                elif scale is None:
                    act.activation(dst, src, ACT.Copy).then_inc(s["setup_act"], 1)
                else:
                    act.activation(dst, src, ACT.Copy, scale=scale).then_inc(s["setup_act"], 1)
            act.wait_ge(s["setup_dve"], 5)
            act.activation(w_v2[0][:, :, D:D + 1], wrg[:, :].unsqueeze(2), ACT.Copy).then_inc(s["setup_act"], 1)
            act.wait_ge(s["bias_set"], 10)
            act.wait_ge(s["setup_dve"], DVE_SETUP)

            def feed_hi(f, m):
                act.wait_ge(s["f1_ps"], count(f, HC, m + 1))
                if m >= 2:
                    act.wait_ge(s["f1_lo"], count(f, HC, m - 1))
                act.activation(gel[m % 2], bank(6 + m % 2), ACT.Gelu, bias=bf1[:, m:m + 1])
                act.activation(hT[0][:, m, :], bank(6 + m % 2), ACT.Gelu, bias=bf1[:, m:m + 1])\
                   .then_inc(s["f1_hi"], 1)

            def both(g, attention, feed):
                f = g - 1
                feeds = list(range(HC)) if feed else []

                def fill(n):
                    for _ in range(n):
                        if feeds:
                            feed_hi(f, feeds.pop(0))

                if attention:
                    act.wait_ge(s["norm1"], count(g, 1, 1))
                    for t in range(TILES):
                        act.activation(y[:, t, :], xin[:, t, :], ACT.Identity, bias=nmr1[:, t:t + 1],
                                       scale=rstd1[:, t:t + 1]).then_inc(s["y_ready"], 1)
                    fill(F1_BEFORE_T1)
                    for c in range(KC):
                        act.wait_ge(s["t1_ps"], count(g, KC, c + 1))
                        act.copy(yT[0][:, c, :], bank(c)).then_inc(s["yT_hi"], 1)
                    fill(2)
                    for c in range(KC):
                        act.wait_ge(s["k_ps"], count(g, KC, c + 1))
                        if c == 0 and not (isinstance(g, int) and g == 0):
                            act.wait_ge(s["resid_set"], count(g, TILES, 0))
                        act.activation(k_stage[:, 0, c, :], bank(3 + c), ACT.Identity, bias=bk[:, c:c + 1])\
                           .then_inc(s["k_hi"], 1)
                        fill(1)
                    fill(HC)
                    for t in range(TILES):
                        act.wait_ge(s["v_ps"], count(g, TILES, t + 1))
                        act.copy(v_stage[:, 0, t, :].rearrange("p (a w) -> p a w", w=VW)[:, :, 0:HD],
                                 bank(t, width=D).rearrange("p (a d) -> p a d", d=HD)).then_inc(s["v_hi"], 1)
                    for c in range(KC):
                        act.wait_ge(s["q_ps"], count(g, KC, c + 1))
                        act.activation(qT[0][:, c, :], bank(Q_BANK[c]), ACT.Identity, bias=bq[:, c:c + 1])\
                           .then_inc(s["q_hi"], 1)
                fill(HC)
                if not attention:
                    return
                def expo(t):
                    act.wait_ge(s["p_shift"], count(g, TILES, t + 1))
                    act.activation(probs[t % 2][:, :, :], probs[t % 2][:, :, :], ACT.Exp).then_inc(s["p_exp"], 1)

                def turned(t):
                    act.wait_ge(s["pt_ps"], count(g, TILES, t + 1))
                    act.copy(pT[t % 2][0].rearrange("p (b n) -> p b n", b=2), banks(0, 2)[:, :, 0:D])\
                       .then_inc(s["pt_hi"], 1)

                expo(0)
                expo(1)
                turned(0)
                expo(2)
                turned(1)
                expo(3)
                turned(2)
                turned(3)
                act.wait_ge(s["norm2"], count(g, 1, 1))
                for t in range(TILES):
                    act.activation(hid[:, t, :], x1[:, t, :], ACT.Identity, bias=nmr2[:, t:t + 1],
                                   scale=rstd2[:, t:t + 1]).then_inc(s["hid_ready"], 1)
                act.wait_ge(s["normh"], count(g, 1, 1))
                for t in range(TILES):
                    act.activation(nh[:, t, :], hid[:, t, :], ACT.Identity, bias=nmrh[:, t:t + 1],
                                   scale=rstdh[:, t:t + 1]).then_inc(s["nh_ready"], 1)
                for c in range(KC):
                    act.wait_ge(s["t2_ps"], count(g, KC, c + 1))
                    act.copy(nT[0][:, c, :], bank(c)).then_inc(s["nT_hi"], 1)
                for t in range(TILES):
                    act.wait_ge(s["v2_ps"], count(g, TILES, t + 1))
                    act.activation(ez[:, t:t + 1], bank(V2_BANK[t])[:, D:D + 1], ACT.Exp, bias=neg_z0[:, 0:1],
                                   scale=-1.0)
                    act.copy(v2[0][:, t, :], bank(V2_BANK[t], width=D)).then_inc(s["v2_hi"], 1)
                for c in range(KC):
                    act.wait_ge(s["k2_ps"], count(g, KC, c + 1))
                    act.activation(kT2[0][:, c, :], bank(c), ACT.Identity, bias=bk2[:, c:c + 1])\
                       .then_inc(s["k2_hi"], 1)
                act.wait_ge(s["gp_ps"], count(g, 1, 1))
                gp = bank(0, width=KC * ZW).rearrange("p (c k) -> p c k", k=ZW)
                act.copy(gat[0][:, :, :], gp[:, :, 0:SELN]).then_inc(s["gat_hi"], 1)
                for o in (0, 32, 64):
                    last = act.copy(pool[0][:, :, o:o + GB], gp[:, :, SELN:ZW])
                last.then_inc(s["pool_hi"], 1)
                act.wait_ge(s["selT_ps"], count(g, 1, 1))
                act.copy(selT[:, :], bank(5, SELN)).then_inc(s["selT_set"], 1)
                act.wait_ge(s["y3T_ps"], count(g, 1, 1))
                act.copy(sT[:, :], bank(3, 96)).then_inc(s["sT_hi"], 1)
                act.wait_ge(s["q2_set"], count(g, 1, 1))
                act.wait_ge(s["qB_clear"], count(g, 2, 2))
                for i in range(HQ):
                    last = act.copy(qB_head(qB[0], i),
                                    q2[HD * i:HD * i + HD, :, :].rearrange("p c (b q) -> p c b q", q=TOPK))
                last.then_inc(s["qB_hi"], 1)
                act.wait_ge(s["pw_set"], count(g, 1, 1))
                act.copy(R[0:64, :], pw[0:64, :])
                act.copy(R[64:64 + GB, :], pw[64:64 + GB, :]).then_inc(s["R_hi"], 1)
                act.wait_ge(s["p2_shift"], count(g, 1, 1))
                act.activation(p2, p2, ACT.Exp).then_inc(s["p2_exp"], 1)
                act.wait_ge(s["pt2_ps"], count(g, 1, 1))
                half_bank = GB // 2 * SROWS
                act.copy(p2T[0].rearrange("p (h b) r -> p h (b r)", h=2), banks(0, 2)[:, :, 0:half_bank])\
                   .then_inc(s["p2T_hi"], 1)
                act.wait_ge(s["cx_ps"], count(g, 1, 1))
                for i in range(HQ):
                    last = act.copy(ctx_head(ctxT[0], i), cx_head(i))
                last.then_inc(s["ctx_hi"], 1)
                act.wait_ge(s["A_set"], count(g, 1, 1))
                act.copy(Ah[0][:, :], A).then_inc(s["A_hi"], 1)
                act.wait_ge(s["norm3"], count(g, 1, 1))
                for t in range(TILES):
                    act.activation(n2[:, t, :], hid[:, t, :], ACT.Identity, bias=nmr3[:, t:t + 1],
                                   scale=rstd3[:, t:t + 1]).then_inc(s["n2_ready"], 1)
                for c in range(KC):
                    act.wait_ge(s["t3_ps"], count(g, KC, c + 1))
                    act.copy(n2T[0][:, c, :], bank(T3_BANK[c])).then_inc(s["n2T_hi"], 1)

            for_groups(act, None, None, both)

        @block.vector
        def _(dve):
            steps = Steps(dve, s["dve_step"])
            dve.memset(ones[:, :], 1.0).then_inc(s["setup_dve"], 1)
            dve.wait_ge(s["const_in"], NCONST)
            dve.wait_ge(s["vec_ps"], 1)
            dve.tensor_copy(vecs[:, :], bank(7, width=NVEC)).then_inc(s["setup_dve"], 1)
            dve.wait_ge(s["setup_dve"], 2)
            dve.tensor_scalar(bq, bq, QSCALE, None, ALU.mult).then_inc(s["setup_dve"], 1)
            dve.tensor_scalar(g1q[:, :], g1, QSCALE, None, ALU.mult).then_inc(s["setup_dve"], 1)
            dve.tensor_tensor(wrg[:, :], wr, g1, ALU.mult).then_inc(s["setup_dve"], 1)
            dve.tensor_copy(wr_bc, wr.unsqueeze(2).to_broadcast([P, KC, P])).then_inc(s["setup_dve"], 1)
            dve.tensor_copy(b1_bc, b1.unsqueeze(2).to_broadcast([P, KC, 96])).then_inc(s["setup_dve"], 1)

            def bias_sums(n):
                name = LOADS[n][0]
                dve.wait_ge(s["bias_ps"], BIAS_AFTER[n])
                ps = bank(n % 8)
                if name == "L0_ffn_Wv":
                    dve.tensor_tensor(bv2, ps[:, 0:KC], bv2, ALU.add).then_inc(s["bias_set"], 1)
                    dve.wait_ge(s["bias_set"], 1)
                    dve.tensor_copy(bv2_bc, bv2.unsqueeze(2).to_broadcast([P, KC, SELN]))\
                       .then_inc(s["bias_set"], 1)
                    dve.scalar_tensor_tensor(neg_z0[:, :], ps[:, KC:KC + 1], -1.0, br_bc[:, :], ALU.mult, ALU.subtract)\
                       .then_inc(s["bias_set"], 1)
                if name == "L0_ffn_Wk":
                    dve.tensor_tensor(bk2, ps[:, 0:KC], bk2, ALU.add).then_inc(s["bias_set"], 1)
                if name == "L0_ffn_Wq":
                    dve.tensor_tensor(bq2, ps[:, 0:KC], bq2, ALU.add).then_inc(s["bias_set"], 1)
                if name == "L0_ffn_Wo":
                    dve.tensor_tensor(bo_bc[:, :], ps[0:SELN, 0:D], bo_bc[:, :], ALU.add).then_inc(s["bias_set"], 1)
                if name == "L0_ffn_Wm":
                    dve.tensor_copy(b1wm_bc[:, :], ps[0:96, 0:D]).then_inc(s["bias_set"], 1)
                    dve.tensor_tensor(bm_bc[:, :], ps[0:96, 0:D], bm_bc[:, :], ALU.add).then_inc(s["bias_set"], 1)
                    dve.wait_ge(s["bias_set"], 8)
                    dve.tensor_copy(Ah[0][0:1, :], bm_bc[0:1, :]).then_inc(s["bm_rows"], 1)
                    dve.wait_ge(s["bm_rows"], 1)
                    dve.tensor_tensor(Ah[1][0:1, :], bm_bc[0:1, :], Ah[0][0:1, :], ALU.subtract).then_inc(s["bm_rows"], 1)
                if name == "L0_ffn_W1":
                    o = 0 if n % 2 == 0 else HC // 2
                    dve.tensor_tensor(bf1[:, o:o + HC // 2], ps[:, 0:HC // 2], bf1[:, o:o + HC // 2], ALU.add)\
                       .then_inc(s["bias_set"], 1)

            for i, (n, c) in enumerate(SPLIT_STEPS):
                dve.wait_ge(s["setup_act"], i + 1)
                dst, src = target(n, c, 1)
                hi, _ = target(n, c, 0)
                scale = gain(n, c)
                if LOADS[n][0] == "L0_ffn_Wq":
                    dve.wait_ge(s["setup_dve"], 4)
                    scale = g1q[:, c:c + 1]
                if LOADS[n][0] == "L0_gnn_Wq":
                    scale = QSCALE
                if scale is None:
                    ins = dve.tensor_tensor(dst, src, hi, ALU.subtract)
                else:
                    ins = dve.scalar_tensor_tensor(dst, src, scale, hi, ALU.mult, ALU.subtract)
                ins.then_inc(s["w_split"], 1)
                if c == LOADS[n][1] - 1 and n in BIAS:
                    bias_sums(n)
            dve.wait_ge(s["setup_act"], len(SPLIT_STEPS) + 1)
            dve.tensor_tensor(w_v2[1][:, :, D:D + 1], wrg[:, :].unsqueeze(2), w_v2[0][:, :, D:D + 1], ALU.subtract)\
               .then_inc(s["setup_dve"], 1)
            dve.wait_ge(s["bias_set"], 5)
            dve.tensor_scalar(bq2, bq2, QSCALE, None, ALU.mult).then_inc(s["setup_dve"], 1)
            dve.wait_ge(s["setup_dve"], DVE_SETUP)

            def stats(src, mv, signal):
                for t in range(TILES):
                    steps.done(dve.bn_stats(bn[:, t, :], src(t)))
                steps.settle()
                steps.done(dve.memset(pause[:, :], 0.0))
                for t in range(TILES):
                    last = dve.bn_aggr(mv[:, t, :], bn[:, t, :])
                last.then_inc(signal, 1)

            def summed(f, t):
                dve.wait_ge(s["resid_set"], count(f, TILES, t + 1))
                dve.wait_ge(s["f2_ps"], count(f, TILES, t + 1))
                dve.tensor_tensor(resid[:, t, :], bank(6 + t % 2, width=D), resid[:, t, :], ALU.add)\
                   .then_inc(s["o_ready"], 1)

            def both(g, attention, feed):
                f = g - 1
                if attention:
                    steps.group(g, 0)
                    dve.wait_ge(s["x_in"], count(g, 16, 16))
                    stats(lambda t: xin[:, t, :], mv1, s["stats1"])
                    dve.wait_ge(s["mask0_set"], count(g, 1, 1))
                    dve.scalar_tensor_tensor(mask[:, :, :], adj_in[:, :, :], beta_bc[:, 0:1], mask[:, :, :],
                                             ALU.mult, ALU.add).then_inc(s["adj_used"], 1)
                    dve.wait_ge(s["adj_used"], count(g, 1, 1))
                    for c in range(KC):
                        dve.wait_ge(s["yT_hi"], count(g, KC, c + 1))
                        dve.tensor_tensor(yT[1][:, c, :], bank(c), yT[0][:, c, :], ALU.subtract)\
                           .then_inc(s["yT_lo"], 1)
                    for c in range(KC):
                        dve.wait_ge(s["k_hi"], count(g, KC, c + 1))
                        dve.scalar_tensor_tensor(k_stage[:, 1, c, :], bank(3 + c), bk[:, c:c + 1],
                                                 k_stage[:, 0, c, :], ALU.add, ALU.subtract).then_inc(s["k_lo"], 1)
                    for t in range(TILES):
                        dve.wait_ge(s["v_hi"], count(g, TILES, t + 1))
                        vs = [v_stage[:, h, t, :].rearrange("p (a w) -> p a w", w=VW)[:, :, 0:HD] for h in range(2)]
                        dve.tensor_tensor(vs[1], bank(t, width=D).rearrange("p (a d) -> p a d", d=HD), vs[0],
                                          ALU.subtract).then_inc(s["v_lo"], 1)
                    for c in range(KC):
                        dve.wait_ge(s["q_hi"], count(g, KC, c + 1))
                        dve.scalar_tensor_tensor(qT[1][:, c, :], bank(Q_BANK[c]), bq[:, c:c + 1],
                                                 qT[0][:, c, :], ALU.add, ALU.subtract).then_inc(s["q_lo"], 1)

                def shift(t):
                    pr = probs[t % 2]
                    sp_ = psum[:, 2 + 2 * (t % 2):4 + 2 * (t % 2), :].rearrange("p b n -> p (b n)")
                    sc = sp_[:, 0:HEADS * NODES].rearrange("p (h n) -> p h n", n=NODES)
                    dve.wait_ge(s["s_ps"], count(g, TILES, t + 1))
                    if t >= 2:
                        dve.wait_ge(s["pt_ps"], count(g, TILES, t - 1))
                    dve.tensor_tensor(pr, sc, mask[:, t, :].unsqueeze(1).to_broadcast([P, HEADS, NODES]),
                                      ALU.add).then_inc(s["s_read"], 1)
                    dve.wait_ge(s["s_read"], count(g, TILES, t + 1))
                    steps.done(dve.tensor_reduce(smax[:, :], pr, AX_X, ALU.max))
                    steps.settle()
                    dve.tensor_tensor(pr, pr, smax[:, :].unsqueeze(2).to_broadcast([P, HEADS, NODES]),
                                      ALU.subtract).then_inc(s["p_shift"], 1)

                def turned(t):
                    dve.wait_ge(s["pt_hi"], count(g, TILES, t + 1))
                    dve.tensor_tensor(pT[t % 2][1].rearrange("p (b n) -> p b n", b=2), banks(0, 2)[:, :, 0:D],
                                      pT[t % 2][0].rearrange("p (b n) -> p b n", b=2), ALU.subtract)\
                       .then_inc(s["pt_lo"], 1)

                def weighted(t):
                    pv = bank(t % 2, width=HEADS * VW).rearrange("p (h w) -> p h w", w=VW)
                    dve.wait_ge(s["pv_ps"], count(g, TILES, t + 1))
                    steps.done(dve.reciprocal(rden[:, :].unsqueeze(2), pv[:, :, HD:VW]))
                    steps.settle()
                    if t >= 2:
                        dve.wait_ge(s["x1_ready"], count(g, TILES, t - 1))
                    dve.tensor_tensor(att[t % 2].rearrange("p (h d) -> p h d", d=HD), pv[:, :, 0:HD],
                                      rden[:, :].unsqueeze(2).to_broadcast([P, HEADS, HD]), ALU.mult)\
                       .then_inc(s["att_ready"], 1)

                if attention:
                    shift(0)
                    shift(1)
                if feed:
                    summed(f, 0)
                if attention:
                    turned(0)
                    shift(2)
                    weighted(0)
                    turned(1)
                    shift(3)
                if feed:
                    summed(f, 1)
                if attention:
                    weighted(1)
                    turned(2)
                    weighted(2)
                    turned(3)
                if feed:
                    summed(f, 2)
                if attention:
                    weighted(3)
                    dve.wait_ge(s["x1_ready"], count(g, TILES, TILES))
                    stats(lambda t: x1[:, t, :], mv2, s["stats2"])
                    dve.wait_ge(s["hid_ready"], count(g, TILES, TILES))
                    stats(lambda t: hid[:, t, :], mvh, s["statsh"])
                    for c in range(KC):
                        dve.wait_ge(s["nT_hi"], count(g, KC, c + 1))
                        dve.tensor_tensor(nT[1][:, c, :], bank(c), nT[0][:, c, :], ALU.subtract)\
                           .then_inc(s["nT_lo"], 1)
                    for t in range(TILES):
                        dve.wait_ge(s["v2_hi"], count(g, TILES, t + 1))
                        dve.tensor_tensor(v2[1][:, t, :], bank(V2_BANK[t], width=D), v2[0][:, t, :], ALU.subtract)\
                           .then_inc(s["v2_lo"], 1)
                    steps.done(dve.tensor_scalar(ez1[:, :], ez[:, :], 1.0, None, ALU.add))
                    steps.settle()
                    steps.done(dve.reciprocal(score[:, :], ez1[:, :]))
                    steps.settle()
                    for t in range(TILES):
                        last = dve.tensor_scalar(diag[:, t, :], ident, score[:, t:t + 1], None, ALU.mult)
                    last.then_inc(s["diag_set"], 1)
                    for c in range(KC):
                        dve.wait_ge(s["k2_hi"], count(g, KC, c + 1))
                        dve.scalar_tensor_tensor(kT2[1][:, c, :], bank(c), bk2[:, c:c + 1], kT2[0][:, c, :],
                                                 ALU.add, ALU.subtract).then_inc(s["k2_lo"], 1)
                    dve.wait_ge(s["bc_ps"], count(g, 1, 1))
                    for t in range(TILES):
                        everyone = bank(4)[:, t * P:(t + 1) * P]
                        dve.scalar_tensor_tensor(scratch[:, 2 * t, :], everyone, score[:, t:t + 1], before, ALU.is_le,
                                                 ALU.mult, accum_out=cnt_b[:, t:t + 1])
                        last = dve.scalar_tensor_tensor(scratch[:, 2 * t + 1, :], everyone, score[:, t:t + 1], after, ALU.is_lt,
                                                        ALU.mult, accum_out=cnt_a[:, t:t + 1])
                        steps.done(last)
                    steps.settle()
                    steps.done(dve.tensor_tensor(rank[:, :], cnt_b[:, :], cnt_a[:, :], ALU.add))
                    steps.settle()
                    dve.tensor_scalar(unchosen[:, :], rank[:, :], float(TOPK), None, ALU.is_ge)
                    dve.tensor_tensor(Z_sel, iota.unsqueeze(1).to_broadcast([P, TILES, 2 * TOPK]),
                                      rank[:, :].unsqueeze(2).to_broadcast([P, TILES, 2 * TOPK]), ALU.is_equal)
                    halves = half.unsqueeze(1).to_broadcast([P, TILES, 2])
                    scores2 = score[:, :].unsqueeze(2).to_broadcast([P, TILES, 2])
                    for v in Y3_score:
                        dve.tensor_tensor(v, halves, scores2, ALU.mult)
                    dve.tensor_tensor(Z_score, halves, scores2, ALU.mult).then_inc(s["z_set"], 1)
                    gp = bank(0, width=KC * ZW).rearrange("p (c k) -> p c k", k=ZW)
                    dve.wait_ge(s["gat_hi"], count(g, 1, 1))
                    dve.wait_ge(s["pool_hi"], count(g, 1, 1))
                    dve.tensor_tensor(gat[1][:, :, :], gp[:, :, 0:SELN], gat[0][:, :, :], ALU.subtract)\
                       .then_inc(s["gat_lo"], 1)
                    for o in (0, 32, 64):
                        dve.tensor_tensor(pool[1][:, :, o:o + GB], gp[:, :, SELN:ZW], pool[0][:, :, o:o + GB],
                                          ALU.subtract)
                    steps.done(dve.tensor_copy(ssum[:, :], bank(0, 96)[:, 300:301]))
                    steps.settle()
                    steps.done(dve.tensor_scalar(ssum_e[:, :], ssum[:, :], 1e-6, None, ALU.add))
                    steps.settle()
                    dve.reciprocal(rsum[:, :], ssum_e[:, :]).then_inc(s["pool_lo"], 1)
                    dve.wait_ge(s["sT_hi"], count(g, 1, 1))
                    dve.tensor_tensor(sT[32:64, :], psum[32:64, 3, :], sT[32:64, :], ALU.subtract)\
                       .then_inc(s["sT_set"], 1)
                    dve.wait_ge(s["q2_ps"], count(g, 1, 1))
                    q2p = bank(1, width=KC * SELN).rearrange("p (c k) -> p c k", k=SELN)
                    dve.tensor_tensor(q2[:, :, :], q2p, bq2.unsqueeze(2).to_broadcast([P, KC, SELN]), ALU.add)\
                       .then_inc(s["q2_set"], 1)
                    dve.wait_ge(s["qB_hi"], count(g, 1, 1))
                    for i in range(HQ):
                        last = dve.tensor_tensor(qB_head(qB[1], i),
                                                 q2[HD * i:HD * i + HD, :, :].rearrange("p c (b q) -> p c b q", q=TOPK),
                                                 qB_head(qB[0], i), ALU.subtract)
                    last.then_inc(s["qB_lo"], 1)
                    dve.wait_ge(s["pw_ps"], count(g, 1, 1))
                    dve.wait_ge(s["pool_lo"], count(g, 1, 1))
                    steps.done(dve.scalar_tensor_tensor(pw[:, :], b1wm_bc[:, :], ssum[:, 0:1], bank(2, 96, D),
                                                        ALU.mult, ALU.add))
                    steps.settle()
                    dve.tensor_scalar(pw[:, :], pw[:, :], rsum[:, 0:1], None, ALU.mult)\
                       .then_inc(s["pw_set"], 1)
                    dve.wait_ge(s["R_hi"], count(g, 1, 1))
                    dve.tensor_tensor(R[64:64 + GB, :], pw[64:64 + GB, :], R[64:64 + GB, :], ALU.subtract)\
                       .then_inc(s["R_lo_set"], 1)
                if feed:
                    summed(f, 3)
                if not attention:
                    return
                dve.wait_ge(s["s2_ps"], count(g, 1, 1))
                s2 = bank(4, SROWS).rearrange("p (b n) -> p b n", n=NODES)
                steps.done(dve.tensor_reduce(smax2[:, :], s2, AX_X, ALU.max))
                steps.settle()
                dve.tensor_tensor(p2, s2, smax2[:, :].unsqueeze(2).to_broadcast([SROWS, GB, NODES]),
                                  ALU.subtract).then_inc(s["p2_shift"], 1)
                dve.wait_ge(s["p2_exp"], count(g, 1, 1))
                steps.done(dve.tensor_reduce(den2[:, :], p2, AX_X, ALU.add))
                steps.settle()
                steps.done(dve.reciprocal(rden2[:, :], den2[:, :]))
                steps.settle()
                dve.wait_ge(s["p2z_clear"], count(g, 1, 1))
                for b in range(2):
                    o = NODES * b
                    last = dve.tensor_tensor(
                        p2z.rearrange("p (t b) k -> p t b k", b=2)[:, :, b, o:o + NODES],
                        p2.rearrange("p (t b) n -> p t b n", b=2)[:, :, b, :],
                        rden2[:, :].rearrange("p (t b) -> p t b", b=2)[:, :, b].unsqueeze(2)
                        .to_broadcast([SROWS, TILES, NODES]), ALU.mult)
                last.then_inc(s["p2_set"], 1)
                half_bank = GB // 2 * SROWS
                dve.wait_ge(s["p2T_hi"], count(g, 1, 1))
                p2v = [p2T[h].rearrange("p (h b) r -> p h (b r)", h=2) for h in range(2)]
                dve.tensor_tensor(p2v[1], banks(0, 2)[:, :, 0:half_bank], p2v[0], ALU.subtract)\
                   .then_inc(s["p2T_lo"], 1)
                dve.wait_ge(s["ctx_hi"], count(g, 1, 1))
                for i in range(HQ):
                    last = dve.tensor_tensor(ctx_head(ctxT[1], i), cx_head(i), ctx_head(ctxT[0], i), ALU.subtract)
                last.then_inc(s["ctx_lo"], 1)
                dve.wait_ge(s["o_ps"], count(g, 1, 1))
                dve.tensor_tensor(A, bank(5, SELN, D), bo_bc[:, :], ALU.add).then_inc(s["A_set"], 1)
                dve.wait_ge(s["A_hi"], count(g, 1, 1))
                dve.tensor_tensor(Ah[1][:, :], A, Ah[0][:, :], ALU.subtract).then_inc(s["A_lo"], 1)
                for t in range(TILES):
                    dve.wait_ge(s["mix_ps"], count(g, TILES, t + 1))
                    dve.scalar_tensor_tensor(mixed[t % 2], bank(t % 2, width=D), unchosen[:, t:t + 1],
                                             hid[:, t, :], ALU.mult, ALU.add).then_inc(s["mix_read"], 1)
                    dve.wait_ge(s["mix_read"], count(g, TILES, t + 1))
                    dve.wait_ge(s["sc_ps"], count(g, TILES, t + 1))
                    dve.tensor_tensor(hid[:, t, :], bank(4 + t % 2, width=D), mixed[t % 2], ALU.add)\
                       .then_inc(s["h_ready"], 1)
                dve.wait_ge(s["h_ready"], count(g, TILES, TILES))
                stats(lambda t: hid[:, t, :], mv3, s["stats3"])
                for c in range(KC):
                    dve.wait_ge(s["n2T_hi"], count(g, KC, c + 1))
                    dve.tensor_tensor(n2T[1][:, c, :], bank(T3_BANK[c]), n2T[0][:, c, :], ALU.subtract)\
                       .then_inc(s["n2T_lo"], 1)
                steps.close()

            for_groups(dve, None, None, both)

        @block.tensor
        def _(pe):
            def product(o, lhs, rhs, terms, before_term=None):
                n, total_ = 0, 3 * len(terms)
                for k in terms:
                    if before_term is not None:
                        before_term(k)
                    for a, b in ((0, 0), (0, 1), (1, 0)):
                        last = pe.matmul(o, lhs(k, a), rhs(k, b), start=(n == 0), stop=(n == total_ - 1))
                        n += 1
                return last

            def turn(src, ready, per, g, bank_of, signal):
                for t in range(TILES):
                    pe.wait_ge(ready, count(g, per, t + 1))
                    for c in range(KC):
                        last = pe.transpose(bank(bank_of[c])[:, t * P:(t + 1) * P], src[:, t, c * P:(c + 1) * P], ident)
                        if t == TILES - 1:
                            last.then_inc(signal, 1)

            pe.wait_ge(s["const_in"], NCONST)
            pe.transpose(bank(7, width=NVEC), vec_rows[:, :], const[0:NVEC, C_ID:C_ID + NVEC]).then_inc(s["vec_ps"], 1)
            pe.wait_ge(s["setup_dve"], 7)
            for n, (name, chunks, cols) in enumerate(LOADS):
                if n not in BIAS:
                    continue
                pe.wait_ge(s[f"w_in{n % NST}"], 16 * (n // NST + 1))
                ps = bank(n % 8)
                W = staged(n)
                if name in ("L0_ffn_Wv", "L0_ffn_Wk", "L0_ffn_Wq", "L0_ffn_W1"):
                    shift_ = b2 if name == "L0_ffn_W1" else b1
                    for m in range(cols // P):
                        for c in range(KC):
                            last = pe.matmul(ps[:, m:m + 1], W[:, c, m * P:(m + 1) * P], shift_[:, c:c + 1],
                                             start=(c == 0), stop=(c == KC - 1))
                    if name == "L0_ffn_Wv":
                        for c in range(KC):
                            last = pe.matmul(ps[:, KC:KC + 1], wr_bc[:, c, :], b1[:, c:c + 1], start=(c == 0),
                                             stop=(c == KC - 1))
                elif name == "L0_ffn_Wo":
                    pe.wait_ge(s["bias_set"], 2)
                    for c in range(KC):
                        last = pe.matmul(ps[0:SELN, 0:D], bv2_bc[:, c, :], W[:, c, :], start=(c == 0), stop=(c == KC - 1))
                else:
                    for c in range(KC):
                        last = pe.matmul(ps[0:96, 0:D], b1_bc[:, c, :], W[:, c, :], start=(c == 0), stop=(c == KC - 1))
                last.then_inc(s["bias_ps"], 1)
            pe.wait_ge(s["w_split"], SPLIT_END[-1])
            pe.wait_ge(s["setup_dve"], DVE_SETUP)
            pe.wait_ge(s["bias_set"], 10)
            pe.wait_ge(s["setup_pool"], POOL_SETUP)
            pe.wait_ge(s["rows_in"], 32)

            def feed1(f, m):
                if m >= 2:
                    pe.wait_ge(s["f1_hi"], count(f, HC, m - 1))
                product(bank(6 + m % 2), lambda c, h: w_1[h][:, c, m * P:(m + 1) * P],
                        lambda c, h: n2T[h][:, c, :], range(KC)).then_inc(s["f1_ps"], 1)

            def feed2(f, t, part):
                if part == 0:
                    if t == 0:
                        pe.wait_ge(s["f1_lo"], count(f, HC, HC))
                    if t < 2:
                        pe.wait_ge(s["f1_hi"], count(f, HC, HC - 1 + t))
                    else:
                        pe.wait_ge(s["o_ready"], count(f, TILES, t - 1))
                n = part * HC // 3 * 3
                for m in range(part * HC // 3, (part + 1) * HC // 3):
                    for a, b in ((0, 0), (0, 1), (1, 0)):
                        last = pe.matmul(bank(6 + t % 2, width=D), hT[a][:, m, t * P:(t + 1) * P], w_2[b][:, m, :],
                                         start=(n == 0), stop=(n == 3 * HC - 1))
                        n += 1
                if part == 2:
                    last.then_inc(s["f2_ps"], 1)

            def both(g, attention, feed):
                f = g - 1
                later = not (isinstance(g, int) and g == 0)
                feeds1 = list(range(HC)) if feed else []
                feeds2 = [(t, part) for t in range(TILES) for part in range(3)] if feed else []

                def fill1(n):
                    for _ in range(n):
                        if feeds1:
                            feed1(f, feeds1.pop(0))

                def fill2(n):
                    for _ in range(n):
                        if feeds2:
                            feed2(f, *feeds2.pop(0))

                if feed:
                    pe.wait_ge(s["n2T_lo"], count(f, KC, KC))
                if attention:
                    fill1(F1_BEFORE_T1)
                    turn(y, s["y_ready"], TILES, g, [0, 1, 2], s["t1_ps"])
                    fill1(2)
                    for m in range(KC):
                        product(bank(3 + m), lambda c, h: w_qk[h][:, c, D + m * P:D + (m + 1) * P],
                                lambda c, h: yT[h][:, c, :], range(KC),
                                (lambda c: pe.wait_ge(s["yT_lo"], count(g, KC, c + 1))) if m == 0 else None)\
                            .then_inc(s["k_ps"], 1)
                        fill1(1)
                    fill1(HC)
                    for t in range(TILES):
                        if t == 3:
                            pe.wait_ge(s["k_lo"], count(g, KC, 1))
                        product(bank(t, width=D), lambda c, h: yT[h][:, c, t * P:(t + 1) * P],
                                lambda c, h: w_v[h][:, c, :], range(KC)).then_inc(s["v_ps"], 1)
                    for m in range(KC):
                        if m < 2:
                            pe.wait_ge(s["k_lo"], count(g, KC, m + 2))
                        else:
                            pe.wait_ge(s["v_lo"], count(g, TILES, 1))
                        product(bank(Q_BANK[m]), lambda c, h: w_qk[h][:, c, m * P:(m + 1) * P],
                                lambda c, h: yT[h][:, c, :], range(KC)).then_inc(s["q_ps"], 1)
                fill1(HC)

                def scores(t):
                    if t == 0:
                        pe.wait_ge(s["q_lo"], count(g, KC, KC))
                        pe.wait_ge(s["v_lo"], count(g, TILES, TILES))
                    if t >= 2:
                        pe.wait_ge(s["s_read"], count(g, TILES, t - 1))
                    pe.wait_ge(s[f"kB_in{t % 2}"], count(g, 128, 64 * (t // 2 + 1)))
                    for b in range(2):
                        own = slice(b * NODES, (b + 1) * NODES)
                        tok = slice(t * P + b * NODES, t * P + (b + 1) * NODES)
                        for c in range(KC):
                            o = psum[b * NODES:(b + 1) * NODES, 2 + 2 * (t % 2) + c // 2,
                                     (c % 2) * 256:(c % 2) * 256 + 256]
                            for n, (a, k) in enumerate(((0, 0), (0, 1), (1, 0))):
                                last = pe.matmul(o, qT[a][:, c, tok], kB[:, t % 2, k * KC + c, :, own], start=(n == 0), stop=(n == 2))
                    last.then_inc(s["s_ps"], 1)

                def turn_probs(t):
                    pe.wait_ge(s["p_exp"], count(g, TILES, t + 1))
                    if t == 0:
                        pe.wait_ge(s["q_lo"], count(g, KC, KC))
                    else:
                        pe.wait_ge(s["att_ready"], count(g, TILES, t))
                    for a in range(PAIRS):
                        o = psum[:, a // 3, (a % 3) * P:(a % 3) * P + P]
                        last = pe.transpose(o, space_p[:, ((t % 2) * PAIRS + a) * P:((t % 2) * PAIRS + a + 1) * P], ident)
                    last.then_inc(s["pt_ps"], 1)

                def weigh(t):
                    pe.wait_ge(s["pt_lo"], count(g, TILES, t + 1))
                    pe.wait_ge(s[f"vB_in{t % 2}"], count(g, 128, 64 * (t // 2 + 1)))
                    for b in range(2):
                        for a in range(PAIRS):
                            o = psum[b * NODES:(b + 1) * NODES, t % 2, a * 2 * VW:(a + 1) * 2 * VW]
                            col = slice(a * P + b * NODES, a * P + (b + 1) * NODES)
                            for n, (i, j) in enumerate(((0, 0), (0, 1), (1, 0))):
                                rhs = vB[:, t % 2, j, b, :].rearrange("p (e k) -> p e k", e=2)[:, :, a * VW:(a + 1) * VW]
                                last = pe.matmul(o, pT[t % 2][i][:, col], rhs, start=(n == 0), stop=(n == 2))
                    last.then_inc(s["pv_ps"], 1)

                if attention:
                    scores(0)
                    scores(1)
                fill2(3)
                if attention:
                    turn_probs(0)
                    scores(2)
                    fill2(1)
                    weigh(0)
                    turn_probs(1)
                    scores(3)
                fill2(2)
                if attention:
                    weigh(1)
                    turn_probs(2)
                    fill2(1)
                    weigh(2)
                    turn_probs(3)
                fill2(2)
                if attention:
                    weigh(3)
                    turn(nh, s["nh_ready"], TILES, g, [0, 1, 2], s["t2_ps"])
                    for t in range(TILES):
                        if t == 3:
                            pe.wait_ge(s["v2_lo"], count(g, TILES, 1))
                        product(bank(V2_BANK[t], width=D + 1), lambda c, h: nT[h][:, c, t * P:(t + 1) * P],
                                lambda c, h: w_v2[h][:, c, :], range(KC),
                                (lambda c: pe.wait_ge(s["nT_lo"], count(g, KC, c + 1))) if t == 0 else None)\
                            .then_inc(s["v2_ps"], 1)
                    for m in range(KC):
                        product(bank(m), lambda c, h: w_k2[h][:, c, m * P:(m + 1) * P],
                                lambda c, h: nT[h][:, c, :], range(KC)).then_inc(s["k2_ps"], 1)
                    pe.wait_ge(s["diag_set"], count(g, 1, 1))
                    pe.matmul(bank(4), ones[:, :], space_g[:, 0, :], start=True, stop=True)\
                      .then_inc(s["bc_ps"], 1)
                fill2(1)
                if attention:
                    pe.wait_ge(s["z_set"], count(g, 1, 1))
                    pe.wait_ge(s["k2_lo"], count(g, KC, 1))
                    for t in range(TILES):
                        pe.matmul(psum[0:96, 0, 300:301], Y3_tiles[:, t, :], ones[:, 0:1], start=(t == 0),
                                  stop=(t == TILES - 1))
                    for c in range(KC):
                        for t in range(TILES):
                            last = pe.matmul(bank(0)[:, c * ZW:(c + 1) * ZW], nh[:, t, c * P:(c + 1) * P],
                                             Z_tiles[:, t, :], start=(t == 0), stop=(t == TILES - 1))
                    last.then_inc(s["gp_ps"], 1)
                    for t in range(TILES):
                        last = pe.transpose(bank(5, SELN)[:, t * P:(t + 1) * P], Z_tiles[:, t, 0:SELN], ident)
                    last.then_inc(s["selT_ps"], 1)
                    for t in range(TILES):
                        last = pe.transpose(bank(3, 96)[:, t * P:(t + 1) * P], Y3_tiles[:, t, :], ident)
                    last.then_inc(s["y3T_ps"], 1)
                    pe.wait_ge(s["k2_lo"], count(g, KC, KC))
                    for m in range(KC):
                        last = product(bank(1)[:, m * SELN:(m + 1) * SELN], lambda c, h: w_q2[h][:, c, m * P:(m + 1) * P],
                                       lambda c, h: gat[h][:, c, :], range(KC),
                                       (lambda c: pe.wait_ge(s["gat_lo"], count(g, 1, 1))) if m == 0 else None)
                    last.then_inc(s["q2_ps"], 1)
                    pe.wait_ge(s["pool_lo"], count(g, 1, 1))
                    product(bank(2, 96, D), lambda c, h: pool[h][:, c, :], lambda c, h: w_m[h][:, c, :], range(KC))\
                        .then_inc(s["pw_ps"], 1)
                fill2(HC)
                if not attention:
                    return
                pe.wait_ge(s["qB_lo"], count(g, 1, 1))
                for b in range(GB):
                    n = 0
                    for c in range(KC):
                        for a, k in ((0, 0), (0, 1), (1, 0)):
                            last = pe.matmul(bank(4, SROWS)[:, b * NODES:(b + 1) * NODES],
                                             qB_rows(qB[a], c, b), kT2[k][:, c, b * NODES:(b + 1) * NODES],
                                             start=(n == 0), stop=(n == 3 * KC - 1))
                            n += 1
                last.then_inc(s["s2_ps"], 1)
                pe.wait_ge(s["p2_set"], count(g, 1, 1))
                for b in range(GB):
                    o = psum[:, b // (GB // 2), (b % (GB // 2)) * SROWS:(b % (GB // 2) + 1) * SROWS]
                    last = pe.transpose(o, p2z[:, b, :], const[0:SROWS, C_ID:C_ID + SROWS])
                last.then_inc(s["pt2_ps"], 1)
                pe.wait_ge(s["p2T_lo"], count(g, 1, 1))
                pe.wait_ge(s["sT_set"], count(g, 1, 1))
                pe.wait_ge(s["R_lo_set"], count(g, 1, 1))
                for t in range(TILES):
                    for c in range(KC):
                        o = psum[:, 2 + c, 2 * t * HQ * TOPK:2 * (t + 1) * HQ * TOPK]
                        for n, (i, j) in enumerate(((0, 0), (0, 1), (1, 0))):
                            last = pe.matmul(o, v2[i][:, t, c * P:(c + 1) * P],
                                             p2T[j][:, 2 * t:2 * t + 2, c * HQ * TOPK:(c + 1) * HQ * TOPK],
                                             start=(n == 0), stop=(n == 2))
                last.then_inc(s["cx_ps"], 1)
                pe.wait_ge(s["ctx_lo"], count(g, 1, 1))
                pe.wait_ge(s["selT_set"], count(g, 1, 1))
                product(bank(5, SELN, D), lambda c, h: ctxT[h][:, c * SELN:(c + 1) * SELN], lambda c, h: w_o[h][:, c, :], range(KC))\
                    .then_inc(s["o_ps"], 1)
                for t in range(TILES):
                    if t >= 2:
                        pe.wait_ge(s["mix_read"], count(g, TILES, t - 1))
                    n = 0
                    tok = slice(t * P, (t + 1) * P)
                    for c in range(KC):
                        for a, b in ((0, 0), (0, 1), (1, 0)):
                            pe.matmul(bank(t % 2, width=D), nT[a][:, c, tok], w_m[b][:, c, :], start=(n == 0), stop=False)
                            n += 1
                    pe.matmul(bank(t % 2, width=D), sT[:, tok], R[:, :], start=False, stop=True).then_inc(s["mix_ps"], 1)
                    if t == 0:
                        pe.wait_ge(s["A_lo"], count(g, 1, 1))
                    if t >= 2:
                        pe.wait_ge(s["h_ready"], count(g, TILES, t - 1))
                    for h in range(2):
                        last = pe.matmul(bank(4 + t % 2, width=D), selT[:, tok], Ah[h][:, :], start=(h == 0), stop=(h == 1))
                    last.then_inc(s["sc_ps"], 1)
                turn(n2, s["n2_ready"], TILES, g, T3_BANK, s["t3_ps"])

            for_groups(pe, None, None, both)


def _constants():
    import numpy as np
    c = np.zeros((P, C_WIDTH), np.float32)
    i = np.arange(P)[:, None]
    j = np.arange(P)[None, :]
    same = i // NODES == j // NODES
    c[:, C_ID:C_ID + P] = i == j
    c[:, C_LT:C_LT + P] = same & (j < i)
    c[:, C_GT:C_GT + P] = same & (j > i)
    c[:, C_HALF:C_HALF + 2] = i // NODES == np.arange(2)[None, :]
    r = np.arange(2 * TOPK)[None, :]
    c[:, C_IOTA:C_IOTA + 2 * TOPK] = np.where(i // NODES == r // TOPK, r % TOPK, -1)
    return c


def kernel(**inputs):
    import numpy as np
    import concourse.bacc as bacc
    from concourse.bass_utils import run_bass_kernel_spmd

    nc = bacc.Bacc("TRN2", target_bir_lowering=False, num_devices=1)
    arrays, aps = {}, {}

    def give(name, a):
        arrays[name + "_dram"] = a
        aps[name] = nc.dram_tensor(name + "_dram", a.shape, mybir.dt.from_np(a.dtype), kind="ExternalInput").ap()

    give("x", np.ascontiguousarray(inputs["x"]).reshape(TOKENS, D))
    give("adj", np.ascontiguousarray(inputs["adj"]).reshape(TOKENS, NODES))
    give("consts", _constants())
    for name, a in inputs.items():
        if name not in ("x", "adj"):
            a = np.ascontiguousarray(a)
            give(name, a.reshape(1) if a.ndim == 0 else a)
    out = nc.dram_tensor("out_dram", (TOKENS, D), F32, kind="ExternalOutput").ap()
    gnn_ffn_kernel(nc, aps["x"], aps["adj"], aps, aps["consts"], out)
    r = run_bass_kernel_spmd(nc, [arrays], core_ids=[0])
    return r.results[0]["out_dram"].reshape(BATCH, NODES, D)
```

```python
from contextlib import ExitStack

import concourse.bass as bass
from concourse import mybir

F32 = mybir.dt.float32
F16 = mybir.dt.float16
ALU = mybir.AluOpType
ACT = mybir.ActivationFunctionType
AX_X = mybir.AxisListType.X

P = 128
BATCH, NODES, D = 128, 64, 384
HEADS, HD = 12, 32
HIDDEN = 1536
KC = D // P
HC = HIDDEN // P
TOKENS = BATCH * NODES
TILES = 4
GROUP = TILES * P
GROUPS = TOKENS // GROUP
GB = GROUP // NODES
HQ = P // HD
PAIRS = HEADS // 2
VW = HD + 1
VROW = PAIRS * VW
TOPK = 10
SELN = GB * TOPK
SROWS = HEADS * TOPK
ZW = SELN + GB
EPS = 1e-5
MASKED = -9.0e15
QSCALE = float(HD) ** -0.5

C_ID, C_LT, C_GT, C_HALF, C_IOTA = 0, 128, 256, 384, 386
C_WIDTH = C_IOTA + 2 * TOPK



def gnn_ffn_kernel(nc, x, adj, w, consts, out, groups=GROUPS):
    ctx = ExitStack()
    with ctx:
        def sb(name, shape, dt=F32):
            return ctx.enter_context(nc.sbuf_tensor(name, shape, dt))

        def sem(name):
            return ctx.enter_context(nc.semaphore(name))

        w_qk = [sb(f"w_qk_{h}", [P, KC, 2 * D], F16) for h in ("hi", "lo")]
        w_v = [sb(f"w_v_{h}", [P, KC, D], F16) for h in ("hi", "lo")]
        w_q2 = [sb(f"w_q2_{h}", [P, KC, D], F16) for h in ("hi", "lo")]
        w_k2 = [sb(f"w_k2_{h}", [P, KC, D], F16) for h in ("hi", "lo")]
        w_v2 = [sb(f"w_v2_{h}", [P, KC, D + 1], F16) for h in ("hi", "lo")]
        w_o = [sb(f"w_o_{h}", [P, KC, D], F16) for h in ("hi", "lo")]
        w_m = [sb(f"w_m_{h}", [P, KC, D], F16) for h in ("hi", "lo")]
        w_1 = [sb(f"w_1_{h}", [P, KC, HIDDEN], F16) for h in ("hi", "lo")]
        w_2 = [sb(f"w_2_{h}", [P, HC, D], F16) for h in ("hi", "lo")]

        const = sb("const", [P, C_WIDTH])
        ident = const[:, C_ID:C_ID + P]
        before = const[:, C_LT:C_LT + P]
        after = const[:, C_GT:C_GT + P]
        half = const[:, C_HALF:C_HALF + 2]
        iota = const[:, C_IOTA:C_IOTA + 2 * TOPK]
        ones = sb("ones", [P, P])
        minus_half = sb("minus_half", [P, 2])
        pause = sb("pause", [P, 1])
        spent = sb("spent", [P, 3])
        beta_bc = sb("beta_bc", [P, 1])
        VECTORS = ["L0_ffn_g1", "L0_ffn_b1", "L0_ffn_g2", "L0_ffn_b2", "L0_ffn_Wr", "L0_gnn_bq", "L0_gnn_bk",
                   "L0_ffn_bq", "L0_ffn_bk", "L0_ffn_bv", "L0_ffn_bf1"]
        NVEC = KC * (len(VECTORS) - 1) + HC
        vec_rows = sb("vec_rows", [NVEC, P])
        vecs = sb("vecs", [P, NVEC])
        g1, b1, g2, b2, wr, bq, bk, bq2, bk2, bv2 = (vecs[:, KC * n:KC * n + KC] for n in range(len(VECTORS) - 1))
        bf1 = vecs[:, KC * (len(VECTORS) - 1):NVEC]
        g1q = sb("g1q", [P, KC])
        wrg = sb("wrg", [P, KC])
        br_bc = sb("br_bc", [P, 1])
        bv_bc = sb("bv_bc", [P, D])
        bf2_bc = sb("bf2_bc", [P, D])
        bo_bc = sb("bo_bc", [SELN, D])
        b1wm_bc = sb("b1wm_bc", [96, D])
        neg_z0 = sb("neg_z0", [P, 1])

        space_n = sb("space_n", [P, TILES * D])
        space_t = [sb(f"space_t_{h}", [P, KC, GROUP], F16) for h in ("hi", "lo")]
        space_q = [sb(f"space_q_{h}", [P, KC, GROUP], F16) for h in ("hi", "lo")]
        space_k = sb("space_k", [P, TILES * D])
        space_v = sb("space_v", [P, 2, TILES * 2 * VROW], F16)
        space_p = sb("space_p", [P, 2 * HEADS * NODES])
        space_u = sb("space_u", [P, 4 * HEADS * NODES], F16)
        space_g = sb("space_g", [P, 2, GROUP])
        space_w = sb("space_w", [96, D])

        xin = sb("xin", [P, TILES, D])
        adj_in = sb("adj_in", [P, TILES, NODES])
        mask = sb("mask", [P, TILES, NODES])
        y = space_n[:, :].rearrange("p (t d) -> p t d", d=D)
        bn = sb("bn", [P, TILES, 6])

        def norm_buffers(k, n):
            return (sb(f"mv_{k}", [P, TILES, 2]), sb(f"ve_{k}", [P, TILES, n]), sb(f"neg_mean_{k}", [P, TILES]),
                    sb(f"rstd_{k}", [P, TILES, n]), sb(f"nmr_{k}", [P, TILES, n]))

        norm1 = norm_buffers(1, 1)
        norm2 = norm_buffers(2, 2)
        norm3 = norm_buffers(3, 1)
        yT = space_t
        qT = space_q
        k_stage = space_k[:, :].bitcast(F16).rearrange("p (h c n) -> p h c n", h=2, c=KC)
        kB = sb("kB", [P, 2, 2 * KC, HQ, P], F16)
        v_stage = space_v[:, :, :].rearrange("p h (t w) -> p h t w", t=TILES)
        vB = sb("vB", [P, 2, 2, 2, 2 * VROW], F16)
        probs = [space_p[:, i * HEADS * NODES:(i + 1) * HEADS * NODES].rearrange("p (h n) -> p h n", n=NODES)
                 for i in range(2)]
        smax = sb("smax", [P, HEADS])
        pT = [[space_u[:, (2 * i + h) * PAIRS * P:(2 * i + h + 1) * PAIRS * P] for h in range(2)] for i in range(2)]
        rden = sb("rden", [P, HEADS])
        att = [space_g[:, i, 0:D] for i in range(2)]
        x1 = sb("x1", [P, TILES, D])

        hid = space_k[:, :].rearrange("p (t d) -> p t d", d=D)
        nh = y
        nT = space_t
        kT2 = space_q
        v2 = [space_v[:, h, 0:TILES * D].rearrange("p (t d) -> p t d", d=D) for h in range(2)]
        ez = sb("ez", [P, TILES])
        ez1 = sb("ez1", [P, TILES])
        score = sb("score", [P, TILES])
        diag = space_g[:, 0, :].rearrange("p (t n) -> p t n", n=P)
        scratch = sb("scratch", [P, 2 * TILES, P], F16)
        cnt_b = sb("cnt_b", [P, TILES])
        cnt_a = sb("cnt_a", [P, TILES])
        rank = sb("rank", [P, TILES])
        unchosen = sb("unchosen", [P, TILES])
        Z = sb("Z", [P, TILES * ZW + 112])
        Y3 = sb("Y3", [P, TILES * 96 + 80])
        selT = sb("selT", [SELN, GROUP], F16)
        sT = sb("sT", [96, GROUP], F16)
        gat = [sb(f"gat_{h}", [P, KC, SELN], F16) for h in ("hi", "lo")]
        pool = [sb(f"pool_{h}", [P, KC, 96], F16) for h in ("hi", "lo")]
        ssum = sb("ssum", [96, 1])
        ssum_e = sb("ssum_e", [96, 1])
        rsum = sb("rsum", [96, 1])
        pw = space_w
        R = sb("R", [96, D], F16)
        q2 = sb("q2", [P, KC, SELN])
        QCHUNK = GB * SROWS + HQ * TOPK
        qB = [space_p[:, :].bitcast(F16), space_u[:, :]]
        smax2 = sb("smax2", [SROWS, GB])
        den2 = sb("den2", [SROWS, GB])
        rden2 = sb("rden2", [SROWS, GB])
        p2 = space_n[0:SROWS, 0:GB * NODES].rearrange("p (b n) -> p b n", n=NODES)
        p2z = space_g[0:SROWS, :, :].rearrange("p a (b k) -> p (a b) k", k=P)
        p2T = [space_n[:, GB * NODES + h * GB * SROWS // 2:GB * NODES + (h + 1) * GB * SROWS // 2].bitcast(F16)
               .rearrange("p (b r) -> p b r", r=SROWS) for h in range(2)]
        ctxT = [sb(f"ctxT_{h}", [P, KC * SELN], F16) for h in ("hi", "lo")]
        A = space_w[0:SELN, :]
        Ah = [sb(f"A_{h}", [SELN, D], F16) for h in ("hi", "lo")]
        n2 = y
        n2T = space_q
        resid = sb("resid", [P, TILES, D])
        gel = [space_g[:, i, :] for i in range(2)]
        hT = [sb(f"hT_{h}", [P, HC, GROUP], F16) for h in ("hi", "lo")]
        bm_bc = space_w
        setup_space = space_g[:, :, :].rearrange("p a b -> p (a b)")
        wr_bc = setup_space[:, 0:KC * P].rearrange("p (c k) -> p c k", c=KC)
        b1_bc = setup_space[:, KC * P:KC * (P + 96)].rearrange("p (c k) -> p c k", c=KC)
        bv2_bc = setup_space[:, KC * (P + 96):KC * (P + 96 + SELN)].rearrange("p (c k) -> p c k", c=KC)

        psum = ctx.enter_context(nc.psum_tensor("psum", [P, 8, 512], F32))

        def bank(i, rows=P, width=512):
            return psum[0:rows, i, 0:width]

        def banks(i, n, rows=P):
            return psum[0:rows, i:i + n, :]

        def along(buf, start, width, step, n=TILES):
            return buf[:, start:start + n * step].rearrange("p (t k) -> p t k", k=step)[:, :, 0:width]

        Z_tiles = along(Z, 0, ZW, ZW)
        Z_sel = along(Z, 0, 2 * TOPK, ZW + 2 * TOPK)
        Z_score = along(Z, SELN, 2, ZW + 2)
        Y3_tiles = along(Y3, 0, 96, 96)
        Y3_score = [along(Y3, o, 2, 98) for o in (0, 32, 64)]

        def qB_head(buf, i):
            q = buf[HD * i:HD * i + HD, TOPK * i:TOPK * i + KC * QCHUNK].rearrange("p (c k) -> p c k", k=QCHUNK)
            return q[:, :, 0:GB * SROWS].rearrange("p c (b k) -> p c b k", k=SROWS)[:, :, :, 0:TOPK]

        def qB_rows(buf, c, b):
            o = (c * GB + b) * SROWS
            return buf[:, o:o + SROWS]

        def cx_head(i):
            return psum[HD * i:HD * i + HD, CX_BANK:CX_BANK + KC, 0:GB * HQ * TOPK].rearrange(
                "p c (b k) -> p c b k", k=HQ * TOPK)[:, :, :, TOPK * i:TOPK * i + TOPK]

        def ctx_head(buf, i):
            return buf[HD * i:HD * i + HD, :].rearrange("p (c b q) -> p c b q", c=KC, q=TOPK)

        stage = [hT[0][:, :, :].rearrange("p a b -> p (a b)").bitcast(F32),
                 hT[1][:, :, :].rearrange("p a b -> p (a b)").bitcast(F32),
                 kB[:, :, :, :, :].rearrange("p t c i n -> p (t c i n)").bitcast(F32)]
        T1_BANK, V_BANK, K_BANK, Q_BANK = [1, 2, 4, 5], [4, 5, 0, 3], [0, 3, 4], [5, 1, 2]
        PV_BANK, T2_BANK, V2_BANK, K2_BANK = [0, 2, 3, 2], [4, 5, 0, 1], [3, 2, 4, 5], [0, 1, 3]
        BC_BANK, GP_BANK, SELT_BANK, Y3T_BANK, Q2_BANK, PW_BANK, S2_BANK = 2, 4, 5, 0, 1, 3, 2
        PT2_BANK, CX_BANK, O_BANK, MIX_BANK, SC_BANK, T3_BANK = 4, 0, 3, [3, 4, 5, 0], [0, 3, 1, 2], [4, 5, 1, 2]
        BIAS = {3: 1, 4: 1, 5: 1, 6: 1, 7: 1, 8: 1, 9: 1}
        BIAS_AFTER = [sum(BIAS.get(m, 0) for m in range(n + 1)) for n in range(12)]
        NCONST = 16 * 18
        PARTS = 6
        PART = HC // PARTS
        POOL_SETUP = 8
        DVE_SETUP = 9

        names = """const_in vec_ps setup_dve setup_pool setup_act w_in0 w_in1 w_in2
            w_split bias_ps bias_set rows_in bm_rows
            x_in adj_in_ stats1 norm1 y_ready t1_ps yT_hi yT_lo k_ps k_hi k_lo kB_in0 kB_in1 v_ps v_hi v_lo vB_in0 vB_in1
            q_ps q_hi q_lo mask0_set ones_set xbv_set qB_clear p2z_clear adj_used s_ps s_read p_shift p_exp pt_ps pt_hi pt_lo pv_ps att_ready
            x1_ready stats2 norm2 hid_ready nh_ready t2_ps nT_hi nT_lo v2_ps v2_hi v2_lo
            k2_ps k2_hi k2_lo diag_set bc_ps z_set selT_ps y3T_ps gp_ps selT_set sT_hi sT_set
            gat_hi gat_lo pool_hi pool_lo q2_ps q2_set qB_hi qB_lo pw_ps pw_set R_lo_set R_hi s2_ps
            p2_shift p2_exp p2_set pt2_ps p2T_hi p2T_lo cx_ps ctx_hi ctx_lo o_ps A_set A_hi A_lo
            mix_ps sc_ps mix_read h_ready stats3 norm3 n2_ready t3_ps n2T_hi n2T_lo resid_set
            f1_ps f1_hi f1_lo f2_ps o_ready out_done dve_step pool_step x1b_set""".split()
        s = {n: sem(n) for n in names}

        block = ctx.enter_context(nc.Block())

        def count(g, per, j):
            return g * per + j

        class Steps:

            def __init__(self, eng, sem_):
                self.eng, self.sem, self.per, self.first, self.n, self.g = eng, sem_, None, 0, 0, 0

            def done(self, ins):
                self.n += 1
                return ins.then_inc(self.sem, 1)

            def settle(self):
                if isinstance(self.g, int) and self.g == 0:
                    self.eng.wait_ge(self.sem, self.first + self.n)
                else:
                    self.eng.wait_ge(self.sem, self.g * self.per + (self.first + self.n))

            def begin(self, g):
                if isinstance(g, int) and g == 0:
                    self.first = self.n
                self.g, self.n = g, 0

            def end(self):
                if self.per is None:
                    self.per = self.n

        def for_groups(eng, first_steps, both):
            first_steps()
            both(0, False, True)
            if groups > 2:
                with eng.Fori(1, groups - 1) as g:
                    both(g, True, True)
            both(groups - 1, True, False)

        LOADS = [("L0_gnn_Wq", KC, D), ("L0_gnn_Wk", KC, D), ("L0_gnn_Wv", KC, D), ("L0_ffn_Wv", KC, D),
                 ("L0_ffn_Wk", KC, D), ("L0_ffn_Wq", KC, D), ("L0_ffn_Wo", KC, D), ("L0_ffn_Wm", KC, D),
                 ("L0_ffn_W1", KC, HIDDEN // 2), ("L0_ffn_W1", KC, HIDDEN // 2),
                 ("L0_ffn_W2", HC // 2, D), ("L0_ffn_W2", HC // 2, D)]
        NST = len(stage)

        def staged(n):
            _, chunks, cols = LOADS[n]
            return stage[n % NST][:, 0:chunks * cols].rearrange("p (c n) -> p c n", c=chunks)

        SPLIT_STEPS = []
        for n_, (_, chunks_, _) in enumerate(LOADS):
            SPLIT_STEPS += [(n_, c_) for c_ in range(chunks_)]
        SPLIT_END = [sum(1 for m_, _ in SPLIT_STEPS if m_ <= n_) for n_ in range(len(LOADS))]

        def target(n, c, half_):
            name, src = LOADS[n][0], staged(n)[:, c, :]
            first_half = n % 2 == 0
            if name == "L0_gnn_Wq":
                return w_qk[half_][:, c, 0:D], src
            if name == "L0_gnn_Wk":
                return w_qk[half_][:, c, D:2 * D], src
            if name == "L0_gnn_Wv":
                return (w_v[half_][:, c, :].rearrange("p (e a d) -> p e a d", e=2, a=PAIRS),
                        src.rearrange("p (a e d) -> p e a d", e=2, a=PAIRS))
            if name == "L0_ffn_Wv":
                return w_v2[half_][:, c, 0:D], src
            if name == "L0_ffn_W1":
                o = 0 if first_half else HIDDEN // 2
                return w_1[half_][:, c, o:o + HIDDEN // 2], src
            if name == "L0_ffn_W2":
                return w_2[half_][:, c + (0 if first_half else HC // 2), :], src
            return {"L0_ffn_Wk": w_k2, "L0_ffn_Wq": w_q2, "L0_ffn_Wo": w_o, "L0_ffn_Wm": w_m}[name][half_][:, c, :], src

        def gain(n, c):
            name = LOADS[n][0]
            if name in ("L0_ffn_Wq", "L0_ffn_Wk", "L0_ffn_Wv", "L0_ffn_Wm"):
                return g1[:, c:c + 1]
            if name == "L0_ffn_W1":
                return g2[:, c:c + 1]
            return None

        x_v = x.rearrange("(g t p) d -> g p t d", p=P, t=TILES)
        adj_v = adj.rearrange("(g t p) d -> g p t d", p=P, t=TILES)
        out_v = out.rearrange("(g t p) d -> g p t d", p=P, t=TILES)

        def of_group(v, g):
            if isinstance(g, int):
                return v[g]
            return v[bass.ds(g, 1)].rearrange("o p t d -> (o p) t d")

        @block.sync
        def _(sp):
            def load_x(g):
                sp.dma_start(xin[:, :, :], of_group(x_v, g)).then_inc(s["x_in"], 16)
                sp.dma_start(adj_in[:, :, :], of_group(adj_v, g)).then_inc(s["adj_in_"], 16)

            def wide(dst, name, rows):
                sp.dma_start(dst, w[name].rearrange("(a n) -> a n", a=1).to_broadcast([rows, D]))\
                  .then_inc(s["const_in"], 16)

            sp.dma_start(const[:, :], consts).then_inc(s["const_in"], 16)
            for n, name in enumerate(VECTORS):
                rows = w[name].rearrange("(c p) -> c p", p=P)
                sp.dma_start(vec_rows[KC * n:KC * n + rows.shape[0], :], rows).then_inc(s["const_in"], 16)
            for dst, name, rows in ((bv_bc, "L0_gnn_bv", P), (bf2_bc, "L0_ffn_bf2", P),
                                    (bo_bc, "L0_ffn_bo", SELN), (bm_bc, "L0_ffn_bm", 96)):
                wide(dst[:, :], name, rows)
            for dst, name in ((beta_bc, "L0_gnn_beta"), (br_bc, "L0_ffn_br")):
                sp.dma_start(dst[:, :], w[name].rearrange("(a n) -> a n", a=1).to_broadcast([P, 1]))\
                  .then_inc(s["const_in"], 16)
            for n, (name, chunks, cols) in enumerate(LOADS):
                if n >= NST:
                    sp.wait_ge(s["w_split"], SPLIT_END[n - NST])
                    sp.wait_ge(s["bias_ps"], BIAS_AFTER[n - NST])
                src = w[name]
                if name == "L0_ffn_W1":
                    o = 0 if n % 2 == 0 else HIDDEN // 2
                    src = src[:, o:o + HIDDEN // 2]
                if name == "L0_ffn_W2":
                    o = 0 if n % 2 == 0 else HIDDEN // 2
                    src = src[o:o + HIDDEN // 2, :]
                sp.dma_start(staged(n), src.rearrange("(c p) n -> p c n", p=P)).then_inc(s[f"w_in{n % NST}"], 16)
                if n == 3:
                    load_x(0)
            sp.wait_ge(s["setup_pool"], POOL_SETUP)
            sp.wait_ge(s["bm_rows"], 2)
            sp.dma_start(R[73:74, :], Ah[0][0:1, :]).then_inc(s["rows_in"], 16)
            sp.dma_start(R[74:75, :], Ah[1][0:1, :]).then_inc(s["rows_in"], 16)

            def spread_k(t):
                for i in range(HQ):
                    q = slice(HD * i, HD * i + HD)
                    sp.dma_start(kB[q, t % 2, :, i, :],
                                 k_stage[q, :, :, t * P:(t + 1) * P].rearrange("p h c n -> p (h c) n"))\
                      .then_inc(s[f"kB_in{t % 2}"], 16)

            def spread_v(t):
                for b in range(2):
                    for e in range(2):
                        sp.dma_start(vB[64 * e:64 * e + 64, t % 2, :, b, e * VROW:(e + 1) * VROW],
                                     v_stage[64 * b:64 * b + 64, :, t, e * VROW:(e + 1) * VROW])\
                          .then_inc(s[f"vB_in{t % 2}"], 16)

            def start_v(g):
                sp.wait_ge(s["v_lo"], count(g, TILES, TILES))
                sp.wait_ge(s["ones_set"], count(g, 2, 2))
                spread_v(0)
                spread_v(1)

            def both(g, feed, more):
                sp.wait_ge(s["k_lo"], count(g, KC, KC))
                spread_k(0)
                spread_k(1)
                for t in range(2, TILES):
                    sp.wait_ge(s["s_ps"], count(g, TILES, t - 1))
                    spread_k(t)
                for t in range(2, TILES):
                    sp.wait_ge(s["pv_ps"], count(g, TILES, t - 1))
                    spread_v(t)
                if more:
                    sp.wait_ge(s["x1_ready"], count(g, TILES, TILES))
                    load_x(g + 1)
                if feed:
                    send(g - 1)
                if more:
                    start_v(g + 1)

            def send(f):
                sp.wait_ge(s["o_ready"], count(f, TILES, TILES))
                sp.dma_start(of_group(out_v, f), resid[:, :, :]).then_inc(s["out_done"], 16)

            for_groups(sp, lambda: start_v(0), both)
            send(groups - 1)
            sp.wait_ge(s["out_done"], 16 * groups)

        @block.gpsimd
        def _(pl):
            steps = Steps(pl, s["pool_step"])
            pl.memset(vB[:, :, :, :, :], 0.0).then_inc(s["setup_pool"], 1)
            for h in range(2):
                pl.memset(pool[h][:, :, :], 0.0).then_inc(s["setup_pool"], 1)
            pl.memset(R[:, :], 0.0).then_inc(s["setup_pool"], 1)
            pl.memset(Z[:, :], 0.0).then_inc(s["setup_pool"], 1)
            pl.memset(minus_half[:, :], -0.5).then_inc(s["setup_pool"], 1)
            pl.memset(Y3[:, :], 0.0).then_inc(s["setup_pool"], 1)
            pl.wait_ge(s["setup_pool"], POOL_SETUP - 1)
            pl.memset(Y3_tiles[:, :, 73:75], 1.0)
            pl.wait_ge(s["w_split"], SPLIT_END[-1])
            pl.wait_ge(s["bias_ps"], BIAS_AFTER[-1])
            pl.memset(kB[:, :, :, :, :], 0.0).then_inc(s["setup_pool"], 1)

            def norm(buffers, t, g, ready, signal):
                _, ve, neg_mean, rstd, nmr = buffers
                n = ve.shape[2]
                pl.wait_ge(ready, count(g, TILES, t + 1))
                steps.done(pl.tensor_tensor(rstd[:, t, :], ve[:, t, :], minus_half[:, 0:n], ALU.pow))
                steps.settle()
                pl.tensor_tensor(nmr[:, t, :], rstd[:, t, :], neg_mean[:, t:t + 1].to_broadcast([P, n]), ALU.mult)\
                  .then_inc(signal, 1)

            def feed_lo(f, m):
                pl.wait_ge(s["f1_hi"], count(f, HC, m + 1))
                pl.tensor_tensor(hT[1][:, m, :], gel[m % 2][:, :], hT[0][:, m, :], ALU.subtract)\
                  .then_inc(s["f1_lo"], 1)

            def rest(i):
                steps.done(pl.tensor_tensor(spent[:, i:i + 1], minus_half[:, 0:1], minus_half[:, 0:1], ALU.add))

            def prepare(g):
                for t in range(TILES):
                    norm(norm1, t, g, s["stats1"], s["norm1"])
                pl.wait_ge(s["adj_in_"], count(g, 16, 16))
                rest(0)
                pl.tensor_scalar(mask[:, :, :], adj_in[:, :, :], 0.0, MASKED, ALU.is_le, ALU.mult)\
                  .then_inc(s["mask0_set"], 1)

            def add_bv(g):
                for t in range(TILES):
                    pl.wait_ge(s["y_ready"], count(g, TILES, t + 1))
                    pl.tensor_tensor(xin[:, t, :], xin[:, t, :], bv_bc[:, :], ALU.add).then_inc(s["xbv_set"], 1)

            def sum_columns(g):
                sums = [v_stage[:, h, :, :].rearrange("p t (a w) -> p (t a) w", w=VW)[:, :, HD:VW] for h in range(2)]
                pl.memset(sums[0], 1.0).then_inc(s["ones_set"], 1)
                pl.memset(sums[1], 0.0).then_inc(s["ones_set"], 1)

            def first_steps():
                pl.wait_ge(s["const_in"], NCONST)
                prepare(0)
                sum_columns(0)
                add_bv(0)

            def both(g, feed, more):
                steps.begin(g)
                if feed:
                    for m in range(HC):
                        feed_lo(g - 1, m)
                for t in range(TILES):
                    pl.wait_ge(s["xbv_set"], count(g, TILES, t + 1))
                    pl.wait_ge(s["att_ready"], count(g, TILES, t + 1))
                    pl.tensor_tensor(x1[:, t, :], att[t % 2], xin[:, t, :], ALU.add).then_inc(s["x1_ready"], 1)
                    if 1 <= t < TILES - 1:
                        norm(norm2, t - 1, g, s["stats2"], s["norm2"])
                    if t == TILES - 2:
                        norm(norm2, t, g, s["stats2"], s["norm2"])
                norm(norm2, TILES - 1, g, s["stats2"], s["norm2"])
                for h in range(2):
                    pl.memset(qB[h].bitcast(F32), 0.0).then_inc(s["qB_clear"], 1)
                for t in range(TILES):
                    pl.wait_ge(s["hid_ready"], count(g, TILES, t + 1))
                    pl.tensor_tensor(x1[:, t, :], x1[:, t, :], bf2_bc[:, :], ALU.add).then_inc(s["x1b_set"], 1)
                pl.wait_ge(s["bc_ps"], count(g, 1, 1))
                rest(1)
                pl.memset(space_g[0:SROWS, :, :], 0.0).then_inc(s["p2z_clear"], 1)
                if more:
                    prepare(g + 1)
                    pl.wait_ge(s["cx_ps"], count(g, 1, 1))
                    rest(2)
                    sum_columns(g + 1)
                    add_bv(g + 1)
                pl.wait_ge(s["x1b_set"], count(g, TILES, TILES))
                if feed:
                    pl.wait_ge(s["out_done"], count(g, 16, 0))
                for t in range(TILES + 1):
                    if t < TILES:
                        norm(norm3, t, g, s["stats3"], s["norm3"])
                    if t >= 1:
                        pl.tensor_tensor(resid[:, t - 1, :], hid[:, t - 1, :], x1[:, t - 1, :], ALU.add)\
                          .then_inc(s["resid_set"], 1)
                steps.end()

            for_groups(pl, first_steps, both)
            for m in range(HC):
                feed_lo(groups - 1, m)

        @block.scalar
        def _(act):
            act.wait_ge(s["const_in"], NCONST)

            act.wait_ge(s["setup_dve"], 2)
            for i, (n, c) in enumerate(SPLIT_STEPS):
                if c == 0:
                    act.wait_ge(s[f"w_in{n % NST}"], 16 * (n // NST + 1))
                dst, src = target(n, c, 0)
                scale = gain(n, c)
                if LOADS[n][0] in ("L0_gnn_Wq",):
                    act.activation(dst, src, ACT.Copy, scale=QSCALE).then_inc(s["setup_act"], 1)
                elif LOADS[n][0] == "L0_ffn_Wq":
                    act.wait_ge(s["setup_dve"], 4)
                    act.activation(dst, src, ACT.Copy, scale=g1q[:, c:c + 1]).then_inc(s["setup_act"], 1)
                elif scale is None:
                    act.activation(dst, src, ACT.Copy).then_inc(s["setup_act"], 1)
                else:
                    act.activation(dst, src, ACT.Copy, scale=scale).then_inc(s["setup_act"], 1)
            act.wait_ge(s["setup_dve"], 5)
            act.activation(w_v2[0][:, :, D:D + 1], wrg[:, :].unsqueeze(2), ACT.Copy).then_inc(s["setup_act"], 1)
            act.wait_ge(s["bias_set"], 10)
            act.wait_ge(s["setup_dve"], DVE_SETUP)

            def feed_hi(f, m):
                act.wait_ge(s["f1_ps"], count(f, HC, m + 1))
                if m >= 2:
                    act.wait_ge(s["f1_lo"], count(f, HC, m - 1))
                act.activation(gel[m % 2], bank(6 + m % 2), ACT.Gelu, bias=bf1[:, m:m + 1])
                act.activation(hT[0][:, m, :], bank(6 + m % 2), ACT.Gelu, bias=bf1[:, m:m + 1])\
                   .then_inc(s["f1_hi"], 1)

            def make_y(g):
                for t in range(TILES):
                    act.wait_ge(s["norm1"], count(g, TILES, t + 1))
                    act.activation(y[:, t, :], xin[:, t, :], ACT.Identity, bias=norm1[4][:, t, 0:1],
                                   scale=norm1[3][:, t, 0:1]).then_inc(s["y_ready"], 1)

            def transposed(dst, t, o, ready, g, signal):
                act.wait_ge(ready, count(g, TILES, t + 1))
                act.copy(dst[0][:, :, t * P:(t + 1) * P], bank(o, width=D).rearrange("p (c n) -> p c n", c=KC))\
                   .then_inc(signal, 1)

            def v_high(g, t):
                act.wait_ge(s["v_ps"], count(g, TILES, t + 1))
                act.copy(v_stage[:, 0, t, :].rearrange("p (a w) -> p a w", w=VW)[:, :, 0:HD],
                         bank(V_BANK[t], width=D).rearrange("p (a d) -> p a d", d=HD)).then_inc(s["v_hi"], 1)

            def first_steps():
                make_y(0)
                for t in range(TILES):
                    transposed(yT, t, T1_BANK[t], s["t1_ps"], 0, s["yT_hi"])
                for t in range(TILES):
                    v_high(0, t)

            def both(g, feed, more):
                for c in range(KC):
                    act.wait_ge(s["k_ps"], count(g, KC, c + 1))
                    if c == 0 and feed:
                        act.wait_ge(s["resid_set"], count(g, TILES, 0))
                    act.activation(k_stage[:, 0, c, :], bank(K_BANK[c]), ACT.Identity, bias=bk[:, c:c + 1])\
                       .then_inc(s["k_hi"], 1)
                if feed:
                    for m in range(HC):
                        feed_hi(g - 1, m)
                for c in range(KC):
                    act.wait_ge(s["q_ps"], count(g, KC, c + 1))
                    act.activation(qT[0][:, c, :], bank(Q_BANK[c]), ACT.Identity, bias=bq[:, c:c + 1])\
                       .then_inc(s["q_hi"], 1)

                def expo(t):
                    act.wait_ge(s["p_shift"], count(g, TILES, t + 1))
                    act.activation(probs[t % 2][:, :, :], probs[t % 2][:, :, :], ACT.Exp).then_inc(s["p_exp"], 1)

                def turned(t):
                    act.wait_ge(s["pt_ps"], count(g, TILES, t + 1))
                    act.copy(pT[t % 2][0].rearrange("p (b n) -> p b n", b=2), banks(0, 2)[:, :, 0:D])\
                       .then_inc(s["pt_hi"], 1)

                def normed(t):
                    act.wait_ge(s["norm2"], count(g, TILES, t + 1))
                    act.activation(nh[:, t, :], x1[:, t, :], ACT.Identity, bias=norm2[4][:, t, 1:2],
                                   scale=norm2[3][:, t, 1:2]).then_inc(s["nh_ready"], 1)

                def v2_high(t):
                    act.wait_ge(s["v2_ps"], count(g, TILES, t + 1))
                    act.activation(ez[:, t:t + 1], bank(V2_BANK[t])[:, D:D + 1], ACT.Exp, bias=neg_z0[:, 0:1],
                                   scale=-1.0)
                    act.copy(v2[0][:, t, :], bank(V2_BANK[t], width=D)).then_inc(s["v2_hi"], 1)

                expo(0)
                turned(0)
                expo(1)
                expo(2)
                turned(1)
                expo(3)
                turned(2)
                normed(0)
                turned(3)
                transposed(nT, 0, T2_BANK[0], s["t2_ps"], g, s["nT_hi"])
                normed(1)
                transposed(nT, 1, T2_BANK[1], s["t2_ps"], g, s["nT_hi"])
                normed(2)
                v2_high(0)
                transposed(nT, 2, T2_BANK[2], s["t2_ps"], g, s["nT_hi"])
                normed(3)
                v2_high(1)
                transposed(nT, 3, T2_BANK[3], s["t2_ps"], g, s["nT_hi"])
                v2_high(2)
                v2_high(3)
                for t in range(TILES):
                    act.activation(hid[:, t, :], x1[:, t, :], ACT.Identity, bias=norm2[4][:, t, 0:1],
                                   scale=norm2[3][:, t, 0:1]).then_inc(s["hid_ready"], 1)
                for c in range(KC):
                    act.wait_ge(s["k2_ps"], count(g, KC, c + 1))
                    act.activation(kT2[0][:, c, :], bank(K2_BANK[c]), ACT.Identity, bias=bk2[:, c:c + 1])\
                       .then_inc(s["k2_hi"], 1)
                act.wait_ge(s["gp_ps"], count(g, 1, 1))
                gp = bank(GP_BANK, width=KC * ZW).rearrange("p (c k) -> p c k", k=ZW)
                act.copy(gat[0][:, :, :], gp[:, :, 0:SELN]).then_inc(s["gat_hi"], 1)
                for o in (0, 32, 64):
                    last = act.copy(pool[0][:, :, o:o + GB], gp[:, :, SELN:ZW])
                last.then_inc(s["pool_hi"], 1)
                act.wait_ge(s["selT_ps"], count(g, 1, 1))
                act.copy(selT[:, :], bank(SELT_BANK, SELN)).then_inc(s["selT_set"], 1)
                act.wait_ge(s["y3T_ps"], count(g, 1, 1))
                act.copy(sT[:, :], bank(Y3T_BANK, 96)).then_inc(s["sT_hi"], 1)
                act.wait_ge(s["q2_set"], count(g, 1, 1))
                act.wait_ge(s["qB_clear"], count(g, 2, 2))
                for i in range(HQ):
                    act.copy(qB_head(qB[0], i), q2[HD * i:HD * i + HD, :, :].rearrange("p c (b q) -> p c b q", q=TOPK))\
                       .then_inc(s["qB_hi"], 1)
                act.wait_ge(s["pw_set"], count(g, 1, 1))
                act.copy(R[0:64, :], pw[0:64, :])
                act.copy(R[64:64 + GB, :], pw[64:64 + GB, :]).then_inc(s["R_hi"], 1)
                act.wait_ge(s["p2_shift"], count(g, 1, 1))
                act.activation(p2, p2, ACT.Exp).then_inc(s["p2_exp"], 1)
                act.wait_ge(s["pt2_ps"], count(g, 1, 1))
                half_bank = GB // 2 * SROWS
                for i in range(2):
                    act.copy(p2T[0].rearrange("p (h b) r -> p h (b r)", h=2)[:, i, :], bank(PT2_BANK + i, width=half_bank))\
                       .then_inc(s["p2T_hi"], 1)
                act.wait_ge(s["cx_ps"], count(g, 1, 1))
                for i in range(HQ):
                    act.copy(ctx_head(ctxT[0], i), cx_head(i)).then_inc(s["ctx_hi"], 1)
                if more:
                    make_y(g + 1)
                act.wait_ge(s["A_set"], count(g, 1, 1))
                act.copy(Ah[0][:, :], A).then_inc(s["A_hi"], 1)
                act.wait_ge(s["mix_ps"], count(g, TILES, TILES))
                if more:
                    for t in range(TILES):
                        transposed(yT, t, T1_BANK[t], s["t1_ps"], g + 1, s["yT_hi"])
                for t in range(TILES):
                    act.wait_ge(s["norm3"], count(g, TILES, t + 1))
                    act.activation(n2[:, t, :], hid[:, t, :], ACT.Identity, bias=norm3[4][:, t, 0:1],
                                   scale=norm3[3][:, t, 0:1]).then_inc(s["n2_ready"], 1)
                    if more:
                        v_high(g + 1, t)
                for t in range(TILES):
                    transposed(n2T, t, T3_BANK[t], s["t3_ps"], g, s["n2T_hi"])

            for_groups(act, first_steps, both)
            for m in range(HC):
                feed_hi(groups - 1, m)

        @block.vector
        def _(dve):
            steps = Steps(dve, s["dve_step"])
            dve.memset(ones[:, :], 1.0).then_inc(s["setup_dve"], 1)
            dve.wait_ge(s["const_in"], NCONST)
            dve.wait_ge(s["vec_ps"], 1)
            dve.tensor_copy(vecs[:, :], bank(7, width=NVEC)).then_inc(s["setup_dve"], 1)
            dve.wait_ge(s["setup_dve"], 2)
            dve.tensor_scalar(bq, bq, QSCALE, None, ALU.mult).then_inc(s["setup_dve"], 1)
            dve.tensor_scalar(g1q[:, :], g1, QSCALE, None, ALU.mult).then_inc(s["setup_dve"], 1)
            dve.tensor_tensor(wrg[:, :], wr, g1, ALU.mult).then_inc(s["setup_dve"], 1)
            dve.tensor_copy(wr_bc, wr.unsqueeze(2).to_broadcast([P, KC, P])).then_inc(s["setup_dve"], 1)
            dve.tensor_copy(b1_bc, b1.unsqueeze(2).to_broadcast([P, KC, 96])).then_inc(s["setup_dve"], 1)

            def bias_sums(n):
                name = LOADS[n][0]
                dve.wait_ge(s["bias_ps"], BIAS_AFTER[n])
                ps = bank(n % 8)
                if name == "L0_ffn_Wv":
                    dve.tensor_tensor(bv2, ps[:, 0:KC], bv2, ALU.add).then_inc(s["bias_set"], 1)
                    dve.wait_ge(s["bias_set"], 1)
                    dve.tensor_copy(bv2_bc, bv2.unsqueeze(2).to_broadcast([P, KC, SELN]))\
                       .then_inc(s["bias_set"], 1)
                    dve.scalar_tensor_tensor(neg_z0[:, :], ps[:, KC:KC + 1], -1.0, br_bc[:, :], ALU.mult, ALU.subtract)\
                       .then_inc(s["bias_set"], 1)
                if name == "L0_ffn_Wk":
                    dve.tensor_tensor(bk2, ps[:, 0:KC], bk2, ALU.add).then_inc(s["bias_set"], 1)
                if name == "L0_ffn_Wq":
                    dve.tensor_tensor(bq2, ps[:, 0:KC], bq2, ALU.add).then_inc(s["bias_set"], 1)
                if name == "L0_ffn_Wo":
                    dve.tensor_tensor(bo_bc[:, :], ps[0:SELN, 0:D], bo_bc[:, :], ALU.add).then_inc(s["bias_set"], 1)
                if name == "L0_ffn_Wm":
                    dve.tensor_copy(b1wm_bc[:, :], ps[0:96, 0:D]).then_inc(s["bias_set"], 1)
                    dve.tensor_tensor(bm_bc[:, :], ps[0:96, 0:D], bm_bc[:, :], ALU.add).then_inc(s["bias_set"], 1)
                    dve.wait_ge(s["bias_set"], 8)
                    dve.tensor_copy(Ah[0][0:1, :], bm_bc[0:1, :]).then_inc(s["bm_rows"], 1)
                    dve.wait_ge(s["bm_rows"], 1)
                    dve.tensor_tensor(Ah[1][0:1, :], bm_bc[0:1, :], Ah[0][0:1, :], ALU.subtract).then_inc(s["bm_rows"], 1)
                if name == "L0_ffn_W1":
                    o = 0 if n % 2 == 0 else HC // 2
                    dve.tensor_tensor(bf1[:, o:o + HC // 2], ps[:, 0:HC // 2], bf1[:, o:o + HC // 2], ALU.add)\
                       .then_inc(s["bias_set"], 1)

            for i, (n, c) in enumerate(SPLIT_STEPS):
                dve.wait_ge(s["setup_act"], i + 1)
                dst, src = target(n, c, 1)
                hi, _ = target(n, c, 0)
                scale = gain(n, c)
                if LOADS[n][0] == "L0_ffn_Wq":
                    dve.wait_ge(s["setup_dve"], 4)
                    scale = g1q[:, c:c + 1]
                if LOADS[n][0] == "L0_gnn_Wq":
                    scale = QSCALE
                if scale is None:
                    ins = dve.tensor_tensor(dst, src, hi, ALU.subtract)
                else:
                    ins = dve.scalar_tensor_tensor(dst, src, scale, hi, ALU.mult, ALU.subtract)
                ins.then_inc(s["w_split"], 1)
                if c == LOADS[n][1] - 1 and n in BIAS:
                    bias_sums(n)
            dve.wait_ge(s["setup_act"], len(SPLIT_STEPS) + 1)
            dve.tensor_tensor(w_v2[1][:, :, D:D + 1], wrg[:, :].unsqueeze(2), w_v2[0][:, :, D:D + 1], ALU.subtract)\
               .then_inc(s["setup_dve"], 1)
            dve.wait_ge(s["bias_set"], 5)
            dve.tensor_scalar(bq2, bq2, QSCALE, None, ALU.mult).then_inc(s["setup_dve"], 1)
            dve.wait_ge(s["setup_dve"], DVE_SETUP)

            def stats(t, src, buffers, signal):
                mv, ve, neg_mean, _, _ = buffers
                steps.done(dve.bn_stats(bn[:, t, :], src))
                steps.settle()
                steps.done(dve.memset(pause[:, :], 0.0))
                steps.done(dve.bn_aggr(mv[:, t, :], bn[:, t, :]))
                steps.settle()
                dve.tensor_scalar(ve[:, t, 0:1], mv[:, t, 1:2], EPS, None, ALU.add)
                if ve.shape[2] == 2:
                    dve.tensor_scalar(ve[:, t, 1:2], mv[:, t, 1:2], 1.0 + EPS, EPS * EPS, ALU.mult, ALU.add)
                dve.tensor_scalar(neg_mean[:, t:t + 1], mv[:, t, 0:1], -1.0, None, ALU.mult).then_inc(signal, 1)

            def summed(f, t):
                dve.wait_ge(s["resid_set"], count(f, TILES, t + 1))
                dve.wait_ge(s["f2_ps"], count(f, TILES, t + 1))
                dve.tensor_tensor(resid[:, t, :], bank(6 + t % 2, width=D), resid[:, t, :], ALU.add)\
                   .then_inc(s["o_ready"], 1)

            def low(dst, t, o, ready, g, signal):
                tok = slice(t * P, (t + 1) * P)
                dve.wait_ge(ready, count(g, TILES, t + 1))
                dve.tensor_tensor(dst[1][:, :, tok], bank(o, width=D).rearrange("p (c n) -> p c n", c=KC),
                                  dst[0][:, :, tok], ALU.subtract).then_inc(signal, 1)

            def y_stats(g, t):
                dve.wait_ge(s["x_in"], count(g, 16, 16))
                stats(t, xin[:, t, :], norm1, s["stats1"])

            def finish_mask(g):
                dve.wait_ge(s["mask0_set"], count(g, 1, 1))
                dve.scalar_tensor_tensor(mask[:, :, :], adj_in[:, :, :], beta_bc[:, 0:1], mask[:, :, :],
                                         ALU.mult, ALU.add).then_inc(s["adj_used"], 1)

            def v_low(g, t):
                dve.wait_ge(s["v_hi"], count(g, TILES, t + 1))
                vs = [v_stage[:, h, t, :].rearrange("p (a w) -> p a w", w=VW)[:, :, 0:HD] for h in range(2)]
                dve.tensor_tensor(vs[1], bank(V_BANK[t], width=D).rearrange("p (a d) -> p a d", d=HD), vs[0],
                                  ALU.subtract).then_inc(s["v_lo"], 1)

            def first_steps():
                for t in range(TILES):
                    y_stats(0, t)
                finish_mask(0)
                for t in range(TILES):
                    low(yT, t, T1_BANK[t], s["yT_hi"], 0, s["yT_lo"])
                for t in range(TILES):
                    v_low(0, t)

            def both(g, feed, more):
                f = g - 1
                steps.begin(g)
                dve.wait_ge(s["adj_used"], count(g, 1, 1))
                for c in range(KC):
                    dve.wait_ge(s["k_hi"], count(g, KC, c + 1))
                    dve.scalar_tensor_tensor(k_stage[:, 1, c, :], bank(K_BANK[c]), bk[:, c:c + 1],
                                             k_stage[:, 0, c, :], ALU.add, ALU.subtract).then_inc(s["k_lo"], 1)
                for c in range(KC):
                    dve.wait_ge(s["q_hi"], count(g, KC, c + 1))
                    dve.scalar_tensor_tensor(qT[1][:, c, :], bank(Q_BANK[c]), bq[:, c:c + 1],
                                             qT[0][:, c, :], ALU.add, ALU.subtract).then_inc(s["q_lo"], 1)

                def shift(t):
                    pr = probs[t % 2]
                    sp_ = psum[:, 2 + 2 * (t % 2):4 + 2 * (t % 2), :].rearrange("p b n -> p (b n)")
                    sc = sp_[:, 0:HEADS * NODES].rearrange("p (h n) -> p h n", n=NODES)
                    dve.wait_ge(s["s_ps"], count(g, TILES, t + 1))
                    if t >= 2:
                        dve.wait_ge(s["pt_ps"], count(g, TILES, t - 1))
                    dve.tensor_tensor(pr, sc, mask[:, t, :].unsqueeze(1).to_broadcast([P, HEADS, NODES]),
                                      ALU.add).then_inc(s["s_read"], 1)
                    dve.wait_ge(s["s_read"], count(g, TILES, t + 1))
                    steps.done(dve.tensor_reduce(smax[:, :], pr, AX_X, ALU.max))
                    steps.settle()
                    dve.tensor_tensor(pr, pr, smax[:, :].unsqueeze(2).to_broadcast([P, HEADS, NODES]),
                                      ALU.subtract).then_inc(s["p_shift"], 1)

                def turned(t):
                    dve.wait_ge(s["pt_hi"], count(g, TILES, t + 1))
                    dve.tensor_tensor(pT[t % 2][1].rearrange("p (b n) -> p b n", b=2), banks(0, 2)[:, :, 0:D],
                                      pT[t % 2][0].rearrange("p (b n) -> p b n", b=2), ALU.subtract)\
                       .then_inc(s["pt_lo"], 1)

                def weighted(t):
                    pv = bank(PV_BANK[t], width=HEADS * VW).rearrange("p (h w) -> p h w", w=VW)
                    dve.wait_ge(s["pv_ps"], count(g, TILES, t + 1))
                    steps.done(dve.reciprocal(rden[:, :].unsqueeze(2), pv[:, :, HD:VW]))
                    steps.settle()
                    if t >= 2:
                        dve.wait_ge(s["x1_ready"], count(g, TILES, t - 1))
                    dve.tensor_tensor(att[t % 2].rearrange("p (h d) -> p h d", d=HD), pv[:, :, 0:HD],
                                      rden[:, :].unsqueeze(2).to_broadcast([P, HEADS, HD]), ALU.mult)\
                       .then_inc(s["att_ready"], 1)

                def x1_stats(t):
                    dve.wait_ge(s["x1_ready"], count(g, TILES, t + 1))
                    stats(t, x1[:, t, :], norm2, s["stats2"])

                def v2_low(t):
                    dve.wait_ge(s["v2_hi"], count(g, TILES, t + 1))
                    dve.tensor_tensor(v2[1][:, t, :], bank(V2_BANK[t], width=D), v2[0][:, t, :], ALU.subtract)\
                       .then_inc(s["v2_lo"], 1)

                def k2_low(c):
                    dve.wait_ge(s["k2_hi"], count(g, KC, c + 1))
                    dve.scalar_tensor_tensor(kT2[1][:, c, :], bank(K2_BANK[c]), bk2[:, c:c + 1], kT2[0][:, c, :],
                                             ALU.add, ALU.subtract).then_inc(s["k2_lo"], 1)

                def sum_of(t):
                    if feed:
                        summed(f, t)

                shift(0)
                shift(1)
                turned(0)
                shift(2)
                weighted(0)
                turned(1)
                shift(3)
                sum_of(0)
                weighted(1)
                x1_stats(0)
                turned(2)
                weighted(2)
                x1_stats(1)
                turned(3)
                x1_stats(2)
                low(nT, 0, T2_BANK[0], s["nT_hi"], g, s["nT_lo"])
                weighted(3)
                low(nT, 1, T2_BANK[1], s["nT_hi"], g, s["nT_lo"])
                x1_stats(3)
                v2_low(0)
                low(nT, 2, T2_BANK[2], s["nT_hi"], g, s["nT_lo"])
                v2_low(1)
                low(nT, 3, T2_BANK[3], s["nT_hi"], g, s["nT_lo"])
                v2_low(2)
                sum_of(1)
                dve.wait_ge(s["v2_hi"], count(g, TILES, TILES))
                steps.done(dve.tensor_scalar(ez1[:, :], ez[:, :], 1.0, None, ALU.add))
                steps.settle()
                steps.done(dve.reciprocal(score[:, :], ez1[:, :]))
                steps.settle()
                for t in range(TILES):
                    last = dve.tensor_scalar(diag[:, t, :], ident, score[:, t:t + 1], None, ALU.mult)
                last.then_inc(s["diag_set"], 1)
                v2_low(3)
                if more:
                    y_stats(g + 1, 0)
                    y_stats(g + 1, 1)
                dve.wait_ge(s["bc_ps"], count(g, 1, 1))
                for t in range(TILES):
                    everyone = bank(BC_BANK)[:, t * P:(t + 1) * P]
                    dve.scalar_tensor_tensor(scratch[:, 2 * t, :], everyone, score[:, t:t + 1], before, ALU.is_le,
                                             ALU.mult, accum_out=cnt_b[:, t:t + 1])
                    last = dve.scalar_tensor_tensor(scratch[:, 2 * t + 1, :], everyone, score[:, t:t + 1], after, ALU.is_lt,
                                                    ALU.mult, accum_out=cnt_a[:, t:t + 1])
                    steps.done(last)
                steps.settle()
                steps.done(dve.tensor_tensor(rank[:, :], cnt_b[:, :], cnt_a[:, :], ALU.add))
                steps.settle()
                dve.tensor_scalar(unchosen[:, :], rank[:, :], float(TOPK), None, ALU.is_ge)
                dve.tensor_tensor(Z_sel, iota.unsqueeze(1).to_broadcast([P, TILES, 2 * TOPK]),
                                  rank[:, :].unsqueeze(2).to_broadcast([P, TILES, 2 * TOPK]), ALU.is_equal)
                halves = half.unsqueeze(1).to_broadcast([P, TILES, 2])
                scores2 = score[:, :].unsqueeze(2).to_broadcast([P, TILES, 2])
                for v in Y3_score:
                    dve.tensor_tensor(v, halves, scores2, ALU.mult)
                dve.tensor_tensor(Z_score, halves, scores2, ALU.mult).then_inc(s["z_set"], 1)
                for c in range(KC):
                    k2_low(c)
                if more:
                    y_stats(g + 1, 2)
                    y_stats(g + 1, 3)
                gp = bank(GP_BANK, width=KC * ZW).rearrange("p (c k) -> p c k", k=ZW)
                dve.wait_ge(s["gat_hi"], count(g, 1, 1))
                dve.wait_ge(s["pool_hi"], count(g, 1, 1))
                dve.tensor_tensor(gat[1][:, :, :], gp[:, :, 0:SELN], gat[0][:, :, :], ALU.subtract)\
                   .then_inc(s["gat_lo"], 1)
                for o in (0, 32, 64):
                    dve.tensor_tensor(pool[1][:, :, o:o + GB], gp[:, :, SELN:ZW], pool[0][:, :, o:o + GB],
                                      ALU.subtract)
                steps.done(dve.tensor_copy(ssum[:, :], bank(GP_BANK, 96)[:, 300:301]))
                steps.settle()
                steps.done(dve.tensor_scalar(ssum_e[:, :], ssum[:, :], 1e-6, None, ALU.add))
                steps.settle()
                dve.reciprocal(rsum[:, :], ssum_e[:, :]).then_inc(s["pool_lo"], 1)
                dve.wait_ge(s["sT_hi"], count(g, 1, 1))
                dve.tensor_tensor(sT[32:64, :], psum[32:64, Y3T_BANK, :], sT[32:64, :], ALU.subtract)\
                   .then_inc(s["sT_set"], 1)
                dve.wait_ge(s["q2_ps"], count(g, 1, 1))
                q2p = bank(Q2_BANK, width=KC * SELN).rearrange("p (c k) -> p c k", k=SELN)
                dve.tensor_tensor(q2[:, :, :], q2p, bq2.unsqueeze(2).to_broadcast([P, KC, SELN]), ALU.add)\
                   .then_inc(s["q2_set"], 1)
                for i in range(HQ):
                    dve.wait_ge(s["qB_hi"], count(g, HQ, i + 1))
                    last = dve.tensor_tensor(qB_head(qB[1], i),
                                             q2[HD * i:HD * i + HD, :, :].rearrange("p c (b q) -> p c b q", q=TOPK),
                                             qB_head(qB[0], i), ALU.subtract)
                last.then_inc(s["qB_lo"], 1)
                dve.wait_ge(s["pw_ps"], count(g, 1, 1))
                dve.wait_ge(s["pool_lo"], count(g, 1, 1))
                steps.done(dve.scalar_tensor_tensor(pw[:, :], b1wm_bc[:, :], ssum[:, 0:1], bank(PW_BANK, 96, D),
                                                    ALU.mult, ALU.add))
                steps.settle()
                dve.tensor_scalar(pw[:, :], pw[:, :], rsum[:, 0:1], None, ALU.mult)\
                   .then_inc(s["pw_set"], 1)
                dve.wait_ge(s["R_hi"], count(g, 1, 1))
                dve.tensor_tensor(R[64:64 + GB, :], pw[64:64 + GB, :], R[64:64 + GB, :], ALU.subtract)\
                   .then_inc(s["R_lo_set"], 1)
                sum_of(2)
                if more:
                    finish_mask(g + 1)
                dve.wait_ge(s["s2_ps"], count(g, 1, 1))
                s2 = bank(S2_BANK, SROWS).rearrange("p (b n) -> p b n", n=NODES)
                steps.done(dve.tensor_reduce(smax2[:, :], s2, AX_X, ALU.max))
                steps.settle()
                dve.tensor_tensor(p2, s2, smax2[:, :].unsqueeze(2).to_broadcast([SROWS, GB, NODES]),
                                  ALU.subtract).then_inc(s["p2_shift"], 1)
                dve.wait_ge(s["p2_exp"], count(g, 1, 1))
                steps.done(dve.tensor_reduce(den2[:, :], p2, AX_X, ALU.add))
                steps.settle()
                steps.done(dve.reciprocal(rden2[:, :], den2[:, :]))
                steps.settle()
                dve.wait_ge(s["p2z_clear"], count(g, 1, 1))
                for b in range(2):
                    o = NODES * b
                    last = dve.tensor_tensor(
                        p2z.rearrange("p (t b) k -> p t b k", b=2)[:, :, b, o:o + NODES],
                        p2.rearrange("p (t b) n -> p t b n", b=2)[:, :, b, :],
                        rden2[:, :].rearrange("p (t b) -> p t b", b=2)[:, :, b].unsqueeze(2)
                        .to_broadcast([SROWS, TILES, NODES]), ALU.mult)
                last.then_inc(s["p2_set"], 1)
                half_bank = GB // 2 * SROWS
                for i in range(2):
                    dve.wait_ge(s["p2T_hi"], count(g, 2, i + 1))
                    p2v = [p2T[h].rearrange("p (h b) r -> p h (b r)", h=2)[:, i, :] for h in range(2)]
                    last = dve.tensor_tensor(p2v[1], bank(PT2_BANK + i, width=half_bank), p2v[0], ALU.subtract)
                last.then_inc(s["p2T_lo"], 1)

                def mix_part(t):
                    dve.wait_ge(s["mix_ps"], count(g, TILES, t + 1))
                    dve.scalar_tensor_tensor(hid[:, t, :], bank(MIX_BANK[t], width=D), unchosen[:, t:t + 1],
                                             hid[:, t, :], ALU.mult, ALU.add).then_inc(s["mix_read"], 1)

                mix_part(0)
                for i in range(HQ):
                    dve.wait_ge(s["ctx_hi"], count(g, HQ, i + 1))
                    last = dve.tensor_tensor(ctx_head(ctxT[1], i), cx_head(i), ctx_head(ctxT[0], i), ALU.subtract)
                last.then_inc(s["ctx_lo"], 1)
                mix_part(1)
                sum_of(3)
                dve.wait_ge(s["o_ps"], count(g, 1, 1))
                dve.tensor_tensor(A, bank(O_BANK, SELN, D), bo_bc[:, :], ALU.add).then_inc(s["A_set"], 1)
                dve.wait_ge(s["A_hi"], count(g, 1, 1))
                dve.tensor_tensor(Ah[1][:, :], A, Ah[0][:, :], ALU.subtract).then_inc(s["A_lo"], 1)
                mix_part(2)
                mix_part(3)

                def whole(t):
                    dve.wait_ge(s["mix_read"], count(g, TILES, t + 1))
                    dve.wait_ge(s["sc_ps"], count(g, TILES, t + 1))
                    dve.tensor_tensor(hid[:, t, :], bank(SC_BANK[t], width=D), hid[:, t, :], ALU.add)\
                       .then_inc(s["h_ready"], 1)
                    dve.wait_ge(s["h_ready"], count(g, TILES, t + 1))
                    stats(t, hid[:, t, :], norm3, s["stats3"])

                if more:
                    for t in range(TILES):
                        low(yT, t, T1_BANK[t], s["yT_hi"], g + 1, s["yT_lo"])
                for t in range(TILES):
                    whole(t)
                    if more and t >= 2:
                        v_low(g + 1, t - 2)
                if more:
                    v_low(g + 1, 2)
                    v_low(g + 1, 3)
                for t in range(TILES):
                    low(n2T, t, T3_BANK[t], s["n2T_hi"], g, s["n2T_lo"])
                steps.end()

            for_groups(dve, first_steps, both)
            for t in range(TILES):
                summed(groups - 1, t)

        @block.tensor
        def _(pe):
            def product(o, lhs, rhs, terms, before_term=None):
                n, total_ = 0, 3 * len(terms)
                for k in terms:
                    if before_term is not None:
                        before_term(k)
                    for a, b in ((0, 0), (0, 1), (1, 0)):
                        last = pe.matmul(o, lhs(k, a), rhs(k, b), start=(n == 0), stop=(n == total_ - 1))
                        n += 1
                return last

            def turn(src, t, o, ready, g, signal):
                pe.wait_ge(ready, count(g, TILES, t + 1))
                for c in range(KC):
                    last = pe.transpose(bank(o)[:, c * P:(c + 1) * P], src[:, t, c * P:(c + 1) * P], ident)
                last.then_inc(signal, 1)

            pe.wait_ge(s["const_in"], NCONST)
            pe.transpose(bank(7, width=NVEC), vec_rows[:, :], const[0:NVEC, C_ID:C_ID + NVEC]).then_inc(s["vec_ps"], 1)
            pe.wait_ge(s["setup_dve"], 7)
            for n, (name, chunks, cols) in enumerate(LOADS):
                if n not in BIAS:
                    continue
                pe.wait_ge(s[f"w_in{n % NST}"], 16 * (n // NST + 1))
                ps = bank(n % 8)
                W = staged(n)
                if name in ("L0_ffn_Wv", "L0_ffn_Wk", "L0_ffn_Wq", "L0_ffn_W1"):
                    shift_ = b2 if name == "L0_ffn_W1" else b1
                    for m in range(cols // P):
                        for c in range(KC):
                            last = pe.matmul(ps[:, m:m + 1], W[:, c, m * P:(m + 1) * P], shift_[:, c:c + 1],
                                             start=(c == 0), stop=(c == KC - 1))
                    if name == "L0_ffn_Wv":
                        for c in range(KC):
                            last = pe.matmul(ps[:, KC:KC + 1], wr_bc[:, c, :], b1[:, c:c + 1], start=(c == 0),
                                             stop=(c == KC - 1))
                elif name == "L0_ffn_Wo":
                    pe.wait_ge(s["bias_set"], 2)
                    for c in range(KC):
                        last = pe.matmul(ps[0:SELN, 0:D], bv2_bc[:, c, :], W[:, c, :], start=(c == 0), stop=(c == KC - 1))
                else:
                    for c in range(KC):
                        last = pe.matmul(ps[0:96, 0:D], b1_bc[:, c, :], W[:, c, :], start=(c == 0), stop=(c == KC - 1))
                last.then_inc(s["bias_ps"], 1)
            pe.wait_ge(s["w_split"], SPLIT_END[-1])
            pe.wait_ge(s["setup_dve"], DVE_SETUP)
            pe.wait_ge(s["bias_set"], 10)
            pe.wait_ge(s["setup_pool"], POOL_SETUP)
            pe.wait_ge(s["rows_in"], 32)

            def feed1(f, m):
                if m == 0:
                    pe.wait_ge(s["n2T_lo"], count(f, TILES, TILES))
                if m >= 2:
                    pe.wait_ge(s["f1_hi"], count(f, HC, m - 1))
                product(bank(6 + m % 2), lambda c, h: w_1[h][:, c, m * P:(m + 1) * P],
                        lambda c, h: n2T[h][:, c, :], range(KC)).then_inc(s["f1_ps"], 1)

            def feed2(f, t, part):
                if part == 0:
                    if t == 0:
                        pe.wait_ge(s["f1_lo"], count(f, HC, HC))
                    if t < 2:
                        pe.wait_ge(s["f1_hi"], count(f, HC, HC - 1 + t))
                    else:
                        pe.wait_ge(s["o_ready"], count(f, TILES, t - 1))
                n = part * PART * 3
                for m in range(part * PART, (part + 1) * PART):
                    for a, b in ((0, 0), (0, 1), (1, 0)):
                        last = pe.matmul(bank(6 + t % 2, width=D), hT[a][:, m, t * P:(t + 1) * P], w_2[b][:, m, :],
                                         start=(n == 0), stop=(n == 3 * HC - 1))
                        n += 1
                if part == PARTS - 1:
                    last.then_inc(s["f2_ps"], 1)

            def front_turns(g):
                for t in range(TILES):
                    if t >= 2 and not (isinstance(g, int) and g == 0):
                        pe.wait_ge(s["mix_read"], count(g - 1, TILES, t))
                    turn(y, t, T1_BANK[t], s["y_ready"], g, s["t1_ps"])

            def front_values(g):
                for t in range(TILES):
                    if t >= 2 and not (isinstance(g, int) and g == 0):
                        pe.wait_ge(s["h_ready"], count(g - 1, TILES, t - 1))
                    pe.wait_ge(s["yT_lo"], count(g, TILES, TILES if t == 1 else max(3, t + 1)))
                    product(bank(V_BANK[t], width=D), lambda c, h: yT[h][:, c, t * P:(t + 1) * P],
                            lambda c, h: w_v[h][:, c, :], range(KC)).then_inc(s["v_ps"], 1)

            def first_steps():
                front_turns(0)
                front_values(0)

            def both(g, feed, more):
                f = g - 1
                feeds2 = [(t, part) for t in range(TILES) for part in range(PARTS)] if feed else []

                def fill(n):
                    for _ in range(n):
                        if feeds2:
                            feed2(f, *feeds2.pop(0))

                for m in range(KC):
                    if m < 2:
                        pe.wait_ge(s["v_lo"], count(g, TILES, 3 + m))
                    elif feed:
                        pe.wait_ge(s["n2T_lo"], count(f, TILES, 1))
                    product(bank(K_BANK[m]), lambda c, h: w_qk[h][:, c, D + m * P:D + (m + 1) * P],
                            lambda c, h: yT[h][:, c, :], range(KC)).then_inc(s["k_ps"], 1)
                if feed:
                    for m in range(HC):
                        feed1(f, m)
                for m in range(KC):
                    product(bank(Q_BANK[m]), lambda c, h: w_qk[h][:, c, m * P:(m + 1) * P],
                            lambda c, h: yT[h][:, c, :], range(KC)).then_inc(s["q_ps"], 1)

                def scores(t):
                    if t == 0:
                        pe.wait_ge(s["q_lo"], count(g, KC, KC))
                    if t >= 2:
                        pe.wait_ge(s["s_read"], count(g, TILES, t - 1))
                    pe.wait_ge(s[f"kB_in{t % 2}"], count(g, 128, 64 * (t // 2 + 1)))
                    for b in range(2):
                        own = slice(b * NODES, (b + 1) * NODES)
                        tok = slice(t * P + b * NODES, t * P + (b + 1) * NODES)
                        for c in range(KC):
                            o = psum[b * NODES:(b + 1) * NODES, 2 + 2 * (t % 2) + c // 2,
                                     (c % 2) * 256:(c % 2) * 256 + 256]
                            for n, (a, k) in enumerate(((0, 0), (0, 1), (1, 0))):
                                last = pe.matmul(o, qT[a][:, c, tok], kB[:, t % 2, k * KC + c, :, own], start=(n == 0), stop=(n == 2))
                    last.then_inc(s["s_ps"], 1)

                def turn_probs(t):
                    pe.wait_ge(s["p_exp"], count(g, TILES, t + 1))
                    if t == 1:
                        pe.wait_ge(s["att_ready"], count(g, TILES, 1))
                    for a in range(PAIRS):
                        o = psum[:, a // 3, (a % 3) * P:(a % 3) * P + P]
                        last = pe.transpose(o, space_p[:, ((t % 2) * PAIRS + a) * P:((t % 2) * PAIRS + a + 1) * P], ident)
                    last.then_inc(s["pt_ps"], 1)

                def weigh(t):
                    pe.wait_ge(s["pt_lo"], count(g, TILES, t + 1))
                    if t >= 1:
                        pe.wait_ge(s["att_ready"] if t == 3 else s["s_read"], count(g, TILES, 2 if t == 3 else 3))
                    pe.wait_ge(s[f"vB_in{t % 2}"], count(g, 128, 64 * (t // 2 + 1)))
                    for b in range(2):
                        for a in range(PAIRS):
                            o = psum[b * NODES:(b + 1) * NODES, PV_BANK[t], a * 2 * VW:(a + 1) * 2 * VW]
                            col = slice(a * P + b * NODES, a * P + (b + 1) * NODES)
                            for n, (i, j) in enumerate(((0, 0), (0, 1), (1, 0))):
                                rhs = vB[:, t % 2, j, b, :].rearrange("p (e k) -> p e k", e=2)[:, :, a * VW:(a + 1) * VW]
                                last = pe.matmul(o, pT[t % 2][i][:, col], rhs, start=(n == 0), stop=(n == 2))
                    last.then_inc(s["pv_ps"], 1)

                def turn_nh(t):
                    turn(nh, t, T2_BANK[t], s["nh_ready"], g, s["t2_ps"])

                def values2(t):
                    if t < 2:
                        pe.wait_ge(s["att_ready"], count(g, TILES, 3 + t))
                    pe.wait_ge(s["nT_lo"], count(g, TILES, t + 1))
                    product(bank(V2_BANK[t], width=D + 1), lambda c, h: nT[h][:, c, t * P:(t + 1) * P],
                            lambda c, h: w_v2[h][:, c, :], range(KC)).then_inc(s["v2_ps"], 1)

                def keys2(m):
                    if m == 2:
                        pe.wait_ge(s["v2_lo"], count(g, TILES, 1))
                    product(bank(K2_BANK[m]), lambda c, h: w_k2[h][:, c, m * P:(m + 1) * P],
                            lambda c, h: nT[h][:, c, :], range(KC)).then_inc(s["k2_ps"], 1)

                fill(2)
                scores(0)
                scores(1)
                fill(3)
                turn_probs(0)
                scores(2)
                fill(2)
                weigh(0)
                scores(3)
                turn_probs(1)
                fill(2)
                weigh(1)
                fill(1)
                turn_probs(2)
                fill(2)
                weigh(2)
                turn_probs(3)
                turn_nh(0)
                fill(2)
                weigh(3)
                turn_nh(1)
                values2(0)
                turn_nh(2)
                fill(2)
                values2(1)
                turn_nh(3)
                values2(2)
                values2(3)
                keys2(0)
                keys2(1)
                pe.wait_ge(s["diag_set"], count(g, 1, 1))
                pe.wait_ge(s["v2_lo"], count(g, TILES, 2))
                pe.matmul(bank(BC_BANK), ones[:, :], space_g[:, 0, :], start=True, stop=True).then_inc(s["bc_ps"], 1)
                keys2(2)
                fill(1)
                pe.wait_ge(s["z_set"], count(g, 1, 1))
                for t in range(TILES):
                    pe.matmul(psum[0:96, GP_BANK, 300:301], Y3_tiles[:, t, :], ones[:, 0:1], start=(t == 0),
                              stop=(t == TILES - 1))
                for c in range(KC):
                    for t in range(TILES):
                        last = pe.matmul(bank(GP_BANK)[:, c * ZW:(c + 1) * ZW], nh[:, t, c * P:(c + 1) * P],
                                         Z_tiles[:, t, :], start=(t == 0), stop=(t == TILES - 1))
                last.then_inc(s["gp_ps"], 1)
                for t in range(TILES):
                    last = pe.transpose(bank(SELT_BANK, SELN)[:, t * P:(t + 1) * P], Z_tiles[:, t, 0:SELN], ident)
                last.then_inc(s["selT_ps"], 1)
                pe.wait_ge(s["k2_lo"], count(g, KC, 1))
                for t in range(TILES):
                    last = pe.transpose(bank(Y3T_BANK, 96)[:, t * P:(t + 1) * P], Y3_tiles[:, t, :], ident)
                last.then_inc(s["y3T_ps"], 1)
                pe.wait_ge(s["gat_lo"], count(g, 1, 1))
                for m in range(KC):
                    last = product(bank(Q2_BANK)[:, m * SELN:(m + 1) * SELN],
                                   lambda c, h: w_q2[h][:, c, m * P:(m + 1) * P],
                                   lambda c, h: gat[h][:, c, :], range(KC))
                last.then_inc(s["q2_ps"], 1)
                pe.wait_ge(s["pool_lo"], count(g, 1, 1))
                product(bank(PW_BANK, 96, D), lambda c, h: pool[h][:, c, :], lambda c, h: w_m[h][:, c, :], range(KC))\
                    .then_inc(s["pw_ps"], 1)
                fill(2)
                pe.wait_ge(s["qB_lo"], count(g, 1, 1))
                for b in range(GB):
                    n = 0
                    for c in range(KC):
                        for a, k in ((0, 0), (0, 1), (1, 0)):
                            last = pe.matmul(bank(S2_BANK, SROWS)[:, b * NODES:(b + 1) * NODES],
                                             qB_rows(qB[a], c, b), kT2[k][:, c, b * NODES:(b + 1) * NODES],
                                             start=(n == 0), stop=(n == 3 * KC - 1))
                            n += 1
                last.then_inc(s["s2_ps"], 1)

                def mix(t):
                    n = 0
                    tok = slice(t * P, (t + 1) * P)
                    if t == 0:
                        pe.wait_ge(s["sT_set"], count(g, 1, 1))
                        pe.wait_ge(s["R_lo_set"], count(g, 1, 1))
                    for c in range(KC):
                        for a, b in ((0, 0), (0, 1), (1, 0)):
                            pe.matmul(bank(MIX_BANK[t], width=D), nT[a][:, c, tok], w_m[b][:, c, :], start=(n == 0),
                                      stop=False)
                            n += 1
                    pe.matmul(bank(MIX_BANK[t], width=D), sT[:, tok], R[:, :], start=False, stop=True)\
                        .then_inc(s["mix_ps"], 1)

                def scatter(t):
                    if t == 0:
                        pe.wait_ge(s["mix_read"], count(g, TILES, TILES))
                    if t >= 2 and more:
                        pe.wait_ge(s["yT_lo"], count(g + 1, TILES, t - 1))
                    for h in range(2):
                        last = pe.matmul(bank(SC_BANK[t], width=D), selT[:, t * P:(t + 1) * P], Ah[h][:, :],
                                         start=(h == 0), stop=(h == 1))
                    last.then_inc(s["sc_ps"], 1)

                mix(0)
                fill(3)
                pe.wait_ge(s["p2_set"], count(g, 1, 1))
                for b in range(GB):
                    o = psum[:, PT2_BANK + b // (GB // 2), (b % (GB // 2)) * SROWS:(b % (GB // 2) + 1) * SROWS]
                    last = pe.transpose(o, p2z[:, b, :], const[0:SROWS, C_ID:C_ID + SROWS])
                last.then_inc(s["pt2_ps"], 1)
                fill(2)
                pe.wait_ge(s["p2T_lo"], count(g, 1, 1))
                for t in range(TILES):
                    for c in range(KC):
                        o = psum[:, CX_BANK + c, 2 * t * HQ * TOPK:2 * (t + 1) * HQ * TOPK]
                        for n, (i, j) in enumerate(((0, 0), (0, 1), (1, 0))):
                            last = pe.matmul(o, v2[i][:, t, c * P:(c + 1) * P],
                                             p2T[j][:, 2 * t:2 * t + 2, c * HQ * TOPK:(c + 1) * HQ * TOPK],
                                             start=(n == 0), stop=(n == 2))
                last.then_inc(s["cx_ps"], 1)
                mix(1)
                pe.wait_ge(s["ctx_lo"], count(g, 1, 1))
                pe.wait_ge(s["mix_read"], count(g, TILES, 1))
                product(bank(O_BANK, SELN, D), lambda c, h: ctxT[h][:, c * SELN:(c + 1) * SELN],
                        lambda c, h: w_o[h][:, c, :], range(KC)).then_inc(s["o_ps"], 1)
                mix(2)
                mix(3)
                fill(HC)
                if more:
                    front_turns(g + 1)
                pe.wait_ge(s["A_lo"], count(g, 1, 1))
                for t in range(TILES):
                    scatter(t)
                if more:
                    front_values(g + 1)
                for t in range(TILES):
                    if more and t < 2:
                        pe.wait_ge(s["v_lo"], count(g + 1, TILES, t + 1))
                    turn(n2, t, T3_BANK[t], s["n2_ready"], g, s["t3_ps"])

            for_groups(pe, first_steps, both)
            for m in range(HC):
                feed1(groups - 1, m)
            for t in range(TILES):
                for part in range(PARTS):
                    feed2(groups - 1, t, part)


def _constants():
    import numpy as np
    c = np.zeros((P, C_WIDTH), np.float32)
    i = np.arange(P)[:, None]
    j = np.arange(P)[None, :]
    same = i // NODES == j // NODES
    c[:, C_ID:C_ID + P] = i == j
    c[:, C_LT:C_LT + P] = same & (j < i)
    c[:, C_GT:C_GT + P] = same & (j > i)
    c[:, C_HALF:C_HALF + 2] = i // NODES == np.arange(2)[None, :]
    r = np.arange(2 * TOPK)[None, :]
    c[:, C_IOTA:C_IOTA + 2 * TOPK] = np.where(i // NODES == r // TOPK, r % TOPK, -1)
    return c


def kernel(**inputs):
    import numpy as np
    import concourse.bacc as bacc
    from concourse.bass_utils import run_bass_kernel_spmd

    nc = bacc.Bacc("TRN2", target_bir_lowering=False, num_devices=1)
    arrays, aps = {}, {}

    def give(name, a):
        arrays[name + "_dram"] = a
        aps[name] = nc.dram_tensor(name + "_dram", a.shape, mybir.dt.from_np(a.dtype), kind="ExternalInput").ap()

    give("x", np.ascontiguousarray(inputs["x"]).reshape(TOKENS, D))
    give("adj", np.ascontiguousarray(inputs["adj"]).reshape(TOKENS, NODES))
    give("consts", _constants())
    for name, a in inputs.items():
        if name not in ("x", "adj"):
            a = np.ascontiguousarray(a)
            give(name, a.reshape(1) if a.ndim == 0 else a)
    out = nc.dram_tensor("out_dram", (TOKENS, D), F32, kind="ExternalOutput").ap()
    gnn_ffn_kernel(nc, aps["x"], aps["adj"], aps, aps["consts"], out)
    r = run_bass_kernel_spmd(nc, [arrays], core_ids=[0])
    return r.results[0]["out_dram"].reshape(BATCH, NODES, D)
```

```python
from contextlib import ExitStack

import concourse.bass as bass
from concourse import mybir

F32 = mybir.dt.float32
F16 = mybir.dt.float16
ALU = mybir.AluOpType
ACT = mybir.ActivationFunctionType
AX_X = mybir.AxisListType.X

P = 128
BATCH, NODES, D = 128, 64, 384
HEADS, HD = 12, 32
HIDDEN = 1536
KC = D // P
HC = HIDDEN // P
TOKENS = BATCH * NODES
TILES = 4
GROUP = TILES * P
GROUPS = TOKENS // GROUP
GB = GROUP // NODES
HQ = P // HD
PAIRS = HEADS // 2
VW = HD + 1
VROW = PAIRS * VW
TOPK = 10
SELN = GB * TOPK
SROWS = HEADS * TOPK
ZW = SELN + GB
EPS = 1e-5
MASKED = -9.0e15
QSCALE = float(HD) ** -0.5

C_ID, C_LT, C_GT, C_HALF, C_IOTA = 0, 128, 256, 384, 386
C_WIDTH = C_IOTA + 2 * TOPK



def gnn_ffn_kernel(nc, x, adj, w, consts, out, groups=GROUPS):
    ctx = ExitStack()
    with ctx:
        def sb(name, shape, dt=F32):
            return ctx.enter_context(nc.sbuf_tensor(name, shape, dt))

        def sem(name):
            return ctx.enter_context(nc.semaphore(name))

        w_qk = [sb(f"w_qk_{h}", [P, KC, 2 * D], F16) for h in ("hi", "lo")]
        w_v = [sb(f"w_v_{h}", [P, KC, D], F16) for h in ("hi", "lo")]
        w_q2 = [sb(f"w_q2_{h}", [P, KC, D], F16) for h in ("hi", "lo")]
        w_k2 = [sb(f"w_k2_{h}", [P, KC, D], F16) for h in ("hi", "lo")]
        w_v2 = [sb(f"w_v2_{h}", [P, KC, D + 1], F16) for h in ("hi", "lo")]
        w_o = [sb(f"w_o_{h}", [P, KC, D], F16) for h in ("hi", "lo")]
        w_m = [sb(f"w_m_{h}", [P, KC, D], F16) for h in ("hi", "lo")]
        w_1 = [sb(f"w_1_{h}", [P, KC, HIDDEN], F16) for h in ("hi", "lo")]
        w_2 = [sb(f"w_2_{h}", [P, HC, D], F16) for h in ("hi", "lo")]

        const = sb("const", [P, C_WIDTH])
        ident = const[:, C_ID:C_ID + P]
        before = const[:, C_LT:C_LT + P]
        after = const[:, C_GT:C_GT + P]
        half = const[:, C_HALF:C_HALF + 2]
        iota = const[:, C_IOTA:C_IOTA + 2 * TOPK]
        ones = sb("ones", [P, P])
        minus_half = sb("minus_half", [P, 2])
        pause = sb("pause", [P, 1])
        spent = sb("spent", [P, 3])
        beta_bc = sb("beta_bc", [P, 1])
        VECTORS = ["L0_ffn_g1", "L0_ffn_b1", "L0_ffn_g2", "L0_ffn_b2", "L0_ffn_Wr", "L0_gnn_bq", "L0_gnn_bk",
                   "L0_ffn_bq", "L0_ffn_bk", "L0_ffn_bv", "L0_ffn_bf1"]
        NVEC = KC * (len(VECTORS) - 1) + HC
        vec_rows = sb("vec_rows", [NVEC, P])
        vecs = sb("vecs", [P, NVEC])
        g1, b1, g2, b2, wr, bq, bk, bq2, bk2, bv2 = (vecs[:, KC * n:KC * n + KC] for n in range(len(VECTORS) - 1))
        bf1 = vecs[:, KC * (len(VECTORS) - 1):NVEC]
        g1q = sb("g1q", [P, KC])
        wrg = sb("wrg", [P, KC])
        br_bc = sb("br_bc", [P, 1])
        bv_bc = sb("bv_bc", [P, D])
        bf2_bc = sb("bf2_bc", [P, D])
        bo_bc = sb("bo_bc", [SELN, D])
        b1wm_bc = sb("b1wm_bc", [96, D])
        neg_z0 = sb("neg_z0", [P, 1])

        space_n = sb("space_n", [P, TILES * D])
        space_t = [sb(f"space_t_{h}", [P, KC, GROUP], F16) for h in ("hi", "lo")]
        space_q = [sb(f"space_q_{h}", [P, KC, GROUP], F16) for h in ("hi", "lo")]
        space_k = sb("space_k", [P, TILES * D])
        space_v = sb("space_v", [P, 2, TILES * 2 * VROW], F16)
        space_p = sb("space_p", [P, 2 * HEADS * NODES])
        space_u = sb("space_u", [P, 4 * HEADS * NODES], F16)
        space_g = sb("space_g", [P, 2, GROUP])
        space_w = sb("space_w", [96, D])

        xin = sb("xin", [P, TILES, D])
        adj_in = sb("adj_in", [P, TILES, NODES])
        mask = sb("mask", [P, TILES, NODES])
        y = space_n[:, :].rearrange("p (t d) -> p t d", d=D)
        bn = sb("bn", [P, TILES, 6])

        def norm_buffers(k, n):
            return (sb(f"mv_{k}", [P, TILES, 2]), sb(f"ve_{k}", [P, TILES, n]), sb(f"neg_mean_{k}", [P, TILES]),
                    sb(f"rstd_{k}", [P, TILES, n]), sb(f"nmr_{k}", [P, TILES, n]))

        norm1 = norm_buffers(1, 1)
        norm2 = norm_buffers(2, 2)
        norm3 = norm_buffers(3, 1)
        yT = space_t
        qT = space_q
        k_stage = space_k[:, :].bitcast(F16).rearrange("p (h c n) -> p h c n", h=2, c=KC)
        kB = sb("kB", [P, 2, 2 * KC, HQ, P], F16)
        v_stage = space_v[:, :, :].rearrange("p h (t w) -> p h t w", t=TILES)
        vB = sb("vB", [P, 2, 2, 2, 2 * VROW], F16)
        probs = [space_p[:, i * HEADS * NODES:(i + 1) * HEADS * NODES].rearrange("p (h n) -> p h n", n=NODES)
                 for i in range(2)]
        smax = sb("smax", [P, HEADS])
        pT = [[space_u[:, (2 * i + h) * PAIRS * P:(2 * i + h + 1) * PAIRS * P] for h in range(2)] for i in range(2)]
        rden = sb("rden", [P, HEADS])
        att = [space_g[:, i, 0:D] for i in range(2)]
        x1 = sb("x1", [P, TILES, D])

        hid = space_k[:, :].rearrange("p (t d) -> p t d", d=D)
        nh = y
        nT = space_t
        kT2 = space_q
        v2 = [space_v[:, h, 0:TILES * D].rearrange("p (t d) -> p t d", d=D) for h in range(2)]
        ez = sb("ez", [P, TILES])
        ez1 = sb("ez1", [P, TILES])
        score = sb("score", [P, TILES])
        diag = space_g[:, 0, :].rearrange("p (t n) -> p t n", n=P)
        scratch = sb("scratch", [P, 2 * TILES, P], F16)
        cnt_b = sb("cnt_b", [P, TILES])
        cnt_a = sb("cnt_a", [P, TILES])
        rank = sb("rank", [P, TILES])
        unchosen = sb("unchosen", [P, TILES])
        Z = sb("Z", [P, TILES * ZW + 112])
        Y3 = sb("Y3", [P, TILES * 96 + 80])
        selT = sb("selT", [SELN, GROUP], F16)
        sT = sb("sT", [96, GROUP], F16)
        gat = [sb(f"gat_{h}", [P, KC, SELN], F16) for h in ("hi", "lo")]
        pool = [sb(f"pool_{h}", [P, KC, 96], F16) for h in ("hi", "lo")]
        ssum = sb("ssum", [96, 1])
        ssum_e = sb("ssum_e", [96, 1])
        rsum = sb("rsum", [96, 1])
        pw = space_w
        R = sb("R", [96, D], F16)
        q2 = sb("q2", [P, KC, SELN])
        QCHUNK = GB * SROWS + HQ * TOPK
        qB = [space_p[:, :].bitcast(F16), space_u[:, :]]
        smax2 = sb("smax2", [SROWS, GB])
        den2 = sb("den2", [SROWS, GB])
        rden2 = sb("rden2", [SROWS, GB])
        p2 = space_n[0:SROWS, 0:GB * NODES].rearrange("p (b n) -> p b n", n=NODES)
        p2z = space_g[0:SROWS, :, :].rearrange("p a (b k) -> p (a b) k", k=P)
        p2T = [space_n[:, GB * NODES + h * GB * SROWS // 2:GB * NODES + (h + 1) * GB * SROWS // 2].bitcast(F16)
               .rearrange("p (b r) -> p b r", r=SROWS) for h in range(2)]
        ctxT = [sb(f"ctxT_{h}", [P, KC * SELN], F16) for h in ("hi", "lo")]
        A = space_w[0:SELN, :]
        Ah = [sb(f"A_{h}", [SELN, D], F16) for h in ("hi", "lo")]
        n2 = y
        n2T = space_q
        resid = sb("resid", [P, TILES, D])
        gel = [space_g[:, i, :] for i in range(2)]
        hT = [sb(f"hT_{h}", [P, HC, GROUP], F16) for h in ("hi", "lo")]
        bm_bc = space_w
        setup_space = space_g[:, :, :].rearrange("p a b -> p (a b)")
        wr_bc = setup_space[:, 0:KC * P].rearrange("p (c k) -> p c k", c=KC)
        b1_bc = setup_space[:, KC * P:KC * (P + 96)].rearrange("p (c k) -> p c k", c=KC)
        bv2_bc = setup_space[:, KC * (P + 96):KC * (P + 96 + SELN)].rearrange("p (c k) -> p c k", c=KC)

        psum = ctx.enter_context(nc.psum_tensor("psum", [P, 8, 512], F32))

        def bank(i, rows=P, width=512):
            return psum[0:rows, i, 0:width]

        def banks(i, n, rows=P):
            return psum[0:rows, i:i + n, :]

        def along(buf, start, width, step, n=TILES):
            return buf[:, start:start + n * step].rearrange("p (t k) -> p t k", k=step)[:, :, 0:width]

        Z_tiles = along(Z, 0, ZW, ZW)
        Z_sel = along(Z, 0, 2 * TOPK, ZW + 2 * TOPK)
        Z_score = along(Z, SELN, 2, ZW + 2)
        Y3_tiles = along(Y3, 0, 96, 96)
        Y3_score = [along(Y3, o, 2, 98) for o in (0, 32, 64)]

        def qB_head(buf, i):
            q = buf[HD * i:HD * i + HD, TOPK * i:TOPK * i + KC * QCHUNK].rearrange("p (c k) -> p c k", k=QCHUNK)
            return q[:, :, 0:GB * SROWS].rearrange("p c (b k) -> p c b k", k=SROWS)[:, :, :, 0:TOPK]

        def qB_rows(buf, c, b):
            o = (c * GB + b) * SROWS
            return buf[:, o:o + SROWS]

        def cx_head(i):
            return psum[HD * i:HD * i + HD, CX_BANK:CX_BANK + KC, 0:GB * HQ * TOPK].rearrange(
                "p c (b k) -> p c b k", k=HQ * TOPK)[:, :, :, TOPK * i:TOPK * i + TOPK]

        def ctx_head(buf, i):
            return buf[HD * i:HD * i + HD, :].rearrange("p (c b q) -> p c b q", c=KC, q=TOPK)

        half_h = HC // 2
        stage = [hT[h][:, i * half_h:(i + 1) * half_h, :].rearrange("p a b -> p (a b)").bitcast(F32)[:, 0:KC * D]
                 for h in range(2) for i in range(2)] + [resid[:, :, :].rearrange("p t d -> p (t d)")[:, 0:KC * D]]

        T1_BANK, V_BANK, K_BANK, Q_BANK = [1, 2, 4, 5], [0, 3, 4, 5], [1, 5, 0], [3, 2, 4]
        PV_BANK, T2_BANK, V2_BANK, K2_BANK = [0, 2, 3, 2], [4, 5, 0, 1], [3, 2, 4, 5], [0, 1, 3]
        BC_BANK, GP_BANK, SELT_BANK, Y3T_BANK, Q2_BANK, PW_BANK, S2_BANK = 2, 4, 5, 0, 1, 3, 2
        PT2_BANK, CX_BANK, O_BANK, MIX_BANK, SC_BANK, T3_BANK = 4, 0, 3, [3, 4, 5, 0], [0, 3, 1, 2], [0, 3, 2, 4]
        PARTS = 6
        PART = HC // PARTS
        FILL = [3, 3, 2, 2, 2, 2, 2, 1, 2, 1, 2, 3, 0, 0, 0, 0, 0, 6]
        PARAMS_IN = 16 * 17
        POOL_SETUP = 9

        names = """const_in params_in vec_ps setup_dve setup_pool w_in0 w_in1 w_in2 w_in3 w_in4
            w_hi w_lo w_lo_pool wr_hi wr_lo bias_ps v2_bias_set k2_bias_set q2_bias_set m_bias_set o_bias_set
            f1_bias_set rows_in bm_rows
            x_in adj_in_ stats1 norm1 y_ready t1_ps yT_hi yT_lo k_ps k_hi k_lo kB_in0 kB_in1 v_ps v_hi v_lo vB_in0 vB_in1
            q_ps q_hi q_lo mask0_set ones_set xbv_set qB_clear p2z_clear adj_used s_ps s_read p_shift p_exp
            pt_ps pt_hi pt_lo pv_ps att_ready
            x1_ready stats2 norm2 hid_ready nh_ready t2_ps nT_hi nT_lo v2_ps v2_hi v2_lo
            k2_ps k2_hi k2_lo diag_set bc_ps z_set selT_ps y3T_ps gp_ps selT_set sT_hi sT_set
            gat_hi gat_lo pool_hi pool_lo q2_ps q2_set qB_hi qB_lo pw_ps pw_set R_lo_set R_hi s2_ps
            p2_shift p2_exp p2_set pt2_ps p2T_hi p2T_lo cx_ps ctx_hi ctx_lo o_ps A_set A_hi A_lo
            mix_ps sc_ps mix_read h_ready stats3 norm3 n2_ready t3_ps n2T_hi n2T_lo resid_set
            f1_ps f1_hi f1_lo f2_ps o_ready out_done dve_step pool_step x1b_set""".split()
        s = {n: sem(n) for n in names}

        block = ctx.enter_context(nc.Block())

        def count(g, per, j):
            return g * per + j

        class Steps:

            def __init__(self, eng, sem_):
                self.eng, self.sem, self.per, self.first, self.n, self.g = eng, sem_, None, 0, 0, 0

            def done(self, ins):
                self.n += 1
                return ins.then_inc(self.sem, 1)

            def settle(self):
                if isinstance(self.g, int) and self.g == 0:
                    self.eng.wait_ge(self.sem, self.first + self.n)
                else:
                    self.eng.wait_ge(self.sem, self.g * self.per + (self.first + self.n))

            def begin(self, g):
                if isinstance(g, int) and g == 0:
                    self.first = self.n
                self.g, self.n = g, 0

            def end(self):
                if self.per is None:
                    self.per = self.n

        def for_groups(eng, first_steps, both):
            first_steps()
            both(0, False, True)
            if groups > 2:
                with eng.Fori(1, groups - 1) as g:
                    both(g, True, True)
            both(groups - 1, True, False)

        LOADS = [("L0_gnn_Wv", 0, 0, None), ("L0_gnn_Wk", 0, 0, None), ("L0_gnn_Wq", 0, 0, QSCALE),
                 ("L0_ffn_Wv", 0, 0, g1), ("L0_ffn_Wm", 0, 0, g1), ("L0_ffn_Wo", 0, 0, None),
                 ("L0_ffn_Wk", 0, 0, g1), ("L0_ffn_Wq", 0, 0, g1q)]
        LOADS += [("L0_ffn_W1", 0, i, g2) for i in range(0, HIDDEN, D)]
        LOADS += [("L0_ffn_W2", i, 0, None) for i in range(0, HIDDEN, D)]
        GNN_V, GNN_K, GNN_Q, FFN_V, FFN_M, FFN_O, FFN_K, FFN_Q, FFN_1, FFN_2 = 0, 1, 2, 3, 4, 5, 6, 7, 8, 12
        STAGE_OF = [0, 1, 2, 3, 4, 0, 1, 2, 3, 4, 0, 1, 2, 3, 0, 1]

        LOWS = {"vector": [*range(FFN_2), FFN_2 + 1, FFN_2 + 2], "pool": [FFN_2, FFN_2 + 3]}

        def is_split(n):
            who = "vector" if n in LOWS["vector"] else "pool"
            return s["w_lo" if who == "vector" else "w_lo_pool"], KC * (LOWS[who].index(n) + 1)

        def loads_in(n):
            return 16 * STAGE_OF[:n + 1].count(STAGE_OF[n])

        def staged(n):
            return stage[STAGE_OF[n]].rearrange("p (c n) -> p c n", c=KC)

        def target(n, c, half_):
            name, row, col, _ = LOADS[n]
            part = staged(n)[:, c, :]
            if name == "L0_gnn_Wq":
                return w_qk[half_][:, c, 0:D], part
            if name == "L0_gnn_Wk":
                return w_qk[half_][:, c, D:2 * D], part
            if name == "L0_gnn_Wv":
                return (w_v[half_][:, c, :].rearrange("p (e a d) -> p e a d", e=2, a=PAIRS),
                        part.rearrange("p (a e d) -> p e a d", e=2, a=PAIRS))
            if name == "L0_ffn_Wv":
                return w_v2[half_][:, c, 0:D], part
            if name == "L0_ffn_W1":
                return w_1[half_][:, c, col:col + D], part
            if name == "L0_ffn_W2":
                return w_2[half_][:, row // P + c, :], part
            return {"L0_ffn_Wk": w_k2, "L0_ffn_Wq": w_q2, "L0_ffn_Wo": w_o, "L0_ffn_Wm": w_m}[name][half_][:, c, :], part

        def gain(n, c):
            by = LOADS[n][3]
            return by if by is None or isinstance(by, float) else by[:, c:c + 1]

        def bias_bank(n):
            return 6 + (n - FFN_V) % 2

        def bias_read(n):
            if n >= FFN_1:
                return s["f1_bias_set"], n - FFN_1 + 1
            return {FFN_V: (s["v2_bias_set"], 3), FFN_M: (s["m_bias_set"], 2), FFN_O: (s["o_bias_set"], 1),
                    FFN_K: (s["k2_bias_set"], 1), FFN_Q: (s["q2_bias_set"], 1)}[n]

        def biases_done(n):
            return min(n, FFN_2 - 1) - FFN_V + 1

        x_v = x.rearrange("(g t p) d -> g p t d", p=P, t=TILES)
        adj_v = adj.rearrange("(g t p) d -> g p t d", p=P, t=TILES)
        out_v = out.rearrange("(g t p) d -> g p t d", p=P, t=TILES)

        def of_group(v, g):
            if isinstance(g, int):
                return v[g]
            return v[bass.ds(g, 1)].rearrange("o p t d -> (o p) t d")

        @block.sync
        def _(sp):
            def load_x(g):
                sp.dma_start(xin[:, :, :], of_group(x_v, g)).then_inc(s["x_in"], 16)
                sp.dma_start(adj_in[:, :, :], of_group(adj_v, g)).then_inc(s["adj_in_"], 16)

            def wide(dst, name, rows):
                sp.dma_start(dst, w[name].rearrange("(a n) -> a n", a=1).to_broadcast([rows, dst.shape[1]]))\
                  .then_inc(s["params_in"], 16)

            def load_w(n):
                name, row, col, _ = LOADS[n]
                before_ = [m for m in range(n) if STAGE_OF[m] == STAGE_OF[n]]
                if before_:
                    sp.wait_ge(*is_split(before_[-1]))
                    if FFN_V <= before_[-1] < FFN_2:
                        sp.wait_ge(s["bias_ps"], biases_done(before_[-1]))
                sp.dma_start(staged(n), w[name][row:row + D, col:col + D].rearrange("(c p) n -> p c n", p=P))\
                  .then_inc(s[f"w_in{STAGE_OF[n]}"], 16)

            load_x(0)
            sp.dma_start(const[:, :], consts).then_inc(s["const_in"], 16)
            load_w(GNN_V)
            load_w(GNN_K)
            load_w(GNN_Q)
            for n, name in enumerate(VECTORS):
                rows = w[name].rearrange("(c p) -> c p", p=P)
                sp.dma_start(vec_rows[KC * n:KC * n + rows.shape[0], :], rows).then_inc(s["params_in"], 16)
            for dst, name, rows in ((bv_bc, "L0_gnn_bv", P), (bf2_bc, "L0_ffn_bf2", P), (bo_bc, "L0_ffn_bo", SELN),
                                    (bm_bc, "L0_ffn_bm", 96), (beta_bc, "L0_gnn_beta", P), (br_bc, "L0_ffn_br", P)):
                wide(dst[:, :], name, rows)
            for n in range(FFN_V, FFN_1):
                load_w(n)

            def load_rows():
                sp.wait_ge(s["bm_rows"], 2)
                sp.dma_start(R[73:74, :], Ah[0][0:1, :]).then_inc(s["rows_in"], 16)
                sp.dma_start(R[74:75, :], Ah[1][0:1, :]).then_inc(s["rows_in"], 16)

            def spread_k(t):
                for i in range(HQ):
                    q = slice(HD * i, HD * i + HD)
                    sp.dma_start(kB[q, t % 2, :, i, :],
                                 k_stage[q, :, :, t * P:(t + 1) * P].rearrange("p h c n -> p (h c) n"))\
                      .then_inc(s[f"kB_in{t % 2}"], 16)

            def spread_v(t):
                for b in range(2):
                    for e in range(2):
                        sp.dma_start(vB[64 * e:64 * e + 64, t % 2, :, b, e * VROW:(e + 1) * VROW],
                                     v_stage[64 * b:64 * b + 64, :, t, e * VROW:(e + 1) * VROW])\
                          .then_inc(s[f"vB_in{t % 2}"], 16)

            def start_v(g):
                sp.wait_ge(s["v_lo"], count(g, TILES, TILES))
                sp.wait_ge(s["ones_set"], count(g, 2, 2))
                spread_v(0)
                spread_v(1)

            def both(g, feed, more):
                sp.wait_ge(s["k_lo"], count(g, KC, KC))
                spread_k(0)
                spread_k(1)
                first = isinstance(g, int) and g == 0
                for t in range(2, TILES):
                    if first:
                        load_w(FFN_1 + t - 2)
                    sp.wait_ge(s["s_ps"], count(g, TILES, t - 1))
                    spread_k(t)
                for t in range(2, TILES):
                    sp.wait_ge(s["pv_ps"], count(g, TILES, t - 1))
                    spread_v(t)
                if more:
                    sp.wait_ge(s["x1_ready"], count(g, TILES, TILES))
                    load_x(g + 1)
                if first:
                    load_w(FFN_1 + 2)
                    load_w(FFN_1 + 3)
                    load_rows()
                    for n in range(FFN_2, len(LOADS)):
                        load_w(n)
                if feed:
                    send(g - 1)
                if more:
                    start_v(g + 1)

            def send(f):
                sp.wait_ge(s["o_ready"], count(f, TILES, TILES))
                sp.dma_start(of_group(out_v, f), resid[:, :, :]).then_inc(s["out_done"], 16)

            def first_steps():
                sp.wait_ge(s["setup_pool"], POOL_SETUP)
                start_v(0)

            for_groups(sp, first_steps, both)
            send(groups - 1)
            sp.wait_ge(s["out_done"], 16 * groups)

        @block.gpsimd
        def _(pl):
            steps = Steps(pl, s["pool_step"])

            for h in range(2):
                pl.memset(pool[h][:, :, :], 0.0).then_inc(s["setup_pool"], 1)
            pl.memset(R[:, :], 0.0).then_inc(s["setup_pool"], 1)
            pl.memset(Z[:, :], 0.0).then_inc(s["setup_pool"], 1)
            pl.memset(minus_half[:, :], -0.5).then_inc(s["setup_pool"], 1)
            pl.memset(Y3[:, :], 0.0).then_inc(s["setup_pool"], 1)
            pl.wait_ge(s["setup_pool"], POOL_SETUP - 3)
            pl.memset(Y3_tiles[:, :, 73:75], 1.0).then_inc(s["setup_pool"], 1)

            def norm(buffers, t, g, ready, signal):
                _, ve, neg_mean, rstd, nmr = buffers
                n = ve.shape[2]
                pl.wait_ge(ready, count(g, TILES, t + 1))
                steps.done(pl.tensor_tensor(rstd[:, t, :], ve[:, t, :], minus_half[:, 0:n], ALU.pow))
                steps.settle()
                pl.tensor_tensor(nmr[:, t, :], rstd[:, t, :], neg_mean[:, t:t + 1].to_broadcast([P, n]), ALU.mult)\
                  .then_inc(signal, 1)

            def feed_lo(f, m):
                pl.wait_ge(s["f1_hi"], count(f, HC, m + 1))
                pl.tensor_tensor(hT[1][:, m, :], gel[m % 2][:, :], hT[0][:, m, :], ALU.subtract)\
                  .then_inc(s["f1_lo"], 1)

            def rest(i):
                steps.done(pl.tensor_tensor(spent[:, i:i + 1], minus_half[:, 0:1], minus_half[:, 0:1], ALU.add))

            def lows(n):
                for c in range(KC):
                    pl.wait_ge(s["w_hi"], KC * n + c + 1)
                    (hi, part), (lo, _) = target(n, c, 0), target(n, c, 1)
                    pl.tensor_tensor(lo, part, hi, ALU.subtract).then_inc(s["w_lo_pool"], 1)

            def prepare(g):
                for t in range(TILES):
                    norm(norm1, t, g, s["stats1"], s["norm1"])
                pl.wait_ge(s["adj_in_"], count(g, 16, 16))
                rest(0)
                pl.tensor_scalar(mask[:, :, :], adj_in[:, :, :], 0.0, MASKED, ALU.is_le, ALU.mult)\
                  .then_inc(s["mask0_set"], 1)

            def add_bv(g):
                for t in range(TILES):
                    pl.wait_ge(s["y_ready"], count(g, TILES, t + 1))
                    pl.tensor_tensor(xin[:, t, :], xin[:, t, :], bv_bc[:, :], ALU.add).then_inc(s["xbv_set"], 1)

            def sum_columns(g):
                sums = [v_stage[:, h, :, :].rearrange("p t (a w) -> p (t a) w", w=VW)[:, :, HD:VW] for h in range(2)]
                pl.memset(sums[0], 1.0).then_inc(s["ones_set"], 1)
                pl.memset(sums[1], 0.0).then_inc(s["ones_set"], 1)

            def first_steps():
                prepare(0)
                sum_columns(0)
                pl.memset(vB[:, :, :, :, :], 0.0).then_inc(s["setup_pool"], 1)
                pl.memset(kB[:, :, :, :, :], 0.0).then_inc(s["setup_pool"], 1)
                pl.wait_ge(s["params_in"], PARAMS_IN)
                add_bv(0)

            def both(g, feed, more):
                steps.begin(g)
                if feed:
                    for m in range(HC):
                        feed_lo(g - 1, m)
                for t in range(TILES):
                    pl.wait_ge(s["xbv_set"], count(g, TILES, t + 1))
                    pl.wait_ge(s["att_ready"], count(g, TILES, t + 1))
                    pl.tensor_tensor(x1[:, t, :], att[t % 2], xin[:, t, :], ALU.add).then_inc(s["x1_ready"], 1)
                    if 1 <= t < TILES - 1:
                        norm(norm2, t - 1, g, s["stats2"], s["norm2"])
                    if t == TILES - 2:
                        norm(norm2, t, g, s["stats2"], s["norm2"])
                norm(norm2, TILES - 1, g, s["stats2"], s["norm2"])
                for h in range(2):
                    pl.memset(qB[h].bitcast(F32), 0.0).then_inc(s["qB_clear"], 1)
                for t in range(TILES):
                    pl.wait_ge(s["hid_ready"], count(g, TILES, t + 1))
                    pl.tensor_tensor(x1[:, t, :], x1[:, t, :], bf2_bc[:, :], ALU.add).then_inc(s["x1b_set"], 1)
                pl.wait_ge(s["bc_ps"], count(g, 1, 1))
                rest(1)
                pl.memset(space_g[0:SROWS, :, :], 0.0).then_inc(s["p2z_clear"], 1)
                if more:
                    prepare(g + 1)
                    pl.wait_ge(s["cx_ps"], count(g, 1, 1))
                    rest(2)
                    sum_columns(g + 1)
                    add_bv(g + 1)
                if not feed:
                    lows(FFN_2)
                pl.wait_ge(s["x1b_set"], count(g, TILES, TILES))
                if feed:
                    pl.wait_ge(s["out_done"], count(g, 16, 0))
                else:
                    pl.wait_ge(*is_split(FFN_1 + 1))
                    pl.wait_ge(s["bias_ps"], biases_done(FFN_1 + 1))
                for t in range(TILES + 1):
                    if t < TILES:
                        norm(norm3, t, g, s["stats3"], s["norm3"])
                    if t >= 1:
                        pl.tensor_tensor(resid[:, t - 1, :], hid[:, t - 1, :], x1[:, t - 1, :], ALU.add)\
                          .then_inc(s["resid_set"], 1)
                if not feed:
                    lows(FFN_2 + 3)
                steps.end()

            for_groups(pl, first_steps, both)
            for m in range(HC):
                feed_lo(groups - 1, m)

        @block.scalar
        def _(act):
            split = iter([(n, c) for n in range(len(LOADS)) for c in range(KC)])

            def high(steps_):
                for _ in range(steps_):
                    n, c = next(split)
                    if c == 0:
                        act.wait_ge(s[f"w_in{STAGE_OF[n]}"], loads_in(n))
                        if n >= FFN_V:
                            act.wait_ge(s["setup_dve"], 4)
                    dst, part = target(n, c, 0)
                    scale = gain(n, c)
                    if scale is None:
                        act.activation(dst, part, ACT.Copy).then_inc(s["w_hi"], 1)
                    else:
                        act.activation(dst, part, ACT.Copy, scale=scale).then_inc(s["w_hi"], 1)
                    if (n, c) == (FFN_V, KC - 1):
                        act.wait_ge(s["setup_dve"], 5)
                        act.activation(w_v2[0][:, :, D:D + 1], wrg[:, :].unsqueeze(2), ACT.Copy).then_inc(s["wr_hi"], 1)

            def feed_hi(f, m):
                act.wait_ge(s["f1_ps"], count(f, HC, m + 1))
                if m >= 2:
                    act.wait_ge(s["f1_lo"], count(f, HC, m - 1))
                act.activation(gel[m % 2], bank(6 + m % 2), ACT.Gelu, bias=bf1[:, m:m + 1])
                act.activation(hT[0][:, m, :], bank(6 + m % 2), ACT.Gelu, bias=bf1[:, m:m + 1])\
                   .then_inc(s["f1_hi"], 1)

            def make_y(g):
                for t in range(TILES):
                    act.wait_ge(s["norm1"], count(g, TILES, t + 1))
                    act.activation(y[:, t, :], xin[:, t, :], ACT.Identity, bias=norm1[4][:, t, 0:1],
                                   scale=norm1[3][:, t, 0:1]).then_inc(s["y_ready"], 1)

            def transposed(dst, t, o, ready, g, signal):
                act.wait_ge(ready, count(g, TILES, t + 1))
                act.copy(dst[0][:, :, t * P:(t + 1) * P], bank(o, width=D).rearrange("p (c n) -> p c n", c=KC))\
                   .then_inc(signal, 1)

            def v_high(g, t):
                act.wait_ge(s["v_ps"], count(g, TILES, t + 1))
                act.copy(v_stage[:, 0, t, :].rearrange("p (a w) -> p a w", w=VW)[:, :, 0:HD],
                         bank(V_BANK[t], width=D).rearrange("p (a d) -> p a d", d=HD)).then_inc(s["v_hi"], 1)

            def first_steps():
                make_y(0)
                high(KC)
                for t in range(TILES):
                    transposed(yT, t, T1_BANK[t], s["t1_ps"], 0, s["yT_hi"])
                high(KC)
                for t in range(TILES):
                    v_high(0, t)
                    if t < KC:
                        high(1)

            def both(g, feed, more):
                first = isinstance(g, int) and g == 0

                def also(n):
                    if first:
                        high(n)

                if first:
                    act.wait_ge(s["setup_dve"], 3)
                for c in range(KC):
                    act.wait_ge(s["k_ps"], count(g, KC, c + 1))
                    if c == 0 and feed:
                        act.wait_ge(s["resid_set"], count(g, TILES, 0))
                    act.activation(k_stage[:, 0, c, :], bank(K_BANK[c]), ACT.Identity, bias=bk[:, c:c + 1])\
                       .then_inc(s["k_hi"], 1)
                    also(1)
                if feed:
                    for m in range(HC):
                        feed_hi(g - 1, m)
                for c in range(KC):
                    act.wait_ge(s["q_ps"], count(g, KC, c + 1))
                    act.activation(qT[0][:, c, :], bank(Q_BANK[c]), ACT.Identity, bias=bq[:, c:c + 1])\
                       .then_inc(s["q_hi"], 1)
                    also(1)

                def expo(t):
                    act.wait_ge(s["p_shift"], count(g, TILES, t + 1))
                    act.activation(probs[t % 2][:, :, :], probs[t % 2][:, :, :], ACT.Exp).then_inc(s["p_exp"], 1)

                def turned(t):
                    act.wait_ge(s["pt_ps"], count(g, TILES, t + 1))
                    act.copy(pT[t % 2][0].rearrange("p (b n) -> p b n", b=2), banks(0, 2)[:, :, 0:D])\
                       .then_inc(s["pt_hi"], 1)

                def normed(t):
                    act.wait_ge(s["norm2"], count(g, TILES, t + 1))
                    act.activation(nh[:, t, :], x1[:, t, :], ACT.Identity, bias=norm2[4][:, t, 1:2],
                                   scale=norm2[3][:, t, 1:2]).then_inc(s["nh_ready"], 1)

                def v2_high(t):
                    if first and t == 0:
                        act.wait_ge(s["v2_bias_set"], 3)
                    act.wait_ge(s["v2_ps"], count(g, TILES, t + 1))
                    act.activation(ez[:, t:t + 1], bank(V2_BANK[t])[:, D:D + 1], ACT.Exp, bias=neg_z0[:, 0:1],
                                   scale=-1.0)
                    act.copy(v2[0][:, t, :], bank(V2_BANK[t], width=D)).then_inc(s["v2_hi"], 1)

                expo(0)
                turned(0)
                expo(1)
                also(KC)
                expo(2)
                turned(1)
                also(KC)
                expo(3)
                turned(2)
                also(KC)
                normed(0)
                turned(3)
                transposed(nT, 0, T2_BANK[0], s["t2_ps"], g, s["nT_hi"])
                normed(1)
                transposed(nT, 1, T2_BANK[1], s["t2_ps"], g, s["nT_hi"])
                normed(2)
                v2_high(0)
                also(2)
                transposed(nT, 2, T2_BANK[2], s["t2_ps"], g, s["nT_hi"])
                normed(3)
                v2_high(1)
                also(2)
                transposed(nT, 3, T2_BANK[3], s["t2_ps"], g, s["nT_hi"])
                v2_high(2)
                also(2)
                v2_high(3)
                for t in range(TILES):
                    act.activation(hid[:, t, :], x1[:, t, :], ACT.Identity, bias=norm2[4][:, t, 0:1],
                                   scale=norm2[3][:, t, 0:1]).then_inc(s["hid_ready"], 1)
                if first:
                    act.wait_ge(s["k2_bias_set"], 1)
                for c in range(KC):
                    act.wait_ge(s["k2_ps"], count(g, KC, c + 1))
                    act.activation(kT2[0][:, c, :], bank(K2_BANK[c]), ACT.Identity, bias=bk2[:, c:c + 1])\
                       .then_inc(s["k2_hi"], 1)
                act.wait_ge(s["gp_ps"], count(g, 1, 1))
                gp = bank(GP_BANK, width=KC * ZW).rearrange("p (c k) -> p c k", k=ZW)
                act.copy(gat[0][:, :, :], gp[:, :, 0:SELN]).then_inc(s["gat_hi"], 1)
                for o in (0, 32, 64):
                    last = act.copy(pool[0][:, :, o:o + GB], gp[:, :, SELN:ZW])
                last.then_inc(s["pool_hi"], 1)
                act.wait_ge(s["selT_ps"], count(g, 1, 1))
                act.copy(selT[:, :], bank(SELT_BANK, SELN)).then_inc(s["selT_set"], 1)
                act.wait_ge(s["y3T_ps"], count(g, 1, 1))
                act.activation(sT[:, :], bank(Y3T_BANK, 96), ACT.Copy, accum_out=ssum[:, :]).then_inc(s["sT_hi"], 1)
                also(KC)
                act.wait_ge(s["q2_set"], count(g, 1, 1))
                act.wait_ge(s["qB_clear"], count(g, 2, 2))
                for i in range(HQ):
                    act.copy(qB_head(qB[0], i), q2[HD * i:HD * i + HD, :, :].rearrange("p c (b q) -> p c b q", q=TOPK))\
                       .then_inc(s["qB_hi"], 1)
                also(KC)
                act.wait_ge(s["pw_set"], count(g, 1, 1))
                act.copy(R[0:64, :], pw[0:64, :])
                act.copy(R[64:64 + GB, :], pw[64:64 + GB, :]).then_inc(s["R_hi"], 1)
                act.wait_ge(s["p2_shift"], count(g, 1, 1))
                act.activation(p2, p2, ACT.Exp).then_inc(s["p2_exp"], 1)
                also(KC)
                act.wait_ge(s["pt2_ps"], count(g, 1, 1))
                half_bank = GB // 2 * SROWS
                for i in range(2):
                    act.copy(p2T[0].rearrange("p (h b) r -> p h (b r)", h=2)[:, i, :], bank(PT2_BANK + i, width=half_bank))\
                       .then_inc(s["p2T_hi"], 1)
                act.wait_ge(s["cx_ps"], count(g, 1, 1))
                for i in range(HQ):
                    act.copy(ctx_head(ctxT[0], i), cx_head(i)).then_inc(s["ctx_hi"], 1)
                if more:
                    make_y(g + 1)
                act.wait_ge(s["A_set"], count(g, 1, 1))
                if first:
                    act.wait_ge(s["rows_in"], 32)
                act.copy(Ah[0][:, :], A).then_inc(s["A_hi"], 1)
                also(KC)
                act.wait_ge(s["mix_ps"], count(g, TILES, TILES))
                if more:
                    for t in range(TILES):
                        transposed(yT, t, T1_BANK[t], s["t1_ps"], g + 1, s["yT_hi"])
                for t in range(TILES):
                    act.wait_ge(s["norm3"], count(g, TILES, t + 1))
                    act.activation(n2[:, t, :], hid[:, t, :], ACT.Identity, bias=norm3[4][:, t, 0:1],
                                   scale=norm3[3][:, t, 0:1]).then_inc(s["n2_ready"], 1)
                    if more:
                        v_high(g + 1, t)
                for t in range(TILES):
                    transposed(n2T, t, T3_BANK[t], s["t3_ps"], g, s["n2T_hi"])
                if first:
                    high(2 * KC)
                    act.wait_ge(s["f1_bias_set"], 4)
                    act.wait_ge(*is_split(FFN_2 + 2))
                    act.wait_ge(*is_split(FFN_2 + 3))

            for_groups(act, first_steps, both)
            for m in range(HC):
                feed_hi(groups - 1, m)

        @block.vector
        def _(dve):
            steps = Steps(dve, s["dve_step"])
            dve.memset(ones[:, :], 1.0).then_inc(s["setup_dve"], 1)

            def prepare_vectors():
                dve.wait_ge(s["vec_ps"], 1)
                dve.tensor_copy(vecs[:, :], bank(7, width=NVEC)).then_inc(s["setup_dve"], 1)
                dve.wait_ge(s["setup_dve"], 2)
                dve.tensor_scalar(bq, bq, QSCALE, None, ALU.mult).then_inc(s["setup_dve"], 1)
                dve.tensor_scalar(g1q[:, :], g1, QSCALE, None, ALU.mult).then_inc(s["setup_dve"], 1)
                dve.tensor_tensor(wrg[:, :], wr, g1, ALU.mult).then_inc(s["setup_dve"], 1)
                dve.tensor_copy(wr_bc, wr.unsqueeze(2).to_broadcast([P, KC, P])).then_inc(s["setup_dve"], 1)
                dve.tensor_copy(b1_bc, b1.unsqueeze(2).to_broadcast([P, KC, 96])).then_inc(s["setup_dve"], 1)
                dve.wait_ge(s["setup_dve"], 7)
                dve.wait_ge(s["params_in"], PARAMS_IN)

            def bias_sums(n):
                dve.wait_ge(s["bias_ps"], biases_done(n))
                ps = bank(bias_bank(n))
                if n == FFN_V:
                    dve.tensor_tensor(bv2, ps[:, 0:KC], bv2, ALU.add).then_inc(s["v2_bias_set"], 1)
                    dve.wait_ge(s["v2_bias_set"], 1)
                    dve.tensor_copy(bv2_bc, bv2.unsqueeze(2).to_broadcast([P, KC, SELN])).then_inc(s["v2_bias_set"], 1)
                    dve.scalar_tensor_tensor(neg_z0[:, :], ps[:, KC:KC + 1], -1.0, br_bc[:, :], ALU.mult, ALU.subtract)\
                       .then_inc(s["v2_bias_set"], 1)
                    dve.wait_ge(s["wr_hi"], 1)
                    dve.tensor_tensor(w_v2[1][:, :, D:D + 1], wrg[:, :].unsqueeze(2), w_v2[0][:, :, D:D + 1],
                                      ALU.subtract).then_inc(s["wr_lo"], 1)
                elif n == FFN_K:
                    dve.tensor_tensor(bk2, ps[:, 0:KC], bk2, ALU.add).then_inc(s["k2_bias_set"], 1)
                elif n == FFN_Q:
                    dve.tensor_tensor(bq2, ps[:, 0:KC], bq2, ALU.add).then_inc(s["q2_bias_set"], 1)
                    dve.wait_ge(s["q2_bias_set"], 1)
                    dve.tensor_scalar(bq2, bq2, QSCALE, None, ALU.mult).then_inc(s["q2_bias_set"], 1)
                elif n == FFN_M:
                    dve.tensor_copy(b1wm_bc[:, :], ps[0:96, 0:D]).then_inc(s["m_bias_set"], 1)
                    dve.tensor_tensor(bm_bc[:, :], ps[0:96, 0:D], bm_bc[:, :], ALU.add).then_inc(s["m_bias_set"], 1)
                    dve.wait_ge(s["m_bias_set"], 2)
                    dve.tensor_copy(Ah[0][0:1, :], bm_bc[0:1, :]).then_inc(s["bm_rows"], 1)
                    dve.wait_ge(s["bm_rows"], 1)
                    dve.tensor_tensor(Ah[1][0:1, :], bm_bc[0:1, :], Ah[0][0:1, :], ALU.subtract)\
                       .then_inc(s["bm_rows"], 1)
                elif n == FFN_O:
                    dve.tensor_tensor(bo_bc[:, :], ps[0:SELN, 0:D], bo_bc[:, :], ALU.add).then_inc(s["o_bias_set"], 1)
                else:
                    mine = bf1[:, KC * (n - FFN_1):KC * (n - FFN_1 + 1)]
                    dve.tensor_tensor(mine, ps[:, 0:KC], mine, ALU.add).then_inc(s["f1_bias_set"], 1)

            split = iter([(n, c) for n in LOWS["vector"] for c in range(KC)])

            def lows(steps_):
                for _ in range(steps_):
                    n, c = next(split)
                    dve.wait_ge(s["w_hi"], KC * n + c + 1)
                    dst, part = target(n, c, 1)
                    hi, _ = target(n, c, 0)
                    scale = gain(n, c)
                    if scale is None:
                        dve.tensor_tensor(dst, part, hi, ALU.subtract).then_inc(s["w_lo"], 1)
                    else:
                        dve.scalar_tensor_tensor(dst, part, scale, hi, ALU.mult, ALU.subtract).then_inc(s["w_lo"], 1)
                    if c == KC - 1 and FFN_O <= n < FFN_1:
                        bias_sums(n)

            def stats(t, src, buffers, signal):
                mv, ve, neg_mean, _, _ = buffers
                steps.done(dve.bn_stats(bn[:, t, :], src))
                steps.settle()
                steps.done(dve.memset(pause[:, :], 0.0))
                steps.done(dve.bn_aggr(mv[:, t, :], bn[:, t, :]))
                steps.settle()
                dve.tensor_scalar(ve[:, t, 0:1], mv[:, t, 1:2], EPS, None, ALU.add)
                if ve.shape[2] == 2:
                    dve.tensor_scalar(ve[:, t, 1:2], mv[:, t, 1:2], 1.0 + EPS, EPS * EPS, ALU.mult, ALU.add)
                dve.tensor_scalar(neg_mean[:, t:t + 1], mv[:, t, 0:1], -1.0, None, ALU.mult).then_inc(signal, 1)

            def summed(f, t):
                dve.wait_ge(s["resid_set"], count(f, TILES, t + 1))
                dve.wait_ge(s["f2_ps"], count(f, TILES, t + 1))
                dve.tensor_tensor(resid[:, t, :], bank(6 + t % 2, width=D), resid[:, t, :], ALU.add)\
                   .then_inc(s["o_ready"], 1)

            def low(dst, t, o, ready, g, signal):
                tok = slice(t * P, (t + 1) * P)
                dve.wait_ge(ready, count(g, TILES, t + 1))
                dve.tensor_tensor(dst[1][:, :, tok], bank(o, width=D).rearrange("p (c n) -> p c n", c=KC),
                                  dst[0][:, :, tok], ALU.subtract).then_inc(signal, 1)

            def y_stats(g, t):
                dve.wait_ge(s["x_in"], count(g, 16, 16))
                stats(t, xin[:, t, :], norm1, s["stats1"])

            def finish_mask(g):
                dve.wait_ge(s["mask0_set"], count(g, 1, 1))
                dve.scalar_tensor_tensor(mask[:, :, :], adj_in[:, :, :], beta_bc[:, 0:1], mask[:, :, :],
                                         ALU.mult, ALU.add).then_inc(s["adj_used"], 1)

            def v_low(g, t):
                dve.wait_ge(s["v_hi"], count(g, TILES, t + 1))
                vs = [v_stage[:, h, t, :].rearrange("p (a w) -> p a w", w=VW)[:, :, 0:HD] for h in range(2)]
                dve.tensor_tensor(vs[1], bank(V_BANK[t], width=D).rearrange("p (a d) -> p a d", d=HD), vs[0],
                                  ALU.subtract).then_inc(s["v_lo"], 1)

            def first_steps():
                for t in range(TILES):
                    y_stats(0, t)
                lows(KC)
                for t in range(TILES):
                    low(yT, t, T1_BANK[t], s["yT_hi"], 0, s["yT_lo"])
                lows(KC)
                prepare_vectors()
                finish_mask(0)
                for t in range(TILES):
                    v_low(0, t)
                    if t < KC:
                        lows(1)

            def both(g, feed, more):
                f = g - 1
                first = isinstance(g, int) and g == 0

                def also(n):
                    if first:
                        lows(n)

                steps.begin(g)
                if first:
                    dve.wait_ge(s["setup_dve"], 3)
                dve.wait_ge(s["adj_used"], count(g, 1, 1))
                for c in range(KC):
                    dve.wait_ge(s["k_hi"], count(g, KC, c + 1))
                    dve.scalar_tensor_tensor(k_stage[:, 1, c, :], bank(K_BANK[c]), bk[:, c:c + 1],
                                             k_stage[:, 0, c, :], ALU.add, ALU.subtract).then_inc(s["k_lo"], 1)
                    also(1)
                for c in range(KC):
                    dve.wait_ge(s["q_hi"], count(g, KC, c + 1))
                    dve.scalar_tensor_tensor(qT[1][:, c, :], bank(Q_BANK[c]), bq[:, c:c + 1],
                                             qT[0][:, c, :], ALU.add, ALU.subtract).then_inc(s["q_lo"], 1)
                    also(1)

                def shift(t):
                    pr = probs[t % 2]
                    sp_ = psum[:, 2 + 2 * (t % 2):4 + 2 * (t % 2), :].rearrange("p b n -> p (b n)")
                    sc = sp_[:, 0:HEADS * NODES].rearrange("p (h n) -> p h n", n=NODES)
                    dve.wait_ge(s["s_ps"], count(g, TILES, t + 1))
                    if t >= 2:
                        dve.wait_ge(s["pt_ps"], count(g, TILES, t - 1))
                    dve.tensor_tensor(pr, sc, mask[:, t, :].unsqueeze(1).to_broadcast([P, HEADS, NODES]),
                                      ALU.add).then_inc(s["s_read"], 1)
                    dve.wait_ge(s["s_read"], count(g, TILES, t + 1))
                    steps.done(dve.tensor_reduce(smax[:, :], pr, AX_X, ALU.max))
                    steps.settle()
                    dve.tensor_tensor(pr, pr, smax[:, :].unsqueeze(2).to_broadcast([P, HEADS, NODES]),
                                      ALU.subtract).then_inc(s["p_shift"], 1)

                def turned(t):
                    dve.wait_ge(s["pt_hi"], count(g, TILES, t + 1))
                    dve.tensor_tensor(pT[t % 2][1].rearrange("p (b n) -> p b n", b=2), banks(0, 2)[:, :, 0:D],
                                      pT[t % 2][0].rearrange("p (b n) -> p b n", b=2), ALU.subtract)\
                       .then_inc(s["pt_lo"], 1)

                def weighted(t):
                    pv = bank(PV_BANK[t], width=HEADS * VW).rearrange("p (h w) -> p h w", w=VW)
                    dve.wait_ge(s["pv_ps"], count(g, TILES, t + 1))
                    steps.done(dve.reciprocal(rden[:, :].unsqueeze(2), pv[:, :, HD:VW]))
                    steps.settle()
                    if t >= 2:
                        dve.wait_ge(s["x1_ready"], count(g, TILES, t - 1))
                    dve.tensor_tensor(att[t % 2].rearrange("p (h d) -> p h d", d=HD), pv[:, :, 0:HD],
                                      rden[:, :].unsqueeze(2).to_broadcast([P, HEADS, HD]), ALU.mult)\
                       .then_inc(s["att_ready"], 1)

                def x1_stats(t):
                    dve.wait_ge(s["x1_ready"], count(g, TILES, t + 1))
                    stats(t, x1[:, t, :], norm2, s["stats2"])

                def v2_low(t):
                    dve.wait_ge(s["v2_hi"], count(g, TILES, t + 1))
                    dve.tensor_tensor(v2[1][:, t, :], bank(V2_BANK[t], width=D), v2[0][:, t, :], ALU.subtract)\
                       .then_inc(s["v2_lo"], 1)

                def k2_low(c):
                    dve.wait_ge(s["k2_hi"], count(g, KC, c + 1))
                    dve.scalar_tensor_tensor(kT2[1][:, c, :], bank(K2_BANK[c]), bk2[:, c:c + 1], kT2[0][:, c, :],
                                             ALU.add, ALU.subtract).then_inc(s["k2_lo"], 1)

                def sum_of(t):
                    if feed:
                        summed(f, t)

                if first:
                    bias_sums(FFN_V)
                    bias_sums(FFN_M)
                shift(0)
                shift(1)
                turned(0)
                shift(2)
                weighted(0)
                turned(1)
                shift(3)
                sum_of(0)
                weighted(1)
                x1_stats(0)
                turned(2)
                weighted(2)
                x1_stats(1)
                turned(3)
                x1_stats(2)
                low(nT, 0, T2_BANK[0], s["nT_hi"], g, s["nT_lo"])
                weighted(3)
                also(1)
                low(nT, 1, T2_BANK[1], s["nT_hi"], g, s["nT_lo"])
                x1_stats(3)
                v2_low(0)
                also(2)
                low(nT, 2, T2_BANK[2], s["nT_hi"], g, s["nT_lo"])
                v2_low(1)
                also(2)
                low(nT, 3, T2_BANK[3], s["nT_hi"], g, s["nT_lo"])
                v2_low(2)
                also(2)
                sum_of(1)
                dve.wait_ge(s["v2_hi"], count(g, TILES, TILES))
                steps.done(dve.tensor_scalar(ez1[:, :], ez[:, :], 1.0, None, ALU.add))
                steps.settle()
                steps.done(dve.reciprocal(score[:, :], ez1[:, :]))
                steps.settle()
                for t in range(TILES):
                    last = dve.tensor_scalar(diag[:, t, :], ident, score[:, t:t + 1], None, ALU.mult)
                last.then_inc(s["diag_set"], 1)
                v2_low(3)
                also(2)
                if more:
                    y_stats(g + 1, 0)
                    y_stats(g + 1, 1)
                dve.wait_ge(s["bc_ps"], count(g, 1, 1))
                for t in range(TILES):
                    everyone = bank(BC_BANK)[:, t * P:(t + 1) * P]
                    dve.scalar_tensor_tensor(scratch[:, 2 * t, :], everyone, score[:, t:t + 1], before, ALU.is_le,
                                             ALU.mult, accum_out=cnt_b[:, t:t + 1])
                    last = dve.scalar_tensor_tensor(scratch[:, 2 * t + 1, :], everyone, score[:, t:t + 1], after, ALU.is_lt,
                                                    ALU.mult, accum_out=cnt_a[:, t:t + 1])
                    steps.done(last)
                steps.settle()
                steps.done(dve.tensor_tensor(rank[:, :], cnt_b[:, :], cnt_a[:, :], ALU.add))
                steps.settle()
                dve.tensor_scalar(unchosen[:, :], rank[:, :], float(TOPK), None, ALU.is_ge)
                dve.tensor_tensor(Z_sel, iota.unsqueeze(1).to_broadcast([P, TILES, 2 * TOPK]),
                                  rank[:, :].unsqueeze(2).to_broadcast([P, TILES, 2 * TOPK]), ALU.is_equal)
                halves = half.unsqueeze(1).to_broadcast([P, TILES, 2])
                scores2 = score[:, :].unsqueeze(2).to_broadcast([P, TILES, 2])
                for v in Y3_score:
                    dve.tensor_tensor(v, halves, scores2, ALU.mult)
                dve.tensor_tensor(Z_score, halves, scores2, ALU.mult).then_inc(s["z_set"], 1)
                if first:
                    dve.wait_ge(s["k2_bias_set"], 1)
                for c in range(KC):
                    k2_low(c)
                if first:
                    bias_sums(FFN_1)
                also(1)
                if more:
                    y_stats(g + 1, 2)
                    y_stats(g + 1, 3)
                gp = bank(GP_BANK, width=KC * ZW).rearrange("p (c k) -> p c k", k=ZW)
                dve.wait_ge(s["gat_hi"], count(g, 1, 1))
                dve.wait_ge(s["pool_hi"], count(g, 1, 1))
                dve.tensor_tensor(gat[1][:, :, :], gp[:, :, 0:SELN], gat[0][:, :, :], ALU.subtract)\
                   .then_inc(s["gat_lo"], 1)
                for o in (0, 32, 64):
                    dve.tensor_tensor(pool[1][:, :, o:o + GB], gp[:, :, SELN:ZW], pool[0][:, :, o:o + GB],
                                      ALU.subtract)
                dve.wait_ge(s["sT_hi"], count(g, 1, 1))
                steps.done(dve.tensor_scalar(ssum_e[:, :], ssum[:, :], 1e-6, None, ALU.add))
                steps.settle()
                dve.reciprocal(rsum[:, :], ssum_e[:, :]).then_inc(s["pool_lo"], 1)
                dve.tensor_tensor(sT[32:64, :], psum[32:64, Y3T_BANK, :], sT[32:64, :], ALU.subtract)\
                   .then_inc(s["sT_set"], 1)
                dve.wait_ge(s["q2_ps"], count(g, 1, 1))
                if first:
                    dve.wait_ge(s["q2_bias_set"], 2)
                    dve.wait_ge(s["m_bias_set"], 2)
                q2p = bank(Q2_BANK, width=KC * SELN).rearrange("p (c k) -> p c k", k=SELN)
                dve.tensor_tensor(q2[:, :, :], q2p, bq2.unsqueeze(2).to_broadcast([P, KC, SELN]), ALU.add)\
                   .then_inc(s["q2_set"], 1)
                for i in range(HQ):
                    dve.wait_ge(s["qB_hi"], count(g, HQ, i + 1))
                    last = dve.tensor_tensor(qB_head(qB[1], i),
                                             q2[HD * i:HD * i + HD, :, :].rearrange("p c (b q) -> p c b q", q=TOPK),
                                             qB_head(qB[0], i), ALU.subtract)
                last.then_inc(s["qB_lo"], 1)
                if first:
                    bias_sums(FFN_1 + 1)
                also(2)
                dve.wait_ge(s["pw_ps"], count(g, 1, 1))
                dve.wait_ge(s["pool_lo"], count(g, 1, 1))
                steps.done(dve.scalar_tensor_tensor(pw[:, :], b1wm_bc[:, :], ssum[:, 0:1], bank(PW_BANK, 96, D),
                                                    ALU.mult, ALU.add))
                steps.settle()
                dve.tensor_scalar(pw[:, :], pw[:, :], rsum[:, 0:1], None, ALU.mult)\
                   .then_inc(s["pw_set"], 1)
                dve.wait_ge(s["R_hi"], count(g, 1, 1))
                dve.tensor_tensor(R[64:64 + GB, :], pw[64:64 + GB, :], R[64:64 + GB, :], ALU.subtract)\
                   .then_inc(s["R_lo_set"], 1)
                sum_of(2)
                if more:
                    finish_mask(g + 1)
                also(2)
                dve.wait_ge(s["s2_ps"], count(g, 1, 1))
                s2 = bank(S2_BANK, SROWS).rearrange("p (b n) -> p b n", n=NODES)
                steps.done(dve.tensor_reduce(smax2[:, :], s2, AX_X, ALU.max))
                steps.settle()
                dve.tensor_tensor(p2, s2, smax2[:, :].unsqueeze(2).to_broadcast([SROWS, GB, NODES]),
                                  ALU.subtract).then_inc(s["p2_shift"], 1)
                also(2)
                dve.wait_ge(s["p2_exp"], count(g, 1, 1))
                steps.done(dve.tensor_reduce(den2[:, :], p2, AX_X, ALU.add))
                steps.settle()
                steps.done(dve.reciprocal(rden2[:, :], den2[:, :]))
                steps.settle()
                dve.wait_ge(s["p2z_clear"], count(g, 1, 1))
                for b in range(2):
                    o = NODES * b
                    last = dve.tensor_tensor(
                        p2z.rearrange("p (t b) k -> p t b k", b=2)[:, :, b, o:o + NODES],
                        p2.rearrange("p (t b) n -> p t b n", b=2)[:, :, b, :],
                        rden2[:, :].rearrange("p (t b) -> p t b", b=2)[:, :, b].unsqueeze(2)
                        .to_broadcast([SROWS, TILES, NODES]), ALU.mult)
                last.then_inc(s["p2_set"], 1)
                also(2)
                half_bank = GB // 2 * SROWS
                for i in range(2):
                    dve.wait_ge(s["p2T_hi"], count(g, 2, i + 1))
                    p2v = [p2T[h].rearrange("p (h b) r -> p h (b r)", h=2)[:, i, :] for h in range(2)]
                    last = dve.tensor_tensor(p2v[1], bank(PT2_BANK + i, width=half_bank), p2v[0], ALU.subtract)
                last.then_inc(s["p2T_lo"], 1)
                if first:
                    bias_sums(FFN_1 + 2)

                def mix_part(t):
                    dve.wait_ge(s["mix_ps"], count(g, TILES, t + 1))
                    dve.scalar_tensor_tensor(hid[:, t, :], bank(MIX_BANK[t], width=D), unchosen[:, t:t + 1],
                                             hid[:, t, :], ALU.mult, ALU.add).then_inc(s["mix_read"], 1)

                mix_part(0)
                for i in range(HQ):
                    dve.wait_ge(s["ctx_hi"], count(g, HQ, i + 1))
                    last = dve.tensor_tensor(ctx_head(ctxT[1], i), cx_head(i), ctx_head(ctxT[0], i), ALU.subtract)
                last.then_inc(s["ctx_lo"], 1)
                mix_part(1)
                sum_of(3)
                if first:
                    dve.wait_ge(s["o_bias_set"], 1)
                dve.wait_ge(s["o_ps"], count(g, 1, 1))
                dve.tensor_tensor(A, bank(O_BANK, SELN, D), bo_bc[:, :], ALU.add).then_inc(s["A_set"], 1)
                dve.wait_ge(s["A_hi"], count(g, 1, 1))
                dve.tensor_tensor(Ah[1][:, :], A, Ah[0][:, :], ALU.subtract).then_inc(s["A_lo"], 1)
                if first:
                    bias_sums(FFN_1 + 3)
                also(3)
                mix_part(2)
                mix_part(3)

                def whole(t):
                    dve.wait_ge(s["mix_read"], count(g, TILES, t + 1))
                    dve.wait_ge(s["sc_ps"], count(g, TILES, t + 1))
                    dve.tensor_tensor(hid[:, t, :], bank(SC_BANK[t], width=D), hid[:, t, :], ALU.add)\
                       .then_inc(s["h_ready"], 1)
                    dve.wait_ge(s["h_ready"], count(g, TILES, t + 1))
                    stats(t, hid[:, t, :], norm3, s["stats3"])

                def y_low(t):
                    if more:
                        low(yT, t, T1_BANK[t], s["yT_hi"], g + 1, s["yT_lo"])

                y_low(0)
                y_low(1)
                whole(0)
                y_low(2)
                whole(1)
                y_low(3)
                whole(2)
                if more:
                    v_low(g + 1, 0)
                whole(3)
                if more:
                    v_low(g + 1, 1)
                    v_low(g + 1, 2)
                    v_low(g + 1, 3)
                for t in range(TILES):
                    low(n2T, t, T3_BANK[t], s["n2T_hi"], g, s["n2T_lo"])
                if first:
                    lows(2 * KC)
                steps.end()

            for_groups(dve, first_steps, both)
            for t in range(TILES):
                summed(groups - 1, t)

        @block.tensor
        def _(pe):
            def product(o, lhs, rhs, terms, before_term=None):
                n, total_ = 0, 3 * len(terms)
                for k in terms:
                    if before_term is not None:
                        before_term(k)
                    for a, b in ((0, 0), (0, 1), (1, 0)):
                        last = pe.matmul(o, lhs(k, a), rhs(k, b), start=(n == 0), stop=(n == total_ - 1))
                        n += 1
                return last

            def turn(src, t, o, ready, g, signal):
                pe.wait_ge(ready, count(g, TILES, t + 1))
                for c in range(KC):
                    last = pe.transpose(bank(o)[:, c * P:(c + 1) * P], src[:, t, c * P:(c + 1) * P], ident)
                last.then_inc(signal, 1)

            pe.wait_ge(s["const_in"], 16)
            pe.wait_ge(s["setup_dve"], 1)

            def turn_vectors():
                pe.wait_ge(s["params_in"], PARAMS_IN)
                pe.transpose(bank(7, width=NVEC), vec_rows[:, :], const[0:NVEC, C_ID:C_ID + NVEC])\
                    .then_inc(s["vec_ps"], 1)

            def bias(n):
                pe.wait_ge(s[f"w_in{STAGE_OF[n]}"], loads_in(n))
                ps, W = bank(bias_bank(n)), staged(n)
                if n >= FFN_V + 2:
                    pe.wait_ge(*bias_read(n - 2))
                if n == FFN_V:
                    pe.wait_ge(s["setup_dve"], 7)
                if n == FFN_O:
                    pe.wait_ge(s["v2_bias_set"], 2)
                if n == FFN_O or n == FFN_M:
                    rows, lhs = (SELN, bv2_bc) if n == FFN_O else (96, b1_bc)
                    for c in range(KC):
                        last = pe.matmul(ps[0:rows, 0:D], lhs[:, c, :], W[:, c, :], start=(c == 0), stop=(c == KC - 1))
                else:
                    by = b2 if n >= FFN_1 else b1
                    for m in range(KC):
                        for c in range(KC):
                            last = pe.matmul(ps[:, m:m + 1], W[:, c, m * P:(m + 1) * P], by[:, c:c + 1],
                                             start=(c == 0), stop=(c == KC - 1))
                if n == FFN_V:
                    for c in range(KC):
                        last = pe.matmul(ps[:, KC:KC + 1], wr_bc[:, c, :], b1[:, c:c + 1], start=(c == 0),
                                         stop=(c == KC - 1))
                last.then_inc(s["bias_ps"], 1)

            def feed1(f, m):
                if m == 0:
                    pe.wait_ge(s["n2T_lo"], count(f, TILES, TILES))
                if m >= 2:
                    pe.wait_ge(s["f1_hi"], count(f, HC, m - 1))
                product(bank(6 + m % 2), lambda c, h: w_1[h][:, c, m * P:(m + 1) * P],
                        lambda c, h: n2T[h][:, c, :], range(KC)).then_inc(s["f1_ps"], 1)

            def feed2(f, t, part):
                if part == 0:
                    if t == 0:
                        pe.wait_ge(s["f1_lo"], count(f, HC, HC))
                    if t < 2:
                        pe.wait_ge(s["f1_hi"], count(f, HC, HC - 1 + t))
                    else:
                        pe.wait_ge(s["o_ready"], count(f, TILES, t - 1))
                n = part * PART * 3
                for m in range(part * PART, (part + 1) * PART):
                    for a, b in ((0, 0), (0, 1), (1, 0)):
                        last = pe.matmul(bank(6 + t % 2, width=D), hT[a][:, m, t * P:(t + 1) * P], w_2[b][:, m, :],
                                         start=(n == 0), stop=(n == 3 * HC - 1))
                        n += 1
                if part == PARTS - 1:
                    last.then_inc(s["f2_ps"], 1)

            def front_turns(g):
                for t in range(TILES):
                    if t >= 2 and not (isinstance(g, int) and g == 0):
                        pe.wait_ge(s["mix_read"], count(g - 1, TILES, t))
                    turn(y, t, T1_BANK[t], s["y_ready"], g, s["t1_ps"])

            def front_values(g):
                for t in range(TILES):
                    if t < 2 and not (isinstance(g, int) and g == 0):
                        pe.wait_ge(s["h_ready"], count(g - 1, TILES, t + 1))
                    pe.wait_ge(s["yT_lo"], count(g, TILES, t + 1))
                    product(bank(V_BANK[t], width=D), lambda c, h: yT[h][:, c, t * P:(t + 1) * P],
                            lambda c, h: w_v[h][:, c, :], range(KC)).then_inc(s["v_ps"], 1)

            def keys(g, m):
                later = not (isinstance(g, int) and g == 0)
                if m == 0 and later:
                    pe.wait_ge(s["h_ready"], count(g - 1, TILES, 3))
                if m == 1:
                    pe.wait_ge(s["v_lo"], count(g, TILES, TILES))
                if m == 2 and later:
                    pe.wait_ge(s["n2T_lo"], count(g - 1, TILES, 1))
                product(bank(K_BANK[m]), lambda c, h: w_qk[h][:, c, D + m * P:D + (m + 1) * P],
                        lambda c, h: yT[h][:, c, :], range(KC)).then_inc(s["k_ps"], 1)

            def first_steps():
                front_turns(0)
                turn_vectors()
                pe.wait_ge(*is_split(GNN_V))
                front_values(0)
                pe.wait_ge(*is_split(GNN_K))
                keys(0, 0)

            def both(g, feed, more):
                f = g - 1
                first = isinstance(g, int) and g == 0

                def needs(n):
                    if first:
                        pe.wait_ge(*is_split(n))

                def also(*loads_):
                    if first:
                        for n in loads_:
                            bias(n)

                feeds2 = [(t, part) for t in range(TILES) for part in range(PARTS)] if feed else []

                def fill(n):
                    for _ in range(n):
                        if feeds2:
                            feed2(f, *feeds2.pop(0))

                keys(g, 1)
                keys(g, 2)
                needs(GNN_Q)
                if feed:
                    for m in range(HC):
                        feed1(f, m)
                for m in range(KC):
                    product(bank(Q_BANK[m]), lambda c, h: w_qk[h][:, c, m * P:(m + 1) * P],
                            lambda c, h: yT[h][:, c, :], range(KC)).then_inc(s["q_ps"], 1)
                also(FFN_V, FFN_M)

                def scores(t):
                    if t == 0:
                        pe.wait_ge(s["q_lo"], count(g, KC, KC))
                    if t >= 2:
                        pe.wait_ge(s["s_read"], count(g, TILES, t - 1))
                    pe.wait_ge(s[f"kB_in{t % 2}"], count(g, 128, 64 * (t // 2 + 1)))
                    for b in range(2):
                        own = slice(b * NODES, (b + 1) * NODES)
                        tok = slice(t * P + b * NODES, t * P + (b + 1) * NODES)
                        for c in range(KC):
                            o = psum[b * NODES:(b + 1) * NODES, 2 + 2 * (t % 2) + c // 2,
                                     (c % 2) * 256:(c % 2) * 256 + 256]
                            for n, (a, k) in enumerate(((0, 0), (0, 1), (1, 0))):
                                    last = pe.matmul(o, qT[a][:, c, tok], kB[:, t % 2, k * KC + c, :, own],
                                                 start=(n == 0), stop=(n == 2))
                    last.then_inc(s["s_ps"], 1)

                def turn_probs(t):
                    pe.wait_ge(s["p_exp"], count(g, TILES, t + 1))
                    if t == 1:
                        pe.wait_ge(s["att_ready"], count(g, TILES, 1))
                    for a in range(PAIRS):
                        o = psum[:, a // 3, (a % 3) * P:(a % 3) * P + P]
                        last = pe.transpose(o, space_p[:, ((t % 2) * PAIRS + a) * P:((t % 2) * PAIRS + a + 1) * P], ident)
                    last.then_inc(s["pt_ps"], 1)

                def weigh(t):
                    pe.wait_ge(s["pt_lo"], count(g, TILES, t + 1))
                    if t >= 1:
                        pe.wait_ge(s["att_ready"] if t == 3 else s["s_read"], count(g, TILES, 2 if t == 3 else 3))
                    pe.wait_ge(s[f"vB_in{t % 2}"], count(g, 128, 64 * (t // 2 + 1)))
                    for b in range(2):
                        for a in range(PAIRS):
                            o = psum[b * NODES:(b + 1) * NODES, PV_BANK[t], a * 2 * VW:(a + 1) * 2 * VW]
                            col = slice(a * P + b * NODES, a * P + (b + 1) * NODES)
                            for n, (i, j) in enumerate(((0, 0), (0, 1), (1, 0))):
                                rhs = vB[:, t % 2, j, b, :].rearrange("p (e k) -> p e k", e=2)[:, :, a * VW:(a + 1) * VW]
                                last = pe.matmul(o, pT[t % 2][i][:, col], rhs, start=(n == 0), stop=(n == 2))
                    last.then_inc(s["pv_ps"], 1)

                def turn_nh(t):
                    turn(nh, t, T2_BANK[t], s["nh_ready"], g, s["t2_ps"])

                def values2(t):
                    if t < 2:
                        pe.wait_ge(s["att_ready"], count(g, TILES, 3 + t))
                    pe.wait_ge(s["nT_lo"], count(g, TILES, t + 1))
                    product(bank(V2_BANK[t], width=D + 1), lambda c, h: nT[h][:, c, t * P:(t + 1) * P],
                            lambda c, h: w_v2[h][:, c, :], range(KC)).then_inc(s["v2_ps"], 1)

                def keys2(m):
                    if m == 2:
                        pe.wait_ge(s["v2_lo"], count(g, TILES, 1))
                    product(bank(K2_BANK[m]), lambda c, h: w_k2[h][:, c, m * P:(m + 1) * P],
                            lambda c, h: nT[h][:, c, :], range(KC)).then_inc(s["k2_ps"], 1)

                fill(FILL[0])
                scores(0)
                scores(1)
                also(FFN_O, FFN_K)
                fill(FILL[1])
                turn_probs(0)
                scores(2)
                fill(FILL[2])
                weigh(0)
                scores(3)
                turn_probs(1)
                fill(FILL[3])
                weigh(1)
                fill(FILL[4])
                turn_probs(2)
                fill(FILL[5])
                weigh(2)
                turn_probs(3)
                turn_nh(0)
                fill(FILL[6])
                weigh(3)
                turn_nh(1)
                needs(FFN_V)
                if first:
                    pe.wait_ge(s["wr_lo"], 1)
                values2(0)
                turn_nh(2)
                fill(FILL[7])
                values2(1)
                turn_nh(3)
                values2(2)
                values2(3)
                needs(FFN_K)
                also(FFN_Q)
                keys2(0)
                keys2(1)
                pe.wait_ge(s["diag_set"], count(g, 1, 1))
                pe.wait_ge(s["v2_lo"], count(g, TILES, 2))
                pe.matmul(bank(BC_BANK), ones[:, :], space_g[:, 0, :], start=True, stop=True).then_inc(s["bc_ps"], 1)
                keys2(2)
                also(FFN_1)
                fill(FILL[8])
                pe.wait_ge(s["z_set"], count(g, 1, 1))
                for c in range(KC):
                    for t in range(TILES):
                        last = pe.matmul(bank(GP_BANK)[:, c * ZW:(c + 1) * ZW], nh[:, t, c * P:(c + 1) * P],
                                         Z_tiles[:, t, :], start=(t == 0), stop=(t == TILES - 1))
                last.then_inc(s["gp_ps"], 1)
                for t in range(TILES):
                    last = pe.transpose(bank(SELT_BANK, SELN)[:, t * P:(t + 1) * P], Z_tiles[:, t, 0:SELN], ident)
                last.then_inc(s["selT_ps"], 1)
                pe.wait_ge(s["k2_lo"], count(g, KC, 1))
                for t in range(TILES):
                    last = pe.transpose(bank(Y3T_BANK, 96)[:, t * P:(t + 1) * P], Y3_tiles[:, t, :], ident)
                last.then_inc(s["y3T_ps"], 1)
                also(FFN_1 + 1)
                pe.wait_ge(s["gat_lo"], count(g, 1, 1))
                needs(FFN_Q)
                for m in range(KC):
                    last = product(bank(Q2_BANK)[:, m * SELN:(m + 1) * SELN],
                                   lambda c, h: w_q2[h][:, c, m * P:(m + 1) * P],
                                   lambda c, h: gat[h][:, c, :], range(KC))
                last.then_inc(s["q2_ps"], 1)
                pe.wait_ge(s["pool_lo"], count(g, 1, 1))
                needs(FFN_M)
                product(bank(PW_BANK, 96, D), lambda c, h: pool[h][:, c, :], lambda c, h: w_m[h][:, c, :], range(KC))\
                    .then_inc(s["pw_ps"], 1)
                fill(FILL[9])
                pe.wait_ge(s["qB_lo"], count(g, 1, 1))
                for b in range(GB):
                    n = 0
                    for c in range(KC):
                        for a, k in ((0, 0), (0, 1), (1, 0)):
                            last = pe.matmul(bank(S2_BANK, SROWS)[:, b * NODES:(b + 1) * NODES],
                                             qB_rows(qB[a], c, b), kT2[k][:, c, b * NODES:(b + 1) * NODES],
                                             start=(n == 0), stop=(n == 3 * KC - 1))
                            n += 1
                last.then_inc(s["s2_ps"], 1)

                def mix(t):
                    n = 0
                    tok = slice(t * P, (t + 1) * P)
                    if t == 0:
                        pe.wait_ge(s["sT_set"], count(g, 1, 1))
                        pe.wait_ge(s["R_lo_set"], count(g, 1, 1))
                        if first:
                            pe.wait_ge(s["rows_in"], 32)
                    for c in range(KC):
                        for a, b in ((0, 0), (0, 1), (1, 0)):
                            pe.matmul(bank(MIX_BANK[t], width=D), nT[a][:, c, tok], w_m[b][:, c, :], start=(n == 0),
                                      stop=False)
                            n += 1
                    pe.matmul(bank(MIX_BANK[t], width=D), sT[:, tok], R[:, :], start=False, stop=True)\
                        .then_inc(s["mix_ps"], 1)

                def scatter(t):
                    if t == 0:
                        pe.wait_ge(s["mix_read"], count(g, TILES, TILES))
                    if t >= 2 and more:
                        pe.wait_ge(s["yT_lo"], count(g + 1, TILES, t - 1))
                    for h in range(2):
                        last = pe.matmul(bank(SC_BANK[t], width=D), selT[:, t * P:(t + 1) * P], Ah[h][:, :],
                                         start=(h == 0), stop=(h == 1))
                    last.then_inc(s["sc_ps"], 1)

                mix(0)
                also(FFN_1 + 2)
                fill(FILL[10])
                pe.wait_ge(s["p2_set"], count(g, 1, 1))
                for b in range(GB):
                    o = psum[:, PT2_BANK + b // (GB // 2), (b % (GB // 2)) * SROWS:(b % (GB // 2) + 1) * SROWS]
                    last = pe.transpose(o, p2z[:, b, :], const[0:SROWS, C_ID:C_ID + SROWS])
                last.then_inc(s["pt2_ps"], 1)
                fill(FILL[11])
                pe.wait_ge(s["p2T_lo"], count(g, 1, 1))
                for t in range(TILES):
                    for c in range(KC):
                        o = psum[:, CX_BANK + c, 2 * t * HQ * TOPK:2 * (t + 1) * HQ * TOPK]
                        for n, (i, j) in enumerate(((0, 0), (0, 1), (1, 0))):
                            last = pe.matmul(o, v2[i][:, t, c * P:(c + 1) * P],
                                             p2T[j][:, 2 * t:2 * t + 2, c * HQ * TOPK:(c + 1) * HQ * TOPK],
                                             start=(n == 0), stop=(n == 2))
                last.then_inc(s["cx_ps"], 1)
                mix(1)
                pe.wait_ge(s["ctx_lo"], count(g, 1, 1))
                pe.wait_ge(s["mix_read"], count(g, TILES, 1))
                needs(FFN_O)
                product(bank(O_BANK, SELN, D), lambda c, h: ctxT[h][:, c * SELN:(c + 1) * SELN],
                        lambda c, h: w_o[h][:, c, :], range(KC)).then_inc(s["o_ps"], 1)
                fill(FILL[12])
                mix(2)
                fill(FILL[13])
                mix(3)
                fill(FILL[14])
                also(FFN_1 + 3)
                if more:
                    front_turns(g + 1)
                fill(FILL[15])
                pe.wait_ge(s["A_lo"], count(g, 1, 1))
                for t in range(TILES):
                    scatter(t)
                fill(FILL[16])
                if more:
                    front_values(g + 1)
                    keys(g + 1, 0)
                fill(FILL[17])
                for t in range(TILES):
                    if more and t != 2:
                        pe.wait_ge(s["v_lo"], count(g + 1, TILES, min(t + 1, 3)))
                    if t == 2:
                        pe.wait_ge(s["h_ready"], count(g, TILES, TILES))
                    turn(n2, t, T3_BANK[t], s["n2_ready"], g, s["t3_ps"])
                needs(FFN_2 - 1)
                if first:
                    pe.wait_ge(*bias_read(FFN_2 - 1))
            for_groups(pe, first_steps, both)
            for m in range(HC):
                feed1(groups - 1, m)
            for t in range(TILES):
                for part in range(PARTS):
                    feed2(groups - 1, t, part)


def _constants():
    import numpy as np
    c = np.zeros((P, C_WIDTH), np.float32)
    i = np.arange(P)[:, None]
    j = np.arange(P)[None, :]
    same = i // NODES == j // NODES
    c[:, C_ID:C_ID + P] = i == j
    c[:, C_LT:C_LT + P] = same & (j < i)
    c[:, C_GT:C_GT + P] = same & (j > i)
    c[:, C_HALF:C_HALF + 2] = i // NODES == np.arange(2)[None, :]
    r = np.arange(2 * TOPK)[None, :]
    c[:, C_IOTA:C_IOTA + 2 * TOPK] = np.where(i // NODES == r // TOPK, r % TOPK, -1)
    return c


def kernel(**inputs):
    import numpy as np
    import concourse.bacc as bacc
    from concourse.bass_utils import run_bass_kernel_spmd

    nc = bacc.Bacc("TRN2", target_bir_lowering=False, num_devices=1)
    arrays, aps = {}, {}

    def give(name, a):
        arrays[name + "_dram"] = a
        aps[name] = nc.dram_tensor(name + "_dram", a.shape, mybir.dt.from_np(a.dtype), kind="ExternalInput").ap()

    give("x", np.ascontiguousarray(inputs["x"]).reshape(TOKENS, D))
    give("adj", np.ascontiguousarray(inputs["adj"]).reshape(TOKENS, NODES))
    give("consts", _constants())
    for name, a in inputs.items():
        if name not in ("x", "adj"):
            a = np.ascontiguousarray(a)
            give(name, a.reshape(1) if a.ndim == 0 else a)
    out = nc.dram_tensor("out_dram", (TOKENS, D), F32, kind="ExternalOutput").ap()
    gnn_ffn_kernel(nc, aps["x"], aps["adj"], aps, aps["consts"], out)
    r = run_bass_kernel_spmd(nc, [arrays], core_ids=[0])
    return r.results[0]["out_dram"].reshape(BATCH, NODES, D)
```
